# Optimizing a Trainium2 kernel written in Bass

```python
import numpy as np
import jax
import jax.numpy as jnp

def _softmax(x, axis=-1):
    return jax.nn.softmax(x, axis=axis)

def _gelu(x):
    return jax.nn.gelu(x, approximate=True)

def _silu(x):
    return jax.nn.silu(x)

def _sigmoid(x):
    return jax.nn.sigmoid(x)

def _layernorm(x, axis=-1, eps=1e-05):
    m = jnp.mean(x, axis=axis, keepdims=True)
    v = jnp.var(x, axis=axis, keepdims=True)
    return (x - m) / jnp.sqrt(v + eps)

def _scatter_add(tgt, idx, src, axis=0):
    return tgt.at[idx].add(src)

def _segment_sum(src, seg, n):
    return jax.ops.segment_sum(src, seg, n)
kernel_name = 'mk_seq_preln_d1_jaxref_r8_45c972'

def setup_inputs(seed: int=0):
    np.random.seed(seed)
    _w = jnp.asarray

    def _L0_attn_setup():
        import jax, jax.numpy as jnp
        import numpy as np
        D_MODEL = 128
        N_HEAD = 16
        HEAD_DIM = D_MODEL // N_HEAD
        D_INNER = 512
        N_LAYER = 4
        NEG = jnp.finfo(jnp.float32).min

        def _ln(x, w, b):
            m = x.mean(-1, keepdims=True)
            v = ((x - m) ** 2).mean(-1, keepdims=True)
            return (x - m) * jax.lax.rsqrt(v + 1e-06) * w + b

        def _pos_emb(k_len):
            pos = jnp.arange(k_len - 1, -1, -1, dtype=jnp.float32)
            inv = 1.0 / 10000.0 ** (jnp.arange(0, HEAD_DIM, 2, dtype=jnp.float32) / HEAD_DIM)
            s = pos[:, None] * inv[None, :]
            return jnp.concatenate([jnp.sin(s), jnp.cos(s)], axis=-1)

        def _rel_shift(x, q_len, k_len):
            B, H = (x.shape[0], x.shape[1])
            zp = jnp.zeros((B, H, q_len, 1), x.dtype)
            xp = jnp.concatenate([zp, x], axis=-1).reshape(B, H, k_len + 1, q_len)
            return xp[:, :, 1:, :].reshape(B, H, q_len, k_len)

        def _attn(xn, Wq, bq, Wk, bk, Wv, bv, Wo, bo, u):
            B, S, _ = xn.shape
            sh = lambda t: t.reshape(B, S, N_HEAD, HEAD_DIM).transpose(0, 2, 1, 3)
            q = sh(xn @ Wq.T + bq)
            k = sh(xn @ Wk.T + bk)
            v = sh(xn @ Wv.T + bv)
            scores = jnp.einsum('bhqd,bhkd->bhqk', q, k)
            r = _pos_emb(S)
            rel = jnp.einsum('bhqd,ld->bhql', q + u[None, :, None, :], r)
            scores = (scores + _rel_shift(rel, S, S)) * HEAD_DIM ** (-0.5)
            mask = jnp.arange(S)[None, :] > jnp.arange(S)[:, None]
            scores = jnp.where(mask[None, None], NEG, scores)
            p = jax.nn.softmax(scores, axis=-1)
            ctx = jnp.einsum('bhqk,bhkd->bhqd', p, v).transpose(0, 2, 1, 3).reshape(B, S, D_MODEL)
            return ctx @ Wo.T + bo
        key = jax.random.key(seed)
        ks = jax.random.split(key, 20)
        B, S = (4, 128)
        p = lambda k, shp, s=0.02: jax.random.normal(k, shp, dtype=jnp.float32) * s
        L = N_LAYER
        return {'x': jax.random.normal(ks[0], (B, S, D_MODEL), dtype=jnp.float32), 'Wq': p(ks[1], (L, D_MODEL, D_MODEL)), 'bq': jnp.zeros((L, D_MODEL)), 'Wk': p(ks[2], (L, D_MODEL, D_MODEL)), 'bk': jnp.zeros((L, D_MODEL)), 'Wv': p(ks[3], (L, D_MODEL, D_MODEL)), 'bv': jnp.zeros((L, D_MODEL)), 'Wo': p(ks[4], (L, D_MODEL, D_MODEL)), 'bo': jnp.zeros((L, D_MODEL)), 'u_bias': p(ks[5], (L, N_HEAD, HEAD_DIM), 0.02), 'W1': p(ks[6], (L, D_INNER, D_MODEL)), 'b1': jnp.zeros((L, D_INNER)), 'W2': p(ks[7], (L, D_MODEL, D_INNER)), 'b2': jnp.zeros((L, D_MODEL)), 'ln1_w': jnp.ones((L, D_MODEL)), 'ln1_b': jnp.zeros((L, D_MODEL)), 'ln2_w': jnp.ones((L, D_MODEL)), 'ln2_b': jnp.zeros((L, D_MODEL))}
    _L0_attn_in = _L0_attn_setup()

    def _L0_ffn_setup():
        import jax, jax.numpy as jnp
        import numpy as np
        E = 16
        G = 4
        EPG = E // G
        K = 4
        TOPK_GROUP = 2
        PER_GROUP_K = K // TOPK_GROUP

        def _route(xf, router_w, correction_bias):
            S = xf.shape[0]
            logits = xf @ router_w.T
            scores = jax.nn.sigmoid(logits)
            sb = scores + correction_bias
            grp_top = jax.lax.top_k(sb.reshape(S, G, EPG), PER_GROUP_K)[0]
            group_scores = grp_top.sum(axis=-1)
            _, group_idx = jax.lax.top_k(group_scores, TOPK_GROUP)
            group_mask = jnp.zeros((S, G), sb.dtype).at[jnp.arange(S)[:, None], group_idx].set(1.0)
            score_mask = jnp.broadcast_to(group_mask[:, :, None], (S, G, EPG)).reshape(S, E)
            masked = jnp.where(score_mask > 0, sb, -jnp.inf)
            _, topk_idx = jax.lax.top_k(masked, K)
            w = jnp.take_along_axis(scores, topk_idx, axis=1)
            w = w / (w.sum(axis=-1, keepdims=True) + 1e-20)
            return (topk_idx, w, scores)
        key = jax.random.key(seed)
        ks = jax.random.split(key, 9)
        B, T, C, H, HS = (2, 128, 128, 32, 256)
        std = 0.02
        return {'x': jax.random.normal(ks[0], (B, T, C), jnp.float32), 'router_w': jax.random.normal(ks[1], (E, C), jnp.float32) * std, 'correction_bias': jnp.zeros((E,), jnp.float32), 'gate_w': jax.random.normal(ks[2], (E, C, H), jnp.float32) * std, 'up_w': jax.random.normal(ks[3], (E, C, H), jnp.float32) * std, 'down_w': jax.random.normal(ks[4], (E, H, C), jnp.float32) * std, 'shared_gate_w': jax.random.normal(ks[5], (HS, C), jnp.float32) * std, 'shared_up_w': jax.random.normal(ks[6], (HS, C), jnp.float32) * std, 'shared_down_w': jax.random.normal(ks[7], (C, HS), jnp.float32) * std}
    _L0_ffn_in = _L0_ffn_setup()
    _d = {'L0_attn_x': _L0_attn_in['x'], 'L0_attn_Wq': _L0_attn_in['Wq'], 'L0_attn_bq': _L0_attn_in['bq'], 'L0_attn_Wk': _L0_attn_in['Wk'], 'L0_attn_bk': _L0_attn_in['bk'], 'L0_attn_Wv': _L0_attn_in['Wv'], 'L0_attn_bv': _L0_attn_in['bv'], 'L0_attn_Wo': _L0_attn_in['Wo'], 'L0_attn_bo': _L0_attn_in['bo'], 'L0_attn_u_bias': _L0_attn_in['u_bias'], 'L0_attn_W1': _L0_attn_in['W1'], 'L0_attn_b1': _L0_attn_in['b1'], 'L0_attn_W2': _L0_attn_in['W2'], 'L0_attn_b2': _L0_attn_in['b2'], 'L0_attn_ln1_w': _L0_attn_in['ln1_w'], 'L0_attn_ln1_b': _L0_attn_in['ln1_b'], 'L0_attn_ln2_w': _L0_attn_in['ln2_w'], 'L0_attn_ln2_b': _L0_attn_in['ln2_b'], 'L0_ffn_router_w': _L0_ffn_in['router_w'], 'L0_ffn_correction_bias': _L0_ffn_in['correction_bias'], 'L0_ffn_gate_w': _L0_ffn_in['gate_w'], 'L0_ffn_up_w': _L0_ffn_in['up_w'], 'L0_ffn_down_w': _L0_ffn_in['down_w'], 'L0_ffn_shared_gate_w': _L0_ffn_in['shared_gate_w'], 'L0_ffn_shared_up_w': _L0_ffn_in['shared_up_w'], 'L0_ffn_shared_down_w': _L0_ffn_in['shared_down_w']}
    _x0 = _d['L0_attn_x']
    _d['L0_attn_x'] = jax.random.normal(jax.random.fold_in(jax.random.key(seed), 1), (32, 256, 128), dtype=_x0.dtype)
    del _x0
    return _d

def reference(L0_attn_x, L0_attn_Wq, L0_attn_bq, L0_attn_Wk, L0_attn_bk, L0_attn_Wv, L0_attn_bv, L0_attn_Wo, L0_attn_bo, L0_attn_u_bias, L0_attn_W1, L0_attn_b1, L0_attn_W2, L0_attn_b2, L0_attn_ln1_w, L0_attn_ln1_b, L0_attn_ln2_w, L0_attn_ln2_b, L0_ffn_router_w, L0_ffn_correction_bias, L0_ffn_gate_w, L0_ffn_up_w, L0_ffn_down_w, L0_ffn_shared_gate_w, L0_ffn_shared_up_w, L0_ffn_shared_down_w):

    def _L0_attn_ref(x, Wq, bq, Wk, bk, Wv, bv, Wo, bo, u_bias, W1, b1, W2, b2, ln1_w, ln1_b, ln2_w, ln2_b):
        import jax, jax.numpy as jnp
        import numpy as np
        D_MODEL = 128
        N_HEAD = 16
        HEAD_DIM = D_MODEL // N_HEAD
        D_INNER = 512
        N_LAYER = 4
        NEG = jnp.finfo(jnp.float32).min

        def _ln(x, w, b):
            m = x.mean(-1, keepdims=True)
            v = ((x - m) ** 2).mean(-1, keepdims=True)
            return (x - m) * jax.lax.rsqrt(v + 1e-06) * w + b

        def _pos_emb(k_len):
            pos = jnp.arange(k_len - 1, -1, -1, dtype=jnp.float32)
            inv = 1.0 / 10000.0 ** (jnp.arange(0, HEAD_DIM, 2, dtype=jnp.float32) / HEAD_DIM)
            s = pos[:, None] * inv[None, :]
            return jnp.concatenate([jnp.sin(s), jnp.cos(s)], axis=-1)

        def _rel_shift(x, q_len, k_len):
            B, H = (x.shape[0], x.shape[1])
            zp = jnp.zeros((B, H, q_len, 1), x.dtype)
            xp = jnp.concatenate([zp, x], axis=-1).reshape(B, H, k_len + 1, q_len)
            return xp[:, :, 1:, :].reshape(B, H, q_len, k_len)

        def _attn(xn, Wq, bq, Wk, bk, Wv, bv, Wo, bo, u):
            B, S, _ = xn.shape
            sh = lambda t: t.reshape(B, S, N_HEAD, HEAD_DIM).transpose(0, 2, 1, 3)
            q = sh(xn @ Wq.T + bq)
            k = sh(xn @ Wk.T + bk)
            v = sh(xn @ Wv.T + bv)
            scores = jnp.einsum('bhqd,bhkd->bhqk', q, k)
            r = _pos_emb(S)
            rel = jnp.einsum('bhqd,ld->bhql', q + u[None, :, None, :], r)
            scores = (scores + _rel_shift(rel, S, S)) * HEAD_DIM ** (-0.5)
            mask = jnp.arange(S)[None, :] > jnp.arange(S)[:, None]
            scores = jnp.where(mask[None, None], NEG, scores)
            p = jax.nn.softmax(scores, axis=-1)
            ctx = jnp.einsum('bhqk,bhkd->bhqd', p, v).transpose(0, 2, 1, 3).reshape(B, S, D_MODEL)
            return ctx @ Wo.T + bo
        h = x
        for l in range(N_LAYER):
            xn = _ln(h, ln1_w[l], ln1_b[l])
            a = _attn(xn, Wq[l], bq[l], Wk[l], bk[l], Wv[l], bv[l], Wo[l], bo[l], u_bias[l])
            h = h + a
            fn = _ln(h, ln2_w[l], ln2_b[l])
            ff = jax.nn.gelu(fn @ W1[l].T + b1[l], approximate=False) @ W2[l].T + b2[l]
            h = h + ff
        return h

    def _L0_ffn_ref(x, router_w, correction_bias, gate_w, up_w, down_w, shared_gate_w, shared_up_w, shared_down_w):
        import jax, jax.numpy as jnp
        import numpy as np
        E = 16
        G = 4
        EPG = E // G
        K = 4
        TOPK_GROUP = 2
        PER_GROUP_K = K // TOPK_GROUP

        def _route(xf, router_w, correction_bias):
            S = xf.shape[0]
            logits = xf @ router_w.T
            scores = jax.nn.sigmoid(logits)
            sb = scores + correction_bias
            grp_top = jax.lax.top_k(sb.reshape(S, G, EPG), PER_GROUP_K)[0]
            group_scores = grp_top.sum(axis=-1)
            _, group_idx = jax.lax.top_k(group_scores, TOPK_GROUP)
            group_mask = jnp.zeros((S, G), sb.dtype).at[jnp.arange(S)[:, None], group_idx].set(1.0)
            score_mask = jnp.broadcast_to(group_mask[:, :, None], (S, G, EPG)).reshape(S, E)
            masked = jnp.where(score_mask > 0, sb, -jnp.inf)
            _, topk_idx = jax.lax.top_k(masked, K)
            w = jnp.take_along_axis(scores, topk_idx, axis=1)
            w = w / (w.sum(axis=-1, keepdims=True) + 1e-20)
            return (topk_idx, w, scores)
        B, T, C = x.shape
        S = B * T
        xf = x.reshape(S, C)
        sg = xf @ shared_gate_w.T
        su = xf @ shared_up_w.T
        shared_out = jax.nn.silu(sg) * su @ shared_down_w.T
        topk_idx, w, _scores = _route(xf, router_w, correction_bias)
        combine = jnp.zeros((S, E), xf.dtype).at[jnp.arange(S)[:, None], topk_idx].add(w)
        g = jnp.einsum('sc,ech->esh', xf, gate_w)
        u = jnp.einsum('sc,ech->esh', xf, up_w)
        h = jax.nn.silu(g) * u
        hw = h * combine.T[:, :, None]
        routed = jnp.einsum('esh,ehc->sc', hw, down_w)
        return (shared_out + routed).reshape(B, T, C)
    x = L0_attn_x
    x = x + _L0_attn_ref(_layernorm(x, axis=-1), L0_attn_Wq, L0_attn_bq, L0_attn_Wk, L0_attn_bk, L0_attn_Wv, L0_attn_bv, L0_attn_Wo, L0_attn_bo, L0_attn_u_bias, L0_attn_W1, L0_attn_b1, L0_attn_W2, L0_attn_b2, L0_attn_ln1_w, L0_attn_ln1_b, L0_attn_ln2_w, L0_attn_ln2_b)
    x = x + _L0_ffn_ref(_layernorm(x, axis=-1), L0_ffn_router_w, L0_ffn_correction_bias, L0_ffn_gate_w, L0_ffn_up_w, L0_ffn_down_w, L0_ffn_shared_gate_w, L0_ffn_shared_up_w, L0_ffn_shared_down_w)
    return x

_drawn_inputs = setup_inputs


def setup_inputs(seed=0):
    import zlib

    import numpy as np

    out = dict(_drawn_inputs(seed))
    spreads = {'L0_attn_bq': (0.0, 0.8),
     'L0_attn_bk': (0.0, 2.0),
     'L0_attn_bv': (0.0, 0.376),
     'L0_attn_bo': (0.0, 0.1),
     'L0_attn_b1': (0.0, 0.338),
     'L0_attn_b2': (0.0, 0.1),
     'L0_attn_ln1_w': (1.0, 0.6),
     'L0_attn_ln1_b': (0.0, 0.8),
     'L0_attn_ln2_w': (1.0, 0.6),
     'L0_attn_ln2_b': (0.0, 0.8),
     'L0_ffn_correction_bias': (0.0, 0.8)}
    factors = {'L0_attn_Wq': 8.0,
     'L0_attn_Wk': 8.0,
     'L0_attn_Wv': 4.32,
     'L0_attn_u_bias': 28.594,
     'L0_ffn_router_w': 8.0,
     'L0_ffn_gate_w': 8.0,
     'L0_ffn_up_w': 8.0,
     'L0_ffn_down_w': 8.0,
     'L0_ffn_shared_gate_w': 8.0,
     'L0_ffn_shared_up_w': 8.0,
     'L0_ffn_shared_down_w': 8.0}
    for name, (base, spread) in spreads.items():
        noise = np.random.default_rng([zlib.crc32(name.encode()), seed]).standard_normal(out[name].shape)
        drawn = base * np.exp(spread * noise) if base else spread * noise
        out[name] = jnp.asarray(drawn.astype(out[name].dtype))
    for name, factor in factors.items():
        out[name] = (out[name] * factor).astype(out[name].dtype)
    return out
```

```python
from contextlib import ExitStack

import numpy as np

import concourse.bass as bass
from concourse import mybir

F32 = mybir.dt.float32
BF16 = mybir.dt.bfloat16
ALU = mybir.AluOpType
ACT = mybir.ActivationFunctionType
AX_X = mybir.AxisListType.X

B, S, D = 32, 256, 128
H, HD = 16, 8
LAYERS, DI = 4, 512
T = S // 128
N = LAYERS * B
FC = DI // 128
SCALE = HD ** -0.5
PARTS_Q = (0, 0, 0, 1, 1, 2)
PARTS_K = (0, 1, 2, 0, 1, 0)
NB = len(PARTS_Q)
ROT0 = NB * HD
MROW = 2 * NB * HD
STACK = MROW + 2
RING = 4
STEPS = 12
PR = 6
VW = 32
MASK = -1.0e30
STACK_DMAS = 3 * NB
PER = 4
E, G, EH = 16, 4, 32
HS = 256
NT = B * T
GU = E * EH + HS
HIGH, LOW = 3.0e38, -3.0e38


def wait_alone(eng, sem, value, apart):
    if not isinstance(value, int):
        eng.wait_ge(sem, value)
        eng.sem_inc(apart, 1)
    elif value > 0:
        eng.wait_ge(sem, value)


def at_least(eng, sem, value):
    if not isinstance(value, int) or value > 0:
        eng.wait_ge(sem, value)


def capped(value, most):
    return min(value, most) if isinstance(value, int) else value


def bf16_parts(x):
    parts = []
    for _ in range(3):
        bits = x.astype(np.float32).view(np.uint32).astype(np.uint64)
        bits = (bits + 0x7FFF + ((bits >> 16) & 1)) & 0xFFFF0000
        p = bits.astype(np.uint32).view(np.float32)
        parts.append(p)
        x = x - p.astype(np.float64)
    return parts


def position_tables():
    inv = (1.0 / np.float32(10000.0) ** (np.arange(0, HD, 2, dtype=np.float32) / np.float32(HD))).astype(np.float64)
    angle = np.arange(S, dtype=np.float64)[:, None] * inv[None, :]
    sin, cos = np.sin(angle), np.cos(angle)
    turn = np.zeros((128, 2, T, D), np.float32)
    for t in range(T):
        rows = slice(t * 128, t * 128 + 128)
        s64 = np.repeat(sin[rows], H, axis=1)
        c64 = np.repeat(cos[rows], H, axis=1)
        turn[:, 0, t] = np.concatenate([s64, s64], axis=1)
        turn[:, 1, t] = np.concatenate([c64, -c64], axis=1)
    parts = bf16_parts(np.ascontiguousarray(np.concatenate([cos, sin], axis=1).T))
    keys = np.concatenate([parts[p] for p in PARTS_K] + [np.ones((2, S), np.float32)], axis=0)
    q, k = np.arange(128)[:, None], np.arange(128)[None, :]
    mask = np.where(k > q, np.float32(MASK), np.float32(0))
    squares = np.concatenate([np.eye(128, dtype=np.float32), mask, mask.T], axis=1)
    return {"c_turn": turn.reshape(128, -1), "c_keys": keys, "c_squares": squares}


def layers_program(nc, a, h_all):
    with ExitStack() as ctx:
        def sb(name, shape, dt=F32):
            return ctx.enter_context(nc.sbuf_tensor(name, shape, dt))

        def sem(name):
            return ctx.enter_context(nc.semaphore(name))

        bank = ctx.enter_context(nc.psum_tensor("bank", [128, 8, 512], F32))

        def bank16(i):
            return bank[:, i, :].bitcast(BF16)

        w_qkv = sb("w_qkv", [128, LAYERS, 3 * D])
        w_o = sb("w_o", [128, LAYERS, D])
        w_1 = sb("w_1", [128, DI])
        w_2 = sb("w_2", [128, LAYERS, FC, D])
        b_qkv = sb("b_qkv", [128, LAYERS, 3 * D])
        b_u = sb("b_u", [128, LAYERS, D])
        b_o = sb("b_o", [128, LAYERS, D])
        b_2 = sb("b_2", [128, LAYERS, D])
        ln_cols = sb("ln_cols", [128, LAYERS, 4])
        b_1 = sb("b_1", [128, LAYERS, FC])
        turn = sb("turn", [128, 2, T, D])
        mask = sb("mask", [128, 4, 128], BF16)
        maskT = sb("maskT", [128, 4, 128], BF16)
        squares = sb("squares", [128, 3, 128])
        eye = squares[:, 0]
        eyeb = sb("eyeb", [128, 128], BF16)
        keys_f = sb("keys_f", [STACK - ROT0, S])
        keys_b = sb("keys_b", [STACK - ROT0, S], BF16)
        expo = sb("expo", [128, 16])

        stats0 = sb("stats0", [128, PER * T, 6])
        mv0 = sb("mv0", [128, PER * T, 2])
        ve0 = sb("ve0", [128, PER * T])
        rstd0 = sb("rstd0", [128, PER * T])

        stats1 = sb("stats1", [128, T, 6])
        mv1 = sb("mv1", [128, T, 2])
        ve1 = sb("ve1", [128, T])
        rstd1 = sb("rstd1", [128, T])
        xn1 = sb("xn1", [128, T, D])
        xn1T = sb("xn1T", [128, S])
        feats = sb("feats", [128, T, 3, D])
        qu = sb("qu", [128, T, D])
        turn_s = sb("turn_s", [128, T, D])
        turn_c = sb("turn_c", [128, T, D])
        rest = sb("rest", [128, T, 3, D])
        parts = sb("parts", [128, T, 3, 3, D], BF16)
        base = sb("base", [128, 2, 3, 3, S], BF16)
        v_tok = sb("v_tok", [128, RING, T, D])
        v_pad = sb("v_pad", [128, 2, T, H, VW])
        qstack = sb("qstack", [STACK, RING, H, S], BF16)
        kstack = sb("kstack", [STACK, RING, H, S], BF16)
        negmax = sb("negmax", [128, 2, T, H])
        negparts = sb("negparts", [128, T, 2, H], BF16)
        negrows = sb("negrows", [2 * H, S], BF16)
        probs = sb("probs", [128, PR, 512])
        ctxT_raw = sb("ctxT_raw", [128, 4, S])
        rsum = sb("rsum", [128, T, H])
        ctx_tok = sb("ctx_tok", [128, T, D])
        ctxT = sb("ctxT", [128, S])
        stats2 = sb("stats2", [128, T, 6])
        mv2 = sb("mv2", [128, T, 2])
        ve2 = sb("ve2", [128, T])
        rstd2 = sb("rstd2", [128, T])
        xn2 = sb("xn2", [128, T, D])
        xn2T = sb("xn2T", [128, S])
        hidden = sb("hidden", [128, FC, S])

        x_landed = sem("x_landed")
        consts_landed = sem("consts_landed")
        keys_landed = sem("keys_landed")
        squares_landed = sem("squares_landed")
        consts_cast = sem("consts_cast")
        prefilled = sem("prefilled")
        zeros_filled = sem("zeros_filled")
        apart_dve, apart_pool, apart_sp = (sem(f"apart_{e}") for e in ("dve", "pool", "sp"))
        stats0_done = sem("stats0_done")
        mv0_ready = sem("mv0_ready")
        ve0_ready = sem("ve0_ready")
        rstd0_ready = sem("rstd0_ready")
        ln0_done = sem("ln0_done")
        w1_landed = sem("w1_landed")
        stats1_done = sem("stats1_done")
        mv1_ready = sem("mv1_ready")
        ve1_ready = sem("ve1_ready")
        rstd1_ready = sem("rstd1_ready")
        xn1_ready = sem("xn1_ready")
        xn1_turned = sem("xn1_turned")
        xn1T_ready = sem("xn1T_ready")
        qkv_done = sem("qkv_done")
        qk_ready = sem("qk_ready")
        v_ready = sem("v_ready")
        qu_ready = sem("qu_ready")
        turn_steps = sem("turn_steps")
        rot_ready = sem("rot_ready")
        qk_split = sem("qk_split")
        rot_split = sem("rot_split")
        parts_turned = sem("parts_turned")
        base_ready = sem("base_ready")
        stack_landed = [sem(f"stack_landed{i}") for i in range(RING)]
        vpad_ready = sem("vpad_ready")
        scores_done = sem("scores_done")
        max_done = sem("max_done")
        neg_split = sem("neg_split")
        neg_turned = sem("neg_turned")
        negrows_ready = sem("negrows_ready")
        negrows_landed = sem("negrows_landed")
        scoresT_done = sem("scoresT_done")
        exp_done = sem("exp_done")
        context_done = sem("context_done")
        context_out = sem("context_out")
        context_turned = sem("context_turned")
        rsum_ready = sem("rsum_ready")
        ctx_ready = sem("ctx_ready")
        ctx_turned = sem("ctx_turned")
        ctxT_ready = sem("ctxT_ready")
        proj_done = sem("proj_done")
        bo_added = sem("bo_added")
        h1_ready = sem("h1_ready")
        stats2_done = sem("stats2_done")
        mv2_ready = sem("mv2_ready")
        ve2_ready = sem("ve2_ready")
        rstd2_ready = sem("rstd2_ready")
        xn2_ready = sem("xn2_ready")
        xn2_turned = sem("xn2_turned")
        xn2T_ready = sem("xn2T_ready")
        up_done = sem("up_done")
        gelu_done = sem("gelu_done")
        down_done = sem("down_done")
        b2_added = sem("b2_added")
        h2_ready = sem("h2_ready")

        x_tiles = a["x"].rearrange("b (t p) d -> p b t d", p=128)
        X_DMAS = B // PER

        def mod(n, m):
            return n % m

        def layer(n):
            return n // B

        CONST_DMAS = 10

        FIRST_LOOP, LAST_LOOP = 2, 31
        LAST_SLOT = N + 5

        def slots(eng, slot):
            for s in range(-1, 4 * FIRST_LOOP):
                slot(s, s % 4)
            with eng.Fori(FIRST_LOOP, LAST_LOOP) as g:
                for u in range(4):
                    slot(4 * g + u, u)
            for s in range(4 * LAST_LOOP, LAST_SLOT):
                slot(s, s % 4)

        def live(n):
            return not isinstance(n, int) or 0 <= n < N

        block = ctx.enter_context(nc.Block())

        @block.sync
        def _(sp):
            sp.dma_start(squares[:], a["c_squares"].rearrange("p (a n) -> p a n", a=3)).then_inc(squares_landed, 16)
            sp.dma_start(keys_f[:], a["c_keys"]).then_inc(squares_landed, 16)
            for c in range(X_DMAS):
                w = B // X_DMAS
                sp.dma_start(h_all[:, c * w:(c + 1) * w], x_tiles[:, c * w:(c + 1) * w]).then_inc(x_landed, 16)
            sp.dma_start(w_qkv[:], a["w_qkv"].rearrange("l p n -> p l n")).then_inc(consts_landed, 16)
            sp.dma_start(ln_cols[:], a["ln_cols"].rearrange("p (l c) -> p l c", l=LAYERS)).then_inc(consts_landed, 16)
            sp.dma_start(b_qkv[:], a["b_qkv"].rearrange("(o l) n -> o l n", o=1).broadcast_to([128, LAYERS, 3 * D])).then_inc(consts_landed, 16)
            sp.dma_start(b_u[:], a["u"].rearrange("(o l) n -> o l n", o=1).broadcast_to([128, LAYERS, D])).then_inc(consts_landed, 16)
            sp.dma_start(turn[:], a["c_turn"].rearrange("p (a t n) -> p a t n", a=2, t=T)).then_inc(consts_landed, 16)
            sp.wait_ge(consts_cast, 4)
            for r in range(RING):
                sp.dma_start(kstack[ROT0:STACK, r], keys_b[:].unsqueeze(1).broadcast_to([STACK - ROT0, H, S])
                             ).then_inc(keys_landed, 16)
            sp.dma_start(b_o[:], a["bo"].rearrange("(o l) n -> o l n", o=1).broadcast_to([128, LAYERS, D])).then_inc(consts_landed, 16)
            sp.dma_start(b_2[:], a["b2"].rearrange("(o l) n -> o l n", o=1).broadcast_to([128, LAYERS, D])).then_inc(consts_landed, 16)
            sp.dma_start(w_o[:], a["w_o"].rearrange("l p n -> p l n")).then_inc(consts_landed, 16)
            sp.dma_start(b_1[:], a["b_1"].rearrange("p (l c) -> p l c", l=LAYERS)).then_inc(consts_landed, 16)
            sp.dma_start(w_2[:], a["w_2"].rearrange("l (c p) n -> p l c n", p=128)).then_inc(consts_landed, 16)
            sp.dma_start(w_1[:], a["w_1"][0]).then_inc(w1_landed, 16)

            def slot(s, u):
                n, r = s - 3, (u - 3) % RING
                if live(n):
                    wait_alone(sp, negrows_ready, n + 1, apart_sp)
                    for i in range(2):
                        sp.dma_start(qstack[MROW + i:MROW + i + 1, r], negrows[i * H:(i + 1) * H, :]
                                     ).then_inc(negrows_landed, 16)
                n, r = s - 1, (u - 1) % RING
                if live(n):
                    wait_alone(sp, base_ready, 3 * (n + 1), apart_sp)
                    wait_alone(sp, scoresT_done, STEPS * (n - 3), apart_sp)
                    for c in range(NB):
                        rows = slice(c * HD, (c + 1) * HD)
                        rot_rows = slice(ROT0 + c * HD, ROT0 + (c + 1) * HD)
                        p = r % 2
                        sp.dma_start(qstack[rows, r], base[:, p, PARTS_Q[c], 0]).then_inc(stack_landed[r], 16)
                        sp.dma_start(kstack[rows, r], base[:, p, PARTS_K[c], 1]).then_inc(stack_landed[r], 16)
                        sp.dma_start(qstack[rot_rows, r], base[:, p, PARTS_Q[c], 2]).then_inc(stack_landed[r], 16)

            def next_w1(ly):
                sp.wait_ge(up_done, 2 * B * ly)
                sp.dma_start(w_1[:], a["w_1"][ly]).then_inc(w1_landed, 16)

            for s in range(-1, 4 * FIRST_LOOP):
                slot(s, s % 4)
            g0 = FIRST_LOOP
            for ly in range(1, LAYERS):
                g1 = (B * ly + 4) // 4
                with sp.Fori(g0, g1) as g:
                    for u in range(4):
                        slot(4 * g + u, u)
                slot(4 * g1, 0)
                next_w1(ly)
                for u in range(1, 4):
                    slot(4 * g1 + u, u)
                g0 = g1 + 1
            with sp.Fori(g0, LAST_LOOP) as g:
                for u in range(4):
                    slot(4 * g + u, u)
            for s in range(4 * LAST_LOOP, LAST_SLOT):
                slot(s, s % 4)

        @block.tensor
        def _(pe):
            def f1(n):
                pe.wait_ge(xn1_ready, 2 * (n + 1))
                at_least(pe, base_ready, 3 * n)
                for t in range(T):
                    last = pe.transpose(bank[:, 5, t * 128:(t + 1) * 128], xn1[:, t], eye)
                last.then_inc(xn1_turned, 1)

            def f2(n, t):
                b = 5 + t
                pe.wait_ge(xn1T_ready, n + 1)
                if t == 1:
                    at_least(pe, negrows_ready, n - 2)
                pe.matmul(bank[:, b, 0:3 * D], xn1T[:, t * 128:(t + 1) * 128], w_qkv[:, layer(n)],
                          start=True, stop=True).then_inc(qkv_done, 1)

            def f3(n, j):
                b = 5 + j % 2
                need = (1, 3, 4)[j]
                pe.wait_ge(qk_split, 4 * n + need)
                pe.wait_ge(rot_split, 4 * n + need)
                if j == 0:
                    pe.wait_ge(v_ready, 2 * n + 1)
                if j == 1:
                    pe.wait_ge(v_ready, 2 * n + 2)
                    at_least(pe, gelu_done, FC * (n - 4))
                if j == 2:
                    pe.wait_ge(base_ready, 3 * n + 1)
                o = bank16(b)[:, 0:3 * S].rearrange("p (s t c) -> p s t c", s=3, t=T)
                for src in range(3):
                    for t in range(T):
                        last = pe.transpose(o[:, src, t], parts[:, t, j, src], eyeb[:])
                last.then_inc(parts_turned, 1)

            def m_bank(n, u, k):
                r = u % RING
                if k == 0:
                    pe.wait_ge(stack_landed[r], 16 * STACK_DMAS * (n // RING + 1))
                at_least(pe, max_done, STEPS * n + k - 1)
                b = k % 2
                if k < 4:
                    pe.matmul(bank[:, b, :], eyeb[:], mask[:], start=True, stop=True)
                    for i in range(4):
                        hd = 4 * k + i
                        last = pe.matmul(bank[:, b, i * 128:(i + 1) * 128], qstack[0:MROW, r, hd, 0:128],
                                         kstack[0:MROW, r, hd, 0:128], start=False, stop=True,
                                         skip_group_check=True)
                else:
                    two = bank[:, b, :].rearrange("p (h k) -> p h k", h=2)
                    pe.matmul(two[:, :, 128:256], eyeb[:], mask[:, 0:2], start=True, stop=True)
                    for i in range(2):
                        hd = 2 * (k - 4) + i
                        last = pe.matmul(two[:, i], qstack[0:MROW, r, hd, 128:256], kstack[0:MROW, r, hd, :],
                                         start=False, stop=True, skip_group_check=True)
                last.then_inc(scores_done, 1)

            def m1(n):
                pe.wait_ge(neg_split, 2 * (n + 1))
                pe.wait_ge(base_ready, capped(3 * (n + 2) + 2, 3 * N))
                if isinstance(n, int) and n + 2 >= N:
                    pe.wait_ge(gelu_done, FC * (n - 2))
                for t in range(T):
                    last = pe.transpose(bank16(6)[0:2 * H, t * 128:(t + 1) * 128],
                                        negparts[:, t].rearrange("p a h -> p (a h)"), eyeb[:])
                last.then_inc(neg_turned, 1)

            def a_bank(n, u, k):
                r = u % RING
                if k == 0:
                    pe.wait_ge(negrows_landed, 32 * (n + 1))
                at_least(pe, exp_done, STEPS * n + k - 1)
                b = 2 + k % 2
                grp, kind = k // 3, k % 3
                if kind < 2:
                    two = bank[:, b, :].rearrange("p (h q) -> p h q", h=2)
                    pe.matmul(two[:, :, 0:128], eyeb[:], maskT[:, 0:2], start=True, stop=True)
                    for i in range(2):
                        hd = 4 * grp + 2 * kind + i
                        last = pe.matmul(two[:, i], kstack[:, r, hd, 0:128], qstack[:, r, hd, :],
                                         start=False, stop=True, skip_group_check=True)
                else:
                    pe.matmul(bank[:, b, :], eyeb[:], maskT[:], start=True, stop=True)
                    for i in range(4):
                        hd = 4 * grp + i
                        last = pe.matmul(bank[:, b, i * 128:(i + 1) * 128], kstack[:, r, hd, 128:256],
                                         qstack[:, r, hd, 128:256], start=False, stop=True, skip_group_check=True)
                last.then_inc(scoresT_done, 1)

            def pv(n, u, grp):
                pe.wait_ge(exp_done, STEPS * n + 3 * grp + 3)
                if grp == 0:
                    pe.wait_ge(vpad_ready, n + 1)
                if grp % 2 == 0:
                    at_least(pe, context_out, 2 * n + grp // 2)
                v = u % 2
                c0 = (grp % 2) * S
                for i in range(4):
                    hd = 4 * grp + i
                    p0 = probs[:, (3 * grp + i // 2) % PR, (i % 2) * S:(i % 2 + 1) * S]
                    pe.matmul(bank[32 * i:32 * i + VW, 4, c0:c0 + S], v_pad[:, v, 0, hd], p0,
                              start=True, stop=True, skip_group_check=True)
                for i in range(4):
                    hd = 4 * grp + i
                    p1 = probs[:, (3 * grp + 2) % PR, i * 128:(i + 1) * 128]
                    last = pe.matmul(bank[32 * i:32 * i + VW, 4, c0 + 128:c0 + S], v_pad[:, v, 1, hd], p1,
                                     start=False, stop=True, skip_group_check=True)
                last.then_inc(context_done, 1)

            def b1(n, t):
                if t == 0:
                    pe.wait_ge(context_out, 2 * (n + 1))
                    at_least(pe, h2_ready, n)
                else:
                    pe.wait_ge(ctx_ready, 2 * n + 1)
                for grp in range(4):
                    last = pe.transpose(bank[:, 7, grp * 128:(grp + 1) * 128],
                                        ctxT_raw[:, grp, t * 128:(t + 1) * 128], eye)
                last.then_inc(context_turned, 1)

            def b2(n):
                pe.wait_ge(ctx_ready, 2 * (n + 1))
                for t in range(T):
                    last = pe.transpose(bank[:, 7, t * 128:(t + 1) * 128], ctx_tok[:, t], eye)
                last.then_inc(ctx_turned, 1)

            def b3(n):
                pe.wait_ge(ctxT_ready, n + 1)
                for t in range(T):
                    last = pe.matmul(bank[:, 7, t * 128:(t + 1) * 128], ctxT[:, t * 128:(t + 1) * 128],
                                     w_o[:, layer(n)], start=True, stop=True)
                last.then_inc(proj_done, 1)

            def b4(n):
                pe.wait_ge(xn2_ready, 2 * (n + 1))
                for t in range(T):
                    last = pe.transpose(bank[:, 7, t * 128:(t + 1) * 128], xn2[:, t], eye)
                last.then_inc(xn2_turned, 1)

            def b5(n, half):
                if half == 0:
                    pe.wait_ge(xn2T_ready, n + 1)
                    pe.wait_ge(w1_landed, 16 * (layer(n) + 1))
                else:
                    pe.wait_ge(v_ready, capped(2 * (n + 6), 2 * N))
                    pe.wait_ge(negrows_ready, capped(n + 3, N))
                b = 7 - half
                for i in range(2):
                    c = 2 * half + i
                    last = pe.matmul(bank[:, b, i * S:(i + 1) * S], w_1[:, c * 128:(c + 1) * 128], xn2T[:],
                                     start=True, stop=True)
                last.then_inc(up_done, 1)

            def b6(n):
                pe.wait_ge(gelu_done, FC * (n + 1))
                for t in range(T):
                    for c in range(FC):
                        last = pe.matmul(bank[:, 7, t * 128:(t + 1) * 128], hidden[:, c, t * 128:(t + 1) * 128],
                                         w_2[:, layer(n), c], start=(c == 0), stop=(c == FC - 1))
                last.then_inc(down_done, 1)

            pe.wait_ge(consts_landed, 16 * CONST_DMAS)
            pe.wait_ge(keys_landed, 16 * RING)
            pe.wait_ge(consts_cast, 4)
            pe.wait_ge(prefilled, 2)

            def slot(s, u):
                for k in range(STEPS):
                    if live(s - 2):
                        m_bank(s - 2, u - 2, k)
                    if k < 4 and live(s - 4):
                        a_bank(s - 4, u - 4, k + 8)
                    if k >= 4 and live(s - 3):
                        a_bank(s - 3, u - 3, k - 4)
                    if k == 9 and live(s - 3):
                        pv(s - 3, u - 3, 0)
                    if k in (0, 3, 6) and live(s - 4):
                        pv(s - 4, u - 4, 1 + k // 3)
                    if k == 0 and live(s):
                        f1(s)
                    if k == 1 and live(s - 3):
                        m1(s - 3)
                    if k in (2, 3) and live(s):
                        f2(s, k - 2)
                    if k == 2 and live(s - 5):
                        b4(s - 5)
                    if k == 3 and live(s - 5):
                        b5(s - 5, 0)
                    if k == 4 and live(s - 5):
                        b5(s - 5, 1)
                    if k == 7 and live(s - 5):
                        b6(s - 5)
                    if k in (8, 9) and live(s - 4):
                        b1(s - 4, k - 8)
                    if k == 10 and live(s - 4):
                        b2(s - 4)
                    if k == 11 and live(s - 4):
                        b3(s - 4)
                    if k in (8, 9, 10) and live(s):
                        f3(s, k - 8)

            slots(pe, slot)

        @block.scalar
        def _(act):
            def exp_bank(n, k):
                act.wait_ge(scoresT_done, STEPS * n + k + 1)
                at_least(act, context_done, 4 * n + (k - PR) // 3 + 1)
                act.activation(probs[:, k % PR], bank[:, 2 + k % 2, :], ACT.Exp, scale=SCALE).then_inc(exp_done, 1)

            def xn1T_out(n):
                act.wait_ge(xn1_turned, n + 1)
                at_least(act, qkv_done, 2 * n)
                act.activation(xn1T[:], bank[:, 5, 0:S], ACT.Identity, scale=ln_cols[:, layer(n), 0:1],
                               bias=ln_cols[:, layer(n), 1:2]).then_inc(xn1T_ready, 1)

            def xn2T_out(n):
                act.wait_ge(xn2_turned, n + 1)
                at_least(act, up_done, 2 * n)
                act.activation(xn2T[:], bank[:, 7, 0:S], ACT.Identity, scale=ln_cols[:, layer(n), 2:3],
                               bias=ln_cols[:, layer(n), 3:4]).then_inc(xn2T_ready, 1)

            def parts_out(n, u, j):
                act.wait_ge(parts_turned, 3 * n + j + 1)
                if j == 0 and not (isinstance(n, int) and n < 2):
                    act.wait_ge(stack_landed[(u - 2) % RING], 16 * STACK_DMAS * ((n - 2) // RING + 1))
                act.copy(base[:, u % 2, j].rearrange("p s c -> p (s c)"), bank16(5 + j % 2)[:, 0:3 * S]
                         ).then_inc(base_ready, 1)

            def context_copy(n, half):
                act.wait_ge(context_done, 4 * n + 2 * half + 2)
                at_least(act, context_turned, 2 * n)
                act.copy(ctxT_raw[:, 2 * half:2 * half + 2].rearrange("p g c -> p (g c)"), bank[:, 4, :]
                         ).then_inc(context_out, 1)

            def ctxT_out(n):
                act.wait_ge(ctx_turned, n + 1)
                at_least(act, proj_done, n)
                act.copy(ctxT[:], bank[:, 7, 0:S]).then_inc(ctxT_ready, 1)

            def gelu(n):
                for c in range(FC):
                    act.wait_ge(up_done, 2 * n + c // 2 + 1)
                    if c == 0:
                        at_least(act, down_done, n)
                    act.activation(hidden[:, c], bank[:, 7 - c // 2, (c % 2) * S:(c % 2 + 1) * S], ACT.Gelu,
                                   bias=b_1[:, layer(n), c:c + 1]).then_inc(gelu_done, 1)

            act.wait_ge(consts_landed, 16 * CONST_DMAS)

            def slot(s, u):
                for k in range(STEPS):
                    if k < 4 and live(s - 4):
                        exp_bank(s - 4, k + 8)
                    if k >= 4 and live(s - 3):
                        exp_bank(s - 3, k - 4)
                    if k == 0 and live(s):
                        xn1T_out(s)
                    if k == 1 and live(s - 4):
                        context_copy(s - 4, 0)
                    if k == 7 and live(s - 4):
                        context_copy(s - 4, 1)
                    if k == 2 and live(s - 5):
                        xn2T_out(s - 5)
                    if k == 5 and live(s - 5):
                        gelu(s - 5)
                    if k == 10 and live(s - 4):
                        ctxT_out(s - 4)
                    if k in (8, 9, 10) and live(s):
                        parts_out(s, u, k - 8)

            slots(act, slot)

        @block.vector
        def _(dve):
            dve.memset(expo[:], -0.5).then_inc(prefilled, 1)
            dve.wait_ge(squares_landed, 32)
            dve.tensor_copy(keys_b[:], keys_f[:]).then_inc(consts_cast, 1)
            dve.tensor_copy(eyeb[:], eye).then_inc(consts_cast, 1)
            dve.tensor_copy(mask[:], squares[:, 1:2].broadcast_to([128, 4, 128])).then_inc(consts_cast, 1)
            dve.tensor_copy(maskT[:], squares[:, 2:3].broadcast_to([128, 4, 128])).then_inc(consts_cast, 1)
            dve.wait_ge(x_landed, 16 * X_DMAS)
            with dve.Fori(0, B // PER) as c:
                for i in range(PER * T):
                    last = dve.bn_stats(stats0[:, i], h_all[:, c * PER + i // T, i % T])
                last.then_inc(stats0_done, 1)
                wait_alone(dve, stats0_done, c + 1, apart_dve)
                for i in range(PER * T):
                    last = dve.bn_aggr(mv0[:, i], stats0[:, i])
                last.then_inc(mv0_ready, 1)
                dve.wait_ge(rstd0_ready, c + 1)
                for i in range(PER * T):
                    tile = h_all[:, c * PER + i // T, i % T]
                    last = dve.tensor_scalar(tile, tile, mv0[:, i, 0:1], rstd0[:, i:i + 1], ALU.subtract, ALU.mult)
                last.then_inc(ln0_done, 1)
            dve.wait_ge(ln0_done, B // PER)

            def norm_stats(stats, mv, stats_sem, mv_sem, n):
                b = mod(n, B)
                for t in range(T):
                    last = dve.bn_stats(stats[:, t], h_all[:, b, t])
                last.then_inc(stats_sem, 1)
                wait_alone(dve, stats_sem, n + 1, apart_dve)
                for t in range(T):
                    last = dve.bn_aggr(mv[:, t], stats[:, t])
                last.then_inc(mv_sem, 1)

            def norm_apply(xn, mv, rstd, rstd_sem, used_sem, xn_sem, n):
                b = mod(n, B)
                dve.wait_ge(rstd_sem, n + 1)
                at_least(dve, used_sem, n)
                for t in range(T):
                    dve.tensor_scalar(xn[:, t], h_all[:, b, t], mv[:, t, 0:1], rstd[:, t:t + 1],
                                      ALU.subtract, ALU.mult).then_inc(xn_sem, 1)

            def stats_1(n):
                norm_stats(stats1, mv1, stats1_done, mv1_ready, n)

            def apply_1(n):
                norm_apply(xn1, mv1, rstd1, rstd1_ready, xn1_turned, xn1_ready, n)

            def stats_2(n):
                wait_alone(dve, h1_ready, n + 1, apart_dve)
                norm_stats(stats2, mv2, stats2_done, mv2_ready, n)

            def apply_2(n):
                norm_apply(xn2, mv2, rstd2, rstd2_ready, xn2_turned, xn2_ready, n)

            def qkv_out(n, u, t):
                dve.wait_ge(qkv_done, 2 * n + t + 1)
                at_least(dve, rot_ready, n)
                dve.tensor_tensor(feats[:, t, 0:2].rearrange("p s c -> p (s c)"), bank[:, 5 + t, 0:2 * D],
                                  b_qkv[:, layer(n), 0:2 * D], ALU.add).then_inc(qk_ready, 1)
                at_least(dve, vpad_ready, n - 3)
                dve.tensor_tensor(v_tok[:, u % RING, t], bank[:, 5 + t, 2 * D:3 * D],
                                  b_qkv[:, layer(n), 2 * D:3 * D], ALU.add).then_inc(v_ready, 1)

            def split(n, lo, hi, split_sem):
                x, r = feats[:, :, lo:hi], rest[:, :, lo:hi]
                p = [parts[:, :, j, lo:hi] for j in range(3)]
                if lo == 0:
                    dve.wait_ge(qk_ready, 2 * (n + 1))
                    at_least(dve, parts_turned, 3 * n)
                dve.tensor_copy(p[0], x).then_inc(split_sem, 1)
                dve.wait_ge(split_sem, 4 * n + 1)
                dve.tensor_tensor(r, x, p[0], ALU.subtract).then_inc(split_sem, 1)
                dve.wait_ge(split_sem, 4 * n + 2)
                dve.tensor_copy(p[1], r).then_inc(split_sem, 1)
                dve.wait_ge(split_sem, 4 * n + 3)
                dve.tensor_tensor(p[2], r, p[1], ALU.subtract).then_inc(split_sem, 1)

            def max_bank(n, u, k):
                dve.wait_ge(scores_done, STEPS * n + k + 1)
                p = u % 2
                if k < 4:
                    o, i = negmax[:, p, 0, 4 * k:4 * k + 4], bank[:, k % 2, :].rearrange("p (h c) -> p h c", h=4)
                else:
                    j = 2 * (k - 4)
                    o, i = negmax[:, p, 1, j:j + 2], bank[:, k % 2, :].rearrange("p (h c) -> p h c", h=2)
                dve.tensor_reduce(o, i, AX_X, ALU.max, negate=True).then_inc(max_done, 1)

            def neg_parts(n, u):
                dve.wait_ge(max_done, STEPS * (n + 1))
                at_least(dve, neg_turned, n)
                m = negmax[:, u % 2]
                dve.tensor_copy(negparts[:, :, 0], m).then_inc(neg_split, 1)
                dve.wait_ge(neg_split, 2 * n + 1)
                dve.tensor_tensor(negparts[:, :, 1], m, negparts[:, :, 0], ALU.subtract).then_inc(neg_split, 1)

            def negrows_out(n):
                dve.wait_ge(neg_turned, n + 1)
                at_least(dve, negrows_landed, 32 * n)
                dve.tensor_copy(negrows[:], bank16(6)[0:2 * H, 0:S]).then_inc(negrows_ready, 1)

            def divide(n, t):
                dve.wait_ge(context_turned, 2 * n + t + 1)
                v = bank[:, 7, :].rearrange("p (h w) -> p h w", w=32)
                dve.reciprocal(rsum[:, t], v[:, :, HD]).then_inc(rsum_ready, 1)
                dve.wait_ge(rsum_ready, 2 * n + t + 1)
                at_least(dve, ctx_turned, n)
                dve.tensor_tensor(ctx_tok[:, t].rearrange("p (h w) -> p h w", w=HD), v[:, :, 0:HD],
                                  rsum[:, t].unsqueeze(2).broadcast_to([128, H, HD]), ALU.mult
                                  ).then_inc(ctx_ready, 1)

            def resid_1(n):
                b = mod(n, B)
                dve.wait_ge(proj_done, n + 1)
                dve.wait_ge(bo_added, n + 1)
                h = h_all[:, b].rearrange("p t c -> p (t c)")
                dve.tensor_tensor(h, bank[:, 7, 0:S], h, ALU.add).then_inc(h1_ready, 1)

            def resid_2(n):
                b = mod(n, B)
                dve.wait_ge(down_done, n + 1)
                dve.wait_ge(b2_added, n + 1)
                h = h_all[:, b].rearrange("p t c -> p (t c)")
                dve.tensor_tensor(h, bank[:, 7, 0:S], h, ALU.add).then_inc(h2_ready, 1)

            dve.wait_ge(consts_landed, 16 * CONST_DMAS)

            def slot(s, u):
                if live(s - 3):
                    neg_parts(s - 3, u - 3)
                for k in range(STEPS):
                    if live(s - 2):
                        max_bank(s - 2, u - 2, k)
                    if k == 1 and live(s - 5):
                        apply_2(s - 5)
                    if k == 1 and live(s - 3):
                        negrows_out(s - 3)
                    if k in (2, 3) and live(s):
                        qkv_out(s, u, k - 2)
                    if k == 4 and live(s):
                        split(s, 0, 2, qk_split)
                    if k == 5 and live(s + 1):
                        stats_1(s + 1)
                    if k == 7 and live(s):
                        dve.wait_ge(rot_ready, s + 1)
                        split(s, 2, 3, rot_split)
                    if k == 7 and live(s - 5):
                        resid_2(s - 5)
                    if k in (8, 9) and live(s - 4):
                        divide(s - 4, k - 8)
                    if k == 10 and live(s + 1):
                        apply_1(s + 1)
                    if k == 11 and live(s - 4):
                        resid_1(s - 4)
                        stats_2(s - 4)

            slots(dve, slot)

        @block.gpsimd
        def _(pool):
            pool.memset(v_pad[:], 0.0).then_inc(zeros_filled, 1)
            pool.wait_ge(zeros_filled, 1)
            pool.memset(v_pad[:, :, :, :, HD:HD + 1], 1.0).then_inc(prefilled, 1)
            pool.wait_ge(prefilled, 2)
            with pool.Fori(0, B // PER) as c:
                wait_alone(pool, mv0_ready, c + 1, apart_pool)
                pool.tensor_scalar(ve0[:], mv0[:, :, 1], 1e-5, None, ALU.add).then_inc(ve0_ready, 1)
                pool.wait_ge(ve0_ready, c + 1)
                pool.tensor_tensor(rstd0[:], ve0[:], expo[:, 0:PER * T], ALU.pow).then_inc(rstd0_ready, 1)
            pool.wait_ge(consts_landed, 16 * CONST_DMAS)

            def power(ve, mv, rstd, mv_sem, ve_sem, rstd_sem, n):
                wait_alone(pool, mv_sem, n + 1, apart_pool)
                pool.tensor_scalar(ve[:], mv[:, :, 1], 1e-6, None, ALU.add).then_inc(ve_sem, 1)
                pool.wait_ge(ve_sem, n + 1)
                pool.tensor_tensor(rstd[:], ve[:], expo[:, 0:T], ALU.pow).then_inc(rstd_sem, 1)

            def turned(n):
                pool.wait_ge(qk_ready, 2 * (n + 1))
                pool.tensor_tensor(qu[:], feats[:, :, 0], b_u[:, layer(n)].unsqueeze(1).broadcast_to([128, T, D]),
                                   ALU.add).then_inc(qu_ready, 1)
                pool.wait_ge(qu_ready, n + 1)
                hf = D // 2
                pool.tensor_tensor(turn_s[:], qu[:], turn[:, 0], ALU.mult)
                pool.tensor_tensor(turn_c[:, :, 0:hf], qu[:, :, hf:D], turn[:, 1, :, 0:hf], ALU.mult)
                pool.tensor_tensor(turn_c[:, :, hf:D], qu[:, :, 0:hf], turn[:, 1, :, hf:D], ALU.mult
                                   ).then_inc(turn_steps, 1)
                pool.wait_ge(turn_steps, n + 1)
                at_least(pool, rot_split, 4 * n)
                pool.tensor_tensor(feats[:, :, 2], turn_s[:], turn_c[:], ALU.add).then_inc(rot_ready, 1)

            def v_padded(n, u):
                pool.wait_ge(v_ready, 2 * (n + 1))
                wait_alone(pool, context_done, 4 * (n - 1), apart_pool)
                pool.tensor_copy(v_pad[:, u % 2, :, :, 0:HD],
                                 v_tok[:, u % RING].rearrange("p t (h w) -> p t h w", w=HD)
                                 ).then_inc(vpad_ready, 1)

            def add_row(n, rows, read_sem, value, added_sem):
                pool.wait_ge(read_sem, value)
                h = h_all[:, mod(n, B)]
                pool.tensor_tensor(h, h, rows[:, layer(n)].unsqueeze(1).broadcast_to([128, T, D]), ALU.add
                                   ).then_inc(added_sem, 1)

            def slot(s, u):
                for k in range(STEPS):
                    if k == 0 and live(s - 5):
                        power(ve2, mv2, rstd2, mv2_ready, ve2_ready, rstd2_ready, s - 5)
                    if k == 2 and live(s - 5):
                        add_row(s - 5, b_2, xn2_ready, 2 * (s - 4), b2_added)
                    if k == 3 and live(s):
                        turned(s)
                    if k == 6 and live(s + 1):
                        power(ve1, mv1, rstd1, mv1_ready, ve1_ready, rstd1_ready, s + 1)
                    if k == 8 and live(s - 2):
                        v_padded(s - 2, u - 2)
                    if k == 9 and live(s - 4):
                        add_row(s - 4, b_o, xn1_ready, 2 * (s - 3), bo_added)

            slots(pool, slot)


def experts_program(nc, a, h_all, out):
    with ExitStack() as ctx:
        def sb(name, shape, dt=F32):
            return ctx.enter_context(nc.sbuf_tensor(name, shape, dt))

        def sem(name):
            return ctx.enter_context(nc.semaphore(name))

        bank = ctx.enter_context(nc.psum_tensor("ebank", [128, 8, 512], F32))

        w_in = sb("w_in", [128, 2 * GU])
        w_down = sb("w_down", [128, GU // 128, D])
        w_router = sb("w_router", [128, E])
        bias_rows = sb("bias_rows", [128, E])
        eye = sb("eeye", [128, 128])
        expo = sb("eexpo", [128, 1])
        XR = 4
        xin = sb("xin", [128, XR, D])
        stats = sb("estats", [128, 6])
        mv = sb("emv", [128, 2])
        ve = sb("eve", [128, 1])
        rstd = sb("erstd", [128, 1])
        xn = sb("exn", [128, D])
        xT = sb("exT", [128, 2, 128])
        score = sb("score", [128, 2, E])
        sb16 = sb("sb16", [128, E])
        pairs = sb("pairs", [128, 2, G, 2])
        tops = sb("tops", [128, 3, G])
        gs = sb("gs", [128, 14])
        gtop = sb("gtop", [128, 8])
        grep = sb("grep", [128, 8])
        gout = sb("gout", [128, 10])
        pen = sb("pen", [128, G])
        cand = sb("cand", [128, E + 4])
        ctop = sb("ctop", [128, 8])
        crep = sb("crep", [128, 8])
        cout = sb("cout", [128, E + 4])
        chosen = sb("chosen", [128, E])
        wsel = sb("wsel", [128, E])
        wsum = sb("wsum", [128, 2])
        winv = sb("winv", [128, 1])
        combine = sb("combine", [128, 2, E])
        gate_sig = sb("gate_sig", [128, 2, GU])
        gated = sb("gated", [128, GU])
        act_all = sb("act_all", [128, 2, GU])
        hw = sb("hw", [128, 2, E * EH])
        hT = sb("hT", [128, GU // 128, 128])
        ot = sb("ot", [128, XR, D])

        weights_landed = sem("weights_landed")
        apart_dve, apart_pool, apart_sp = (sem(f"eapart_{e}") for e in ("dve", "pool", "sp"))
        xin_landed = [sem(f"xin_landed{i}") for i in range(XR)]
        filled = sem("filled")
        x1_ready = sem("x1_ready")
        stats_done = sem("estats_done")
        mv_ready = sem("emv_ready")
        ve_ready = sem("eve_ready")
        rstd_ready = sem("erstd_ready")
        xn_ready = sem("exn_ready")
        xn_turned = sem("exn_turned")
        xT_ready = sem("exT_ready")
        logits_done = sem("logits_done")
        score_ready = sem("score_ready")
        route = sem("route")
        combine_ready = sem("combine_ready")
        in_done = sem("in_done")
        sig_ready = sem("sig_ready")
        gated_ready = sem("gated_ready")
        act_ready = sem("act_ready")
        hw_ready = sem("hw_ready")
        h_turned = sem("h_turned")
        hT_ready = sem("hT_ready")
        down_done = sem("edown_done")
        out_ready = sem("out_ready")
        out_landed = [sem(f"out_landed{i}") for i in range(XR)]

        h_tiles = h_all[:].rearrange("p b t d -> p (b t) d")
        x_tiles = a["x"].rearrange("b (t p) d -> (b t) p d", p=128)
        out_tiles = out.rearrange("b (t p) d -> (b t) p d", p=128)
        WEIGHT_DMAS = 5
        ROUTE = 17
        FIRST, LAST = 2, 15

        def live(n):
            return not isinstance(n, int) or 0 <= n < NT

        def slots(eng, slot):
            for s in range(-2, 4 * FIRST):
                slot(s, s % 4)
            with eng.Fori(FIRST, LAST) as g:
                for u in range(4):
                    slot(4 * g + u, u)
            for s in range(4 * LAST, NT + 1):
                slot(s, s % 4)

        block = ctx.enter_context(nc.Block())

        @block.sync
        def _(sp):
            sp.dma_start(eye[:], a["c_squares"][:, 0:128]).then_inc(weights_landed, 16)

            def load(n, u):
                if live(n):
                    r = u % XR
                    wait_alone(sp, x1_ready, n - XR + 1, apart_sp)
                    sp.dma_start(xin[:, r], x_tiles[n]).then_inc(xin_landed[r], 16)

            load(0, 0)
            load(1, 1)
            sp.dma_start(w_router[:], a["router"]).then_inc(weights_landed, 16)
            sp.dma_start(bias_rows[:], a["correction"].rearrange("(o e) -> o e", o=1).broadcast_to([128, E])
                         ).then_inc(weights_landed, 16)
            sp.dma_start(w_in[:], a["w_in"]).then_inc(weights_landed, 16)
            sp.dma_start(w_down[:], a["w_down"].rearrange("(c p) n -> p c n", p=128)).then_inc(weights_landed, 16)

            def slot(s, u):
                if not (isinstance(s, int) and s < -2):
                    load(s + 4, u + 4)
                if live(s - 1):
                    r = (u - 1) % XR
                    wait_alone(sp, out_ready, s, apart_sp)
                    sp.dma_start(out_tiles[s - 1], ot[:, r]).then_inc(out_landed[r], 16)

            slots(sp, slot)
            for r in range(XR):
                sp.wait_ge(out_landed[r], 16 * (NT // XR))

        @block.tensor
        def _(pe):
            pe.wait_ge(weights_landed, 16 * WEIGHT_DMAS)

            def x_turn(n):
                pe.wait_ge(xn_ready, n + 1)
                at_least(pe, score_ready, n)
                pe.transpose(bank[:, 6, 0:128], xn[:], eye[:]).then_inc(xn_turned, 1)

            def router(n, u):
                pe.wait_ge(xT_ready, n + 1)
                pe.matmul(bank[:, 6, 0:E], xT[:, u % 2], w_router[:], start=True, stop=True
                          ).then_inc(logits_done, 1)

            def product(n, u, i):
                if i == 0:
                    at_least(pe, act_ready, n - 1)
                last = pe.matmul(bank[:, 3 * (u % 2) + i, :], xT[:, u % 2], w_in[:, i * 512:(i + 1) * 512],
                                 start=True, stop=True)
                if i == 2:
                    last.then_inc(in_done, 1)

            def h_turn(n, u, half):
                if half == 0:
                    pe.wait_ge(hw_ready, n + 1)
                    pe.wait_ge(act_ready, n + 1)
                    at_least(pe, out_ready, n)
                else:
                    pe.wait_ge(hT_ready, 2 * n + 1)
                for i in range(3):
                    c = 3 * half + i
                    src = hw[:, u % 2, c * 128:(c + 1) * 128] if c < E * EH // 128 else \
                        act_all[:, u % 2, c * 128:(c + 1) * 128]
                    last = pe.transpose(bank[:, 7, i * 128:(i + 1) * 128], src, eye[:])
                last.then_inc(h_turned, 1)

            def down(n):
                pe.wait_ge(hT_ready, 2 * (n + 1))
                for c in range(GU // 128):
                    last = pe.matmul(bank[:, 7, 0:D], hT[:, c], w_down[:, c], start=(c == 0),
                                     stop=(c == GU // 128 - 1))
                last.then_inc(down_done, 1)

            def slot(s, u):
                if live(s + 1):
                    x_turn(s + 1)
                if live(s - 1):
                    h_turn(s - 1, u - 1, 0)
                if live(s):
                    product(s, u, 0)
                if live(s - 1):
                    h_turn(s - 1, u - 1, 1)
                if live(s + 1):
                    router(s + 1, u + 1)
                if live(s):
                    product(s, u, 1)
                    product(s, u, 2)
                if live(s - 1):
                    down(s - 1)

            slots(pe, slot)

        @block.scalar
        def _(act):
            def slot(s, u):
                n = s + 1
                if live(n):
                    act.wait_ge(xn_turned, n + 1)
                    at_least(act, in_done, n - 1)
                    act.copy(xT[:, (u + 1) % 2], bank[:, 6, 0:128]).then_inc(xT_ready, 1)
                n = s - 1
                if live(n):
                    for half in range(2):
                        act.wait_ge(h_turned, 2 * n + half + 1)
                        if half == 0:
                            at_least(act, down_done, n)
                        act.copy(hT[:, 3 * half:3 * half + 3].rearrange("p c n -> p (c n)"), bank[:, 7, 0:384]
                                 ).then_inc(hT_ready, 1)
                n = s + 1
                if live(n):
                    act.wait_ge(logits_done, n + 1)
                    at_least(act, combine_ready, n - 1)
                    act.activation(score[:, (u + 1) % 2], bank[:, 6, 0:E], ACT.Sigmoid).then_inc(score_ready, 1)
                if live(s):
                    act.wait_ge(in_done, s + 1)
                    at_least(act, gated_ready, s - 1)
                    b = 3 * (u % 2)
                    act.activation(gate_sig[:, u % 2], bank[:, b:b + 3].rearrange("p b c -> p (b c)")[:, 0:GU],
                                   ACT.Sigmoid).then_inc(sig_ready, 1)

            slots(act, slot)

        @block.vector
        def _(dve):
            dve.memset(expo[:], -0.5)
            dve.memset(gs[:, 0:6], HIGH)
            dve.memset(gs[:, 10:14], LOW)
            dve.memset(grep[:], HIGH)
            dve.memset(cand[:, E:E + 4], HIGH)
            dve.memset(crep[:], HIGH).then_inc(filled, 1)
            dve.wait_ge(filled, 1)
            dve.wait_ge(weights_landed, 16 * WEIGHT_DMAS)

            def residual(n, u):
                r = u % XR
                dve.wait_ge(xin_landed[r], 16 * (n // XR + 1))
                dve.tensor_tensor(h_tiles[:, n], xin[:, r], h_tiles[:, n], ALU.add).then_inc(x1_ready, 1)
                wait_alone(dve, x1_ready, n + 1, apart_dve)
                dve.bn_stats(stats[:], h_tiles[:, n]).then_inc(stats_done, 1)
                wait_alone(dve, stats_done, n + 1, apart_dve)
                dve.bn_aggr(mv[:], stats[:]).then_inc(mv_ready, 1)

            def norm(n):
                dve.wait_ge(rstd_ready, n + 1)
                at_least(dve, xn_turned, n)
                dve.tensor_scalar(xn[:], h_tiles[:, n], mv[:, 0:1], rstd[:, 0:1], ALU.subtract, ALU.mult
                                  ).then_inc(xn_ready, 1)

            def routing(n, u):
                sc = score[:, u % 2]
                step = [0]

                def link(ins):
                    step[0] += 1
                    ins.then_inc(route, 1)
                    wait_alone(dve, route, ROUTE * n + step[0], apart_dve)

                dve.wait_ge(score_ready, n + 1)
                link(dve.tensor_tensor(sb16[:], sc, bias_rows[:], ALU.add))
                v = sb16[:].rearrange("p (g a b) -> p g a b", g=G, a=2)
                dve.tensor_tensor(pairs[:, 0], v[:, :, 0], v[:, :, 1], ALU.max)
                link(dve.tensor_tensor(pairs[:, 1], v[:, :, 0], v[:, :, 1], ALU.min))
                dve.tensor_tensor(tops[:, 0], pairs[:, 0, :, 0], pairs[:, 0, :, 1], ALU.max)
                dve.tensor_tensor(tops[:, 1], pairs[:, 0, :, 0], pairs[:, 0, :, 1], ALU.min)
                link(dve.tensor_tensor(tops[:, 2], pairs[:, 1, :, 0], pairs[:, 1, :, 1], ALU.max))
                link(dve.tensor_tensor(tops[:, 1], tops[:, 1], tops[:, 2], ALU.max))
                link(dve.tensor_tensor(gs[:, 6:10], tops[:, 0], tops[:, 1], ALU.add))
                link(dve.max(gtop[:], gs[:, 6:14]))
                link(dve.tensor_copy(grep[:, 0:2], gtop[:, 0:2]))
                link(dve.match_replace(gout[:], grep[:], gs[:, 0:10], LOW))
                link(dve.tensor_tensor(pen[:], gout[:, 6:10], gs[:, 6:10], ALU.is_equal))
                link(dve.tensor_scalar(pen[:], pen[:], LOW, None, ALU.mult))
                link(dve.tensor_tensor(cand[:, 0:E].rearrange("p (g k) -> p g k", g=G),
                                       sb16[:].rearrange("p (g k) -> p g k", g=G),
                                       pen[:].unsqueeze(2).broadcast_to([128, G, E // G]), ALU.add))
                link(dve.max(ctop[:], cand[:, 0:E]))
                link(dve.tensor_copy(crep[:, 0:4], ctop[:, 0:4]))
                link(dve.match_replace(cout[:], crep[:], cand[:], 2 * LOW / 2.1))
                link(dve.tensor_tensor(chosen[:], cout[:, 0:E], cand[:, 0:E], ALU.not_equal))
                link(dve.tensor_tensor_reduce(out=wsel[:], in0=chosen[:], in1=sc, scale=1.0, scalar=1e-20,
                                              op0=ALU.mult, op1=ALU.add, accum_out=wsum[:, 0:1]))
                link(dve.reciprocal(winv[:], wsum[:, 0:1]))
                at_least(dve, hw_ready, n - 1)
                dve.tensor_scalar(combine[:, u % 2], wsel[:], winv[:, 0:1], None, ALU.mult
                                  ).then_inc(combine_ready, 1)
                assert step[0] == ROUTE, step[0]

            def gating(n, u):
                g = bank[:, 3 * (u % 2):3 * (u % 2) + 3].rearrange("p b c -> p (b c)")
                dve.wait_ge(sig_ready, n + 1)
                dve.tensor_tensor(gated[:], g[:, 0:GU], gate_sig[:, u % 2], ALU.mult).then_inc(gated_ready, 1)
                dve.wait_ge(gated_ready, n + 1)
                at_least(dve, h_turned, 2 * (n - 1))
                at_least(dve, hw_ready, n - 1)
                dve.tensor_tensor(act_all[:, u % 2], g[:, GU:2 * GU], gated[:], ALU.mult).then_inc(act_ready, 1)

            def result(n, u):
                r = u % XR
                dve.wait_ge(down_done, n + 1)
                if not (isinstance(n, int) and n < XR):
                    dve.wait_ge(out_landed[r], 16 * (n // XR))
                dve.tensor_tensor(ot[:, r], bank[:, 7, 0:D], h_tiles[:, n], ALU.add).then_inc(out_ready, 1)

            def slot(s, u):
                if live(s + 2):
                    residual(s + 2, u + 2)
                if live(s + 1):
                    routing(s + 1, u + 1)
                if live(s + 2):
                    norm(s + 2)
                if live(s):
                    gating(s, u)
                if live(s - 1):
                    result(s - 1, u - 1)

            slots(dve, slot)

        @block.gpsimd
        def _(pool):
            pool.wait_ge(filled, 1)

            def slot(s, u):
                n = s + 2
                if live(n):
                    wait_alone(pool, mv_ready, n + 1, apart_pool)
                    pool.tensor_scalar(ve[:], mv[:, 1:2], 1e-5, None, ALU.add).then_inc(ve_ready, 1)
                    pool.wait_ge(ve_ready, n + 1)
                    pool.tensor_tensor(rstd[:], ve[:], expo[:], ALU.pow).then_inc(rstd_ready, 1)
                if live(s):
                    pool.wait_ge(combine_ready, s + 1)
                    pool.wait_ge(act_ready, s + 1)
                    at_least(pool, h_turned, 2 * (s - 1))
                    pool.tensor_tensor(hw[:, u % 2].rearrange("p (e h) -> p e h", e=E),
                                       act_all[:, u % 2, 0:E * EH].rearrange("p (e h) -> p e h", e=E),
                                       combine[:, u % 2].unsqueeze(2).broadcast_to([128, E, EH]), ALU.mult
                                       ).then_inc(hw_ready, 1)

            slots(pool, slot)


def kernel(**inputs):
    import concourse.bacc as bacc
    from concourse.bass_utils import run_bass_kernel_spmd

    def i(name):
        return np.asarray(inputs[name])

    def feature_major(w):
        return w.reshape(LAYERS, H, HD, D).transpose(0, 2, 1, 3).reshape(LAYERS, D, D)

    def feature_major_row(b):
        return b.reshape(LAYERS, H, HD).transpose(0, 2, 1).reshape(LAYERS, D)

    arrays = {
        "x": i("L0_attn_x"),
        "w_qkv": np.concatenate([feature_major(i("L0_attn_Wq")), feature_major(i("L0_attn_Wk")), i("L0_attn_Wv")],
                                axis=1).transpose(0, 2, 1),
        "b_qkv": np.concatenate([feature_major_row(i("L0_attn_bq")), feature_major_row(i("L0_attn_bk")),
                                 i("L0_attn_bv")], axis=1),
        "u": feature_major_row(i("L0_attn_u_bias")),
        "w_o": i("L0_attn_Wo").transpose(0, 2, 1),
        "bo": i("L0_attn_bo"),
        "w_1": i("L0_attn_W1").transpose(0, 2, 1),
        "b_1": i("L0_attn_b1").reshape(LAYERS * FC, 128).T,
        "w_2": i("L0_attn_W2").transpose(0, 2, 1),
        "b2": i("L0_attn_b2"),
        "ln_cols": np.stack([i("L0_attn_ln1_w"), i("L0_attn_ln1_b"), i("L0_attn_ln2_w"), i("L0_attn_ln2_b")],
                            axis=1).reshape(LAYERS * 4, D).T,
        "router": i("L0_ffn_router_w").T,
        "correction": i("L0_ffn_correction_bias"),
        "w_in": np.concatenate([i("L0_ffn_gate_w").transpose(1, 0, 2).reshape(D, E * EH),
                                i("L0_ffn_shared_gate_w").T,
                                i("L0_ffn_up_w").transpose(1, 0, 2).reshape(D, E * EH),
                                i("L0_ffn_shared_up_w").T], axis=1),
        "w_down": np.concatenate([i("L0_ffn_down_w").reshape(E * EH, D), i("L0_ffn_shared_down_w").T], axis=0),
    }
    arrays.update(position_tables())
    arrays = {f"in_{name}": np.ascontiguousarray(x) for name, x in arrays.items()}
    nc = bacc.Bacc("TRN2", target_bir_lowering=False, num_devices=1)
    a = {name[3:]: nc.dram_tensor(name, x.shape, mybir.dt.from_np(x.dtype), kind="ExternalInput").ap()
         for name, x in arrays.items()}
    out = nc.dram_tensor("out", (B, S, D), F32, kind="ExternalOutput").ap()
    with nc.sbuf_tensor("h_all", [128, B, T, D], F32) as h_all:
        layers_program(nc, a, h_all)
        experts_program(nc, a, h_all, out)
    r = run_bass_kernel_spmd(nc, [arrays], core_ids=[0])
    return r.results[0]["out"]
```

```python
from contextlib import ExitStack

import numpy as np

import concourse.bass as bass
from concourse import mybir

F32 = mybir.dt.float32
BF16 = mybir.dt.bfloat16
ALU = mybir.AluOpType
ACT = mybir.ActivationFunctionType
AX_X = mybir.AxisListType.X

B, S, D = 32, 256, 128
H, HD = 16, 8
LAYERS, DI = 4, 512
T = S // 128
N = LAYERS * B
FC = DI // 128
SCALE = HD ** -0.5
PARTS_Q = (0, 0, 0, 1, 1, 2)
PARTS_K = (0, 1, 2, 0, 1, 0)
NB = len(PARTS_Q)
ROT0 = NB * HD
MROW = 2 * NB * HD
STACK = MROW + 2
RING = 4
STEPS = 12
PR = 6
VW = 32
MASK = -1.0e30
STACK_DMAS = 3 * NB
PER = 4
E, G, EH = 16, 4, 32
HS = 256
NT = B * T
GU = E * EH + HS
HIGH, LOW = 3.0e38, -3.0e38


def wait_alone(eng, sem, value, apart):
    if not isinstance(value, int):
        eng.wait_ge(sem, value)
        eng.sem_inc(apart, 1)
    elif value > 0:
        eng.wait_ge(sem, value)


def at_least(eng, sem, value):
    if not isinstance(value, int) or value > 0:
        eng.wait_ge(sem, value)


def capped(value, most):
    return min(value, most) if isinstance(value, int) else value


def bf16_parts(x):
    parts = []
    for _ in range(3):
        bits = x.astype(np.float32).view(np.uint32).astype(np.uint64)
        bits = (bits + 0x7FFF + ((bits >> 16) & 1)) & 0xFFFF0000
        p = bits.astype(np.uint32).view(np.float32)
        parts.append(p)
        x = x - p.astype(np.float64)
    return parts


def position_tables():
    inv = (1.0 / np.float32(10000.0) ** (np.arange(0, HD, 2, dtype=np.float32) / np.float32(HD))).astype(np.float64)
    angle = np.arange(S, dtype=np.float64)[:, None] * inv[None, :]
    sin, cos = np.sin(angle), np.cos(angle)
    turn = np.zeros((128, 2, T, D), np.float32)
    for t in range(T):
        rows = slice(t * 128, t * 128 + 128)
        s64 = np.repeat(sin[rows], H, axis=1)
        c64 = np.repeat(cos[rows], H, axis=1)
        turn[:, 0, t] = np.concatenate([s64, s64], axis=1)
        turn[:, 1, t] = np.concatenate([c64, -c64], axis=1)
    parts = bf16_parts(np.ascontiguousarray(np.concatenate([cos, sin], axis=1).T))
    keys = np.concatenate([parts[p] for p in PARTS_K] + [np.ones((2, S), np.float32)], axis=0)
    q, k = np.arange(128)[:, None], np.arange(128)[None, :]
    mask = np.where(k > q, np.float32(MASK), np.float32(0))
    squares = np.concatenate([np.eye(128, dtype=np.float32), mask, mask.T], axis=1)
    return {"c_turn": turn.reshape(128, -1), "c_keys": keys, "c_squares": squares}


def layers_program(nc, a, h_all):
    with ExitStack() as ctx:
        def sb(name, shape, dt=F32):
            return ctx.enter_context(nc.sbuf_tensor(name, shape, dt))

        def sem(name):
            return ctx.enter_context(nc.semaphore(name))

        bank = ctx.enter_context(nc.psum_tensor("bank", [128, 8, 512], F32))

        def bank16(i):
            return bank[:, i, :].bitcast(BF16)

        w_qkv = sb("w_qkv", [128, LAYERS, 3 * D])
        w_o = sb("w_o", [128, LAYERS, D])
        w_1 = sb("w_1", [128, DI])
        w_2 = sb("w_2", [128, LAYERS, FC, D])
        b_qkv = sb("b_qkv", [128, LAYERS, 3 * D])
        b_u = sb("b_u", [128, LAYERS, D])
        b_o = sb("b_o", [128, LAYERS, D])
        b_2 = sb("b_2", [128, LAYERS, D])
        ln_cols = sb("ln_cols", [128, LAYERS, 4])
        b_1 = sb("b_1", [128, LAYERS, FC])
        turn = sb("turn", [128, 2, T, D])
        mask = sb("mask", [128, 4, 128], BF16)
        maskT = sb("maskT", [128, 4, 128], BF16)
        squares = sb("squares", [128, 3, 128])
        eye = squares[:, 0]
        eyeb = sb("eyeb", [128, 128], BF16)
        keys_f = sb("keys_f", [STACK - ROT0, S])
        keys_b = sb("keys_b", [STACK - ROT0, S], BF16)
        expo = sb("expo", [128, 16])

        stats0 = sb("stats0", [128, PER * T, 6])
        mv0 = sb("mv0", [128, PER * T, 2])
        ve0 = sb("ve0", [128, PER * T])
        rstd0 = sb("rstd0", [128, PER * T])

        stats1 = sb("stats1", [128, T, 6])
        mv1 = sb("mv1", [128, T, 2])
        ve1 = sb("ve1", [128, T])
        rstd1 = sb("rstd1", [128, T])
        xn1 = sb("xn1", [128, T, D])
        xn1T = sb("xn1T", [128, S])
        feats = sb("feats", [128, T, 3, D])
        qu = sb("qu", [128, T, D])
        turn_s = sb("turn_s", [128, T, D])
        turn_c = sb("turn_c", [128, T, D])
        rest = sb("rest", [128, T, 3, D])
        parts = sb("parts", [128, T, 3, 3, D], BF16)
        base = sb("base", [128, 2, 3, 3, S], BF16)
        v_tok = sb("v_tok", [128, RING, T, D])
        v_pad = sb("v_pad", [128, 2, T, H, VW])
        qstack = sb("qstack", [STACK, RING, H, S], BF16)
        kstack = sb("kstack", [STACK, RING, H, S], BF16)
        negmax = sb("negmax", [128, 2, T, H])
        negparts = sb("negparts", [128, T, 2, H], BF16)
        negrows = sb("negrows", [2 * H, S], BF16)
        probs = sb("probs", [128, PR, 512])
        ctxT_raw = sb("ctxT_raw", [128, 4, S])
        rsum = sb("rsum", [128, T, H])
        ctx_tok = sb("ctx_tok", [128, T, D])
        ctxT = sb("ctxT", [128, S])
        stats2 = sb("stats2", [128, T, 6])
        mv2 = sb("mv2", [128, T, 2])
        ve2 = sb("ve2", [128, T])
        rstd2 = sb("rstd2", [128, T])
        xn2 = sb("xn2", [128, T, D])
        xn2T = sb("xn2T", [128, S])
        hidden = sb("hidden", [128, FC, S])

        x_landed = sem("x_landed")
        consts_landed = sem("consts_landed")
        keys_landed = sem("keys_landed")
        squares_landed = sem("squares_landed")
        consts_cast = sem("consts_cast")
        prefilled = sem("prefilled")
        zeros_filled = sem("zeros_filled")
        apart_dve, apart_pool, apart_sp = (sem(f"apart_{e}") for e in ("dve", "pool", "sp"))
        stats0_done = sem("stats0_done")
        mv0_ready = sem("mv0_ready")
        ve0_ready = sem("ve0_ready")
        rstd0_ready = sem("rstd0_ready")
        ln0_done = sem("ln0_done")
        w1_landed = sem("w1_landed")
        stats1_done = sem("stats1_done")
        mv1_ready = sem("mv1_ready")
        ve1_ready = sem("ve1_ready")
        rstd1_ready = sem("rstd1_ready")
        xn1_ready = sem("xn1_ready")
        xn1_turned = sem("xn1_turned")
        xn1T_ready = sem("xn1T_ready")
        qkv_done = sem("qkv_done")
        qk_ready = sem("qk_ready")
        v_ready = sem("v_ready")
        qu_ready = sem("qu_ready")
        turn_steps = sem("turn_steps")
        rot_ready = sem("rot_ready")
        qk_split = sem("qk_split")
        rot_split = sem("rot_split")
        parts_turned = sem("parts_turned")
        base_ready = sem("base_ready")
        stack_landed = [sem(f"stack_landed{i}") for i in range(RING)]
        vpad_ready = sem("vpad_ready")
        scores_done = sem("scores_done")
        max_done = sem("max_done")
        neg_split = sem("neg_split")
        neg_turned = sem("neg_turned")
        negrows_ready = sem("negrows_ready")
        negrows_landed = sem("negrows_landed")
        scoresT_done = sem("scoresT_done")
        exp_done = sem("exp_done")
        context_done = sem("context_done")
        context_out = sem("context_out")
        context_turned = sem("context_turned")
        rsum_ready = sem("rsum_ready")
        ctx_ready = sem("ctx_ready")
        ctx_turned = sem("ctx_turned")
        ctxT_ready = sem("ctxT_ready")
        proj_done = sem("proj_done")
        bo_added = sem("bo_added")
        h1_ready = sem("h1_ready")
        stats2_done = sem("stats2_done")
        mv2_ready = sem("mv2_ready")
        ve2_ready = sem("ve2_ready")
        rstd2_ready = sem("rstd2_ready")
        xn2_ready = sem("xn2_ready")
        xn2_turned = sem("xn2_turned")
        xn2T_ready = sem("xn2T_ready")
        up_done = sem("up_done")
        gelu_done = sem("gelu_done")
        down_done = sem("down_done")
        b2_added = sem("b2_added")
        h2_ready = sem("h2_ready")

        x_tiles = a["x"].rearrange("b (t p) d -> p b t d", p=128)
        X_DMAS = B // PER

        def mod(n, m):
            return n % m

        def layer(n):
            return n // B

        CONST_DMAS = 10

        FIRST_LOOP, LAST_LOOP = 2, 31
        LAST_SLOT = N + 5

        def slots(eng, slot):
            for s in range(-1, 4 * FIRST_LOOP):
                slot(s, s % 4)
            with eng.Fori(FIRST_LOOP, LAST_LOOP) as g:
                for u in range(4):
                    slot(4 * g + u, u)
            for s in range(4 * LAST_LOOP, LAST_SLOT):
                slot(s, s % 4)

        def live(n):
            return not isinstance(n, int) or 0 <= n < N

        block = ctx.enter_context(nc.Block())

        @block.sync
        def _(sp):
            sp.dma_start(squares[:], a["c_squares"].rearrange("p (a n) -> p a n", a=3)).then_inc(squares_landed, 16)
            sp.dma_start(keys_f[:], a["c_keys"]).then_inc(squares_landed, 16)
            for c in range(X_DMAS):
                w = B // X_DMAS
                sp.dma_start(h_all[:, c * w:(c + 1) * w], x_tiles[:, c * w:(c + 1) * w]).then_inc(x_landed, 16)
            sp.dma_start(w_qkv[:], a["w_qkv"].rearrange("l p n -> p l n")).then_inc(consts_landed, 16)
            sp.dma_start(ln_cols[:], a["ln_cols"].rearrange("p (l c) -> p l c", l=LAYERS)).then_inc(consts_landed, 16)
            sp.dma_start(b_qkv[:], a["b_qkv"].rearrange("(o l) n -> o l n", o=1).broadcast_to([128, LAYERS, 3 * D])).then_inc(consts_landed, 16)
            sp.dma_start(b_u[:], a["u"].rearrange("(o l) n -> o l n", o=1).broadcast_to([128, LAYERS, D])).then_inc(consts_landed, 16)
            sp.dma_start(turn[:], a["c_turn"].rearrange("p (a t n) -> p a t n", a=2, t=T)).then_inc(consts_landed, 16)
            sp.wait_ge(consts_cast, 4)
            for r in range(RING):
                sp.dma_start(kstack[ROT0:STACK, r], keys_b[:].unsqueeze(1).broadcast_to([STACK - ROT0, H, S])
                             ).then_inc(keys_landed, 16)
            sp.dma_start(b_o[:], a["bo"].rearrange("(o l) n -> o l n", o=1).broadcast_to([128, LAYERS, D])).then_inc(consts_landed, 16)
            sp.dma_start(b_2[:], a["b2"].rearrange("(o l) n -> o l n", o=1).broadcast_to([128, LAYERS, D])).then_inc(consts_landed, 16)
            sp.dma_start(w_o[:], a["w_o"].rearrange("l p n -> p l n")).then_inc(consts_landed, 16)
            sp.dma_start(b_1[:], a["b_1"].rearrange("p (l c) -> p l c", l=LAYERS)).then_inc(consts_landed, 16)
            sp.dma_start(w_2[:], a["w_2"].rearrange("l (c p) n -> p l c n", p=128)).then_inc(consts_landed, 16)
            sp.dma_start(w_1[:], a["w_1"][0]).then_inc(w1_landed, 16)

            def slot(s, u):
                n, r = s - 3, (u - 3) % RING
                if live(n):
                    wait_alone(sp, negrows_ready, n + 1, apart_sp)
                    for i in range(2):
                        sp.dma_start(qstack[MROW + i:MROW + i + 1, r], negrows[i * H:(i + 1) * H, :]
                                     ).then_inc(negrows_landed, 16)
                n, r = s - 1, (u - 1) % RING
                if live(n):
                    wait_alone(sp, base_ready, 3 * (n + 1), apart_sp)
                    wait_alone(sp, scoresT_done, STEPS * (n - 3), apart_sp)
                    for c in range(NB):
                        rows = slice(c * HD, (c + 1) * HD)
                        rot_rows = slice(ROT0 + c * HD, ROT0 + (c + 1) * HD)
                        p = r % 2
                        sp.dma_start(qstack[rows, r], base[:, p, PARTS_Q[c], 0]).then_inc(stack_landed[r], 16)
                        sp.dma_start(kstack[rows, r], base[:, p, PARTS_K[c], 1]).then_inc(stack_landed[r], 16)
                        sp.dma_start(qstack[rot_rows, r], base[:, p, PARTS_Q[c], 2]).then_inc(stack_landed[r], 16)

            def next_w1(ly):
                sp.wait_ge(up_done, 2 * B * ly)
                sp.dma_start(w_1[:], a["w_1"][ly]).then_inc(w1_landed, 16)

            for s in range(-1, 4 * FIRST_LOOP):
                slot(s, s % 4)
            g0 = FIRST_LOOP
            for ly in range(1, LAYERS):
                g1 = (B * ly + 4) // 4
                with sp.Fori(g0, g1) as g:
                    for u in range(4):
                        slot(4 * g + u, u)
                slot(4 * g1, 0)
                next_w1(ly)
                for u in range(1, 4):
                    slot(4 * g1 + u, u)
                g0 = g1 + 1
            with sp.Fori(g0, LAST_LOOP) as g:
                for u in range(4):
                    slot(4 * g + u, u)
            for s in range(4 * LAST_LOOP, LAST_SLOT):
                slot(s, s % 4)

        @block.tensor
        def _(pe):
            def f1(n):
                pe.wait_ge(xn1_ready, 2 * (n + 1))
                at_least(pe, base_ready, 3 * n)
                for t in range(T):
                    last = pe.transpose(bank[:, 5, t * 128:(t + 1) * 128], xn1[:, t], eye)
                last.then_inc(xn1_turned, 1)

            def f2(n, t):
                b = 5 + t
                pe.wait_ge(xn1T_ready, n + 1)
                if t == 1:
                    at_least(pe, negrows_ready, n - 2)
                pe.matmul(bank[:, b, 0:3 * D], xn1T[:, t * 128:(t + 1) * 128], w_qkv[:, layer(n)],
                          start=True, stop=True).then_inc(qkv_done, 1)

            def f3(n, j):
                b = 5 + j % 2
                need = (1, 3, 4)[j]
                pe.wait_ge(qk_split, 4 * n + need)
                pe.wait_ge(rot_split, 4 * n + need)
                if j == 0:
                    pe.wait_ge(v_ready, 2 * n + 1)
                if j == 1:
                    pe.wait_ge(v_ready, 2 * n + 2)
                    at_least(pe, gelu_done, FC * (n - 4))
                if j == 2:
                    pe.wait_ge(base_ready, 3 * n + 1)
                o = bank16(b)[:, 0:3 * S].rearrange("p (s t c) -> p s t c", s=3, t=T)
                for src in range(3):
                    for t in range(T):
                        last = pe.transpose(o[:, src, t], parts[:, t, j, src], eyeb[:])
                last.then_inc(parts_turned, 1)

            def m_bank(n, u, k):
                r = u % RING
                if k == 0:
                    pe.wait_ge(stack_landed[r], 16 * STACK_DMAS * (n // RING + 1))
                at_least(pe, max_done, STEPS * n + k - 1)
                b = k % 2
                if k < 4:
                    pe.matmul(bank[:, b, :], eyeb[:], mask[:], start=True, stop=True)
                    for i in range(4):
                        hd = 4 * k + i
                        last = pe.matmul(bank[:, b, i * 128:(i + 1) * 128], qstack[0:MROW, r, hd, 0:128],
                                         kstack[0:MROW, r, hd, 0:128], start=False, stop=True,
                                         skip_group_check=True)
                else:
                    two = bank[:, b, :].rearrange("p (h k) -> p h k", h=2)
                    pe.matmul(two[:, :, 128:256], eyeb[:], mask[:, 0:2], start=True, stop=True)
                    for i in range(2):
                        hd = 2 * (k - 4) + i
                        last = pe.matmul(two[:, i], qstack[0:MROW, r, hd, 128:256], kstack[0:MROW, r, hd, :],
                                         start=False, stop=True, skip_group_check=True)
                last.then_inc(scores_done, 1)

            def m1(n):
                pe.wait_ge(neg_split, 2 * (n + 1))
                pe.wait_ge(base_ready, capped(3 * (n + 2) + 2, 3 * N))
                if isinstance(n, int) and n + 2 >= N:
                    pe.wait_ge(gelu_done, FC * (n - 2))
                for t in range(T):
                    last = pe.transpose(bank16(6)[0:2 * H, t * 128:(t + 1) * 128],
                                        negparts[:, t].rearrange("p a h -> p (a h)"), eyeb[:])
                last.then_inc(neg_turned, 1)

            def a_bank(n, u, k):
                r = u % RING
                if k == 0:
                    pe.wait_ge(negrows_landed, 32 * (n + 1))
                at_least(pe, exp_done, STEPS * n + k - 1)
                b = 2 + k % 2
                grp, kind = k // 3, k % 3
                if kind < 2:
                    two = bank[:, b, :].rearrange("p (h q) -> p h q", h=2)
                    pe.matmul(two[:, :, 0:128], eyeb[:], maskT[:, 0:2], start=True, stop=True)
                    for i in range(2):
                        hd = 4 * grp + 2 * kind + i
                        last = pe.matmul(two[:, i], kstack[:, r, hd, 0:128], qstack[:, r, hd, :],
                                         start=False, stop=True, skip_group_check=True)
                else:
                    pe.matmul(bank[:, b, :], eyeb[:], maskT[:], start=True, stop=True)
                    for i in range(4):
                        hd = 4 * grp + i
                        last = pe.matmul(bank[:, b, i * 128:(i + 1) * 128], kstack[:, r, hd, 128:256],
                                         qstack[:, r, hd, 128:256], start=False, stop=True, skip_group_check=True)
                last.then_inc(scoresT_done, 1)

            def pv(n, u, grp):
                pe.wait_ge(exp_done, STEPS * n + 3 * grp + 3)
                if grp == 0:
                    pe.wait_ge(vpad_ready, n + 1)
                if grp % 2 == 0:
                    at_least(pe, context_out, 2 * n + grp // 2)
                v = u % 2
                c0 = (grp % 2) * S
                for i in range(4):
                    hd = 4 * grp + i
                    p0 = probs[:, (3 * grp + i // 2) % PR, (i % 2) * S:(i % 2 + 1) * S]
                    pe.matmul(bank[32 * i:32 * i + VW, 4, c0:c0 + S], v_pad[:, v, 0, hd], p0,
                              start=True, stop=True, skip_group_check=True)
                for i in range(4):
                    hd = 4 * grp + i
                    p1 = probs[:, (3 * grp + 2) % PR, i * 128:(i + 1) * 128]
                    last = pe.matmul(bank[32 * i:32 * i + VW, 4, c0 + 128:c0 + S], v_pad[:, v, 1, hd], p1,
                                     start=False, stop=True, skip_group_check=True)
                last.then_inc(context_done, 1)

            def b1(n, t):
                if t == 0:
                    pe.wait_ge(context_out, 2 * (n + 1))
                    at_least(pe, h2_ready, n)
                else:
                    pe.wait_ge(ctx_ready, 2 * n + 1)
                for grp in range(4):
                    last = pe.transpose(bank[:, 7, grp * 128:(grp + 1) * 128],
                                        ctxT_raw[:, grp, t * 128:(t + 1) * 128], eye)
                last.then_inc(context_turned, 1)

            def b2(n):
                pe.wait_ge(ctx_ready, 2 * (n + 1))
                for t in range(T):
                    last = pe.transpose(bank[:, 7, t * 128:(t + 1) * 128], ctx_tok[:, t], eye)
                last.then_inc(ctx_turned, 1)

            def b3(n):
                pe.wait_ge(ctxT_ready, n + 1)
                for t in range(T):
                    last = pe.matmul(bank[:, 7, t * 128:(t + 1) * 128], ctxT[:, t * 128:(t + 1) * 128],
                                     w_o[:, layer(n)], start=True, stop=True)
                last.then_inc(proj_done, 1)

            def b4(n):
                pe.wait_ge(xn2_ready, 2 * (n + 1))
                for t in range(T):
                    last = pe.transpose(bank[:, 7, t * 128:(t + 1) * 128], xn2[:, t], eye)
                last.then_inc(xn2_turned, 1)

            def b5(n, half):
                if half == 0:
                    pe.wait_ge(xn2T_ready, n + 1)
                    pe.wait_ge(w1_landed, 16 * (layer(n) + 1))
                else:
                    pe.wait_ge(v_ready, capped(2 * (n + 6), 2 * N))
                    pe.wait_ge(negrows_ready, capped(n + 3, N))
                b = 7 - half
                for i in range(2):
                    c = 2 * half + i
                    last = pe.matmul(bank[:, b, i * S:(i + 1) * S], w_1[:, c * 128:(c + 1) * 128], xn2T[:],
                                     start=True, stop=True)
                last.then_inc(up_done, 1)

            def b6(n):
                pe.wait_ge(gelu_done, FC * (n + 1))
                for t in range(T):
                    for c in range(FC):
                        last = pe.matmul(bank[:, 7, t * 128:(t + 1) * 128], hidden[:, c, t * 128:(t + 1) * 128],
                                         w_2[:, layer(n), c], start=(c == 0), stop=(c == FC - 1))
                last.then_inc(down_done, 1)

            pe.wait_ge(consts_landed, 16 * CONST_DMAS)
            pe.wait_ge(keys_landed, 16 * RING)
            pe.wait_ge(consts_cast, 4)
            pe.wait_ge(prefilled, 2)

            def slot(s, u):
                for k in range(STEPS):
                    if live(s - 2):
                        m_bank(s - 2, u - 2, k)
                    if k < 4 and live(s - 4):
                        a_bank(s - 4, u - 4, k + 8)
                    if k >= 4 and live(s - 3):
                        a_bank(s - 3, u - 3, k - 4)
                    if k == 9 and live(s - 3):
                        pv(s - 3, u - 3, 0)
                    if k in (0, 3, 6) and live(s - 4):
                        pv(s - 4, u - 4, 1 + k // 3)
                    if k == 0 and live(s):
                        f1(s)
                    if k == 1 and live(s - 3):
                        m1(s - 3)
                    if k in (2, 3) and live(s):
                        f2(s, k - 2)
                    if k == 2 and live(s - 5):
                        b4(s - 5)
                    if k == 3 and live(s - 5):
                        b5(s - 5, 0)
                    if k == 4 and live(s - 5):
                        b5(s - 5, 1)
                    if k == 7 and live(s - 5):
                        b6(s - 5)
                    if k in (8, 9) and live(s - 4):
                        b1(s - 4, k - 8)
                    if k == 10 and live(s - 4):
                        b2(s - 4)
                    if k == 11 and live(s - 4):
                        b3(s - 4)
                    if k in (8, 9, 10) and live(s):
                        f3(s, k - 8)

            slots(pe, slot)

        @block.scalar
        def _(act):
            def exp_bank(n, k):
                act.wait_ge(scoresT_done, STEPS * n + k + 1)
                at_least(act, context_done, 4 * n + (k - PR) // 3 + 1)
                act.activation(probs[:, k % PR], bank[:, 2 + k % 2, :], ACT.Exp, scale=SCALE).then_inc(exp_done, 1)

            def xn1T_out(n):
                act.wait_ge(xn1_turned, n + 1)
                at_least(act, qkv_done, 2 * n)
                act.activation(xn1T[:], bank[:, 5, 0:S], ACT.Identity, scale=ln_cols[:, layer(n), 0:1],
                               bias=ln_cols[:, layer(n), 1:2]).then_inc(xn1T_ready, 1)

            def xn2T_out(n):
                act.wait_ge(xn2_turned, n + 1)
                at_least(act, up_done, 2 * n)
                act.activation(xn2T[:], bank[:, 7, 0:S], ACT.Identity, scale=ln_cols[:, layer(n), 2:3],
                               bias=ln_cols[:, layer(n), 3:4]).then_inc(xn2T_ready, 1)

            def parts_out(n, u, j):
                act.wait_ge(parts_turned, 3 * n + j + 1)
                if j == 0 and not (isinstance(n, int) and n < 2):
                    act.wait_ge(stack_landed[(u - 2) % RING], 16 * STACK_DMAS * ((n - 2) // RING + 1))
                act.copy(base[:, u % 2, j].rearrange("p s c -> p (s c)"), bank16(5 + j % 2)[:, 0:3 * S]
                         ).then_inc(base_ready, 1)

            def context_copy(n, half):
                act.wait_ge(context_done, 4 * n + 2 * half + 2)
                at_least(act, context_turned, 2 * n)
                act.copy(ctxT_raw[:, 2 * half:2 * half + 2].rearrange("p g c -> p (g c)"), bank[:, 4, :]
                         ).then_inc(context_out, 1)

            def ctxT_out(n):
                act.wait_ge(ctx_turned, n + 1)
                at_least(act, proj_done, n)
                act.copy(ctxT[:], bank[:, 7, 0:S]).then_inc(ctxT_ready, 1)

            def gelu(n):
                for c in range(FC):
                    act.wait_ge(up_done, 2 * n + c // 2 + 1)
                    if c == 0:
                        at_least(act, down_done, n)
                    act.activation(hidden[:, c], bank[:, 7 - c // 2, (c % 2) * S:(c % 2 + 1) * S], ACT.Gelu,
                                   bias=b_1[:, layer(n), c:c + 1]).then_inc(gelu_done, 1)

            act.wait_ge(consts_landed, 16 * CONST_DMAS)

            def slot(s, u):
                for k in range(STEPS):
                    if k < 4 and live(s - 4):
                        exp_bank(s - 4, k + 8)
                    if k >= 4 and live(s - 3):
                        exp_bank(s - 3, k - 4)
                    if k == 0 and live(s):
                        xn1T_out(s)
                    if k == 1 and live(s - 4):
                        context_copy(s - 4, 0)
                    if k == 7 and live(s - 4):
                        context_copy(s - 4, 1)
                    if k == 2 and live(s - 5):
                        xn2T_out(s - 5)
                    if k == 5 and live(s - 5):
                        gelu(s - 5)
                    if k == 10 and live(s - 4):
                        ctxT_out(s - 4)
                    if k in (8, 9, 10) and live(s):
                        parts_out(s, u, k - 8)

            slots(act, slot)

        @block.vector
        def _(dve):
            dve.memset(expo[:], -0.5).then_inc(prefilled, 1)
            dve.wait_ge(squares_landed, 32)
            dve.tensor_copy(keys_b[:], keys_f[:]).then_inc(consts_cast, 1)
            dve.tensor_copy(eyeb[:], eye).then_inc(consts_cast, 1)
            dve.tensor_copy(mask[:], squares[:, 1:2].broadcast_to([128, 4, 128])).then_inc(consts_cast, 1)
            dve.tensor_copy(maskT[:], squares[:, 2:3].broadcast_to([128, 4, 128])).then_inc(consts_cast, 1)
            dve.wait_ge(x_landed, 16 * X_DMAS)
            with dve.Fori(0, B // PER) as c:
                for i in range(PER * T):
                    last = dve.bn_stats(stats0[:, i], h_all[:, c * PER + i // T, i % T])
                last.then_inc(stats0_done, 1)
                wait_alone(dve, stats0_done, c + 1, apart_dve)
                for i in range(PER * T):
                    last = dve.bn_aggr(mv0[:, i], stats0[:, i])
                last.then_inc(mv0_ready, 1)
                dve.wait_ge(rstd0_ready, c + 1)
                for i in range(PER * T):
                    tile = h_all[:, c * PER + i // T, i % T]
                    last = dve.tensor_scalar(tile, tile, mv0[:, i, 0:1], rstd0[:, i:i + 1], ALU.subtract, ALU.mult)
                last.then_inc(ln0_done, 1)
            dve.wait_ge(ln0_done, B // PER)

            def norm_stats(stats, mv, stats_sem, mv_sem, n):
                b = mod(n, B)
                for t in range(T):
                    last = dve.bn_stats(stats[:, t], h_all[:, b, t])
                last.then_inc(stats_sem, 1)
                wait_alone(dve, stats_sem, n + 1, apart_dve)
                for t in range(T):
                    last = dve.bn_aggr(mv[:, t], stats[:, t])
                last.then_inc(mv_sem, 1)

            def norm_apply(xn, mv, rstd, rstd_sem, used_sem, xn_sem, n):
                b = mod(n, B)
                dve.wait_ge(rstd_sem, n + 1)
                at_least(dve, used_sem, n)
                for t in range(T):
                    dve.tensor_scalar(xn[:, t], h_all[:, b, t], mv[:, t, 0:1], rstd[:, t:t + 1],
                                      ALU.subtract, ALU.mult).then_inc(xn_sem, 1)

            def stats_1(n):
                norm_stats(stats1, mv1, stats1_done, mv1_ready, n)

            def apply_1(n):
                norm_apply(xn1, mv1, rstd1, rstd1_ready, xn1_turned, xn1_ready, n)

            def stats_2(n):
                wait_alone(dve, h1_ready, n + 1, apart_dve)
                norm_stats(stats2, mv2, stats2_done, mv2_ready, n)

            def apply_2(n):
                norm_apply(xn2, mv2, rstd2, rstd2_ready, xn2_turned, xn2_ready, n)

            def qkv_out(n, u, t):
                dve.wait_ge(qkv_done, 2 * n + t + 1)
                at_least(dve, rot_ready, n)
                dve.tensor_tensor(feats[:, t, 0:2].rearrange("p s c -> p (s c)"), bank[:, 5 + t, 0:2 * D],
                                  b_qkv[:, layer(n), 0:2 * D], ALU.add).then_inc(qk_ready, 1)
                at_least(dve, vpad_ready, n - 3)
                dve.tensor_tensor(v_tok[:, u % RING, t], bank[:, 5 + t, 2 * D:3 * D],
                                  b_qkv[:, layer(n), 2 * D:3 * D], ALU.add).then_inc(v_ready, 1)

            def split(n, lo, hi, split_sem):
                x, r = feats[:, :, lo:hi], rest[:, :, lo:hi]
                p = [parts[:, :, j, lo:hi] for j in range(3)]
                if lo == 0:
                    dve.wait_ge(qk_ready, 2 * (n + 1))
                    at_least(dve, parts_turned, 3 * n)
                dve.tensor_copy(p[0], x).then_inc(split_sem, 1)
                dve.wait_ge(split_sem, 4 * n + 1)
                dve.tensor_tensor(r, x, p[0], ALU.subtract).then_inc(split_sem, 1)
                dve.wait_ge(split_sem, 4 * n + 2)
                dve.tensor_copy(p[1], r).then_inc(split_sem, 1)
                dve.wait_ge(split_sem, 4 * n + 3)
                dve.tensor_tensor(p[2], r, p[1], ALU.subtract).then_inc(split_sem, 1)

            def max_bank(n, u, k):
                dve.wait_ge(scores_done, STEPS * n + k + 1)
                p = u % 2
                if k < 4:
                    o, i = negmax[:, p, 0, 4 * k:4 * k + 4], bank[:, k % 2, :].rearrange("p (h c) -> p h c", h=4)
                else:
                    j = 2 * (k - 4)
                    o, i = negmax[:, p, 1, j:j + 2], bank[:, k % 2, :].rearrange("p (h c) -> p h c", h=2)
                dve.tensor_reduce(o, i, AX_X, ALU.max, negate=True).then_inc(max_done, 1)

            def neg_parts(n, u):
                dve.wait_ge(max_done, STEPS * (n + 1))
                at_least(dve, neg_turned, n)
                m = negmax[:, u % 2]
                dve.tensor_copy(negparts[:, :, 0], m).then_inc(neg_split, 1)
                dve.wait_ge(neg_split, 2 * n + 1)
                dve.tensor_tensor(negparts[:, :, 1], m, negparts[:, :, 0], ALU.subtract).then_inc(neg_split, 1)

            def negrows_out(n):
                dve.wait_ge(neg_turned, n + 1)
                at_least(dve, negrows_landed, 32 * n)
                dve.tensor_copy(negrows[:], bank16(6)[0:2 * H, 0:S]).then_inc(negrows_ready, 1)

            def divide(n, t):
                dve.wait_ge(context_turned, 2 * n + t + 1)
                v = bank[:, 7, :].rearrange("p (h w) -> p h w", w=32)
                dve.reciprocal(rsum[:, t], v[:, :, HD]).then_inc(rsum_ready, 1)
                dve.wait_ge(rsum_ready, 2 * n + t + 1)
                at_least(dve, ctx_turned, n)
                dve.tensor_tensor(ctx_tok[:, t].rearrange("p (h w) -> p h w", w=HD), v[:, :, 0:HD],
                                  rsum[:, t].unsqueeze(2).broadcast_to([128, H, HD]), ALU.mult
                                  ).then_inc(ctx_ready, 1)

            def resid_1(n):
                b = mod(n, B)
                dve.wait_ge(proj_done, n + 1)
                dve.wait_ge(bo_added, n + 1)
                h = h_all[:, b].rearrange("p t c -> p (t c)")
                dve.tensor_tensor(h, bank[:, 7, 0:S], h, ALU.add).then_inc(h1_ready, 1)

            def resid_2(n):
                b = mod(n, B)
                dve.wait_ge(down_done, n + 1)
                dve.wait_ge(b2_added, n + 1)
                h = h_all[:, b].rearrange("p t c -> p (t c)")
                dve.tensor_tensor(h, bank[:, 7, 0:S], h, ALU.add).then_inc(h2_ready, 1)

            dve.wait_ge(consts_landed, 16 * CONST_DMAS)

            def slot(s, u):
                if live(s - 3):
                    neg_parts(s - 3, u - 3)
                for k in range(STEPS):
                    if live(s - 2):
                        max_bank(s - 2, u - 2, k)
                    if k == 1 and live(s - 5):
                        apply_2(s - 5)
                    if k == 1 and live(s - 3):
                        negrows_out(s - 3)
                    if k in (2, 3) and live(s):
                        qkv_out(s, u, k - 2)
                    if k == 4 and live(s):
                        split(s, 0, 2, qk_split)
                    if k == 5 and live(s + 1):
                        stats_1(s + 1)
                    if k == 7 and live(s):
                        dve.wait_ge(rot_ready, s + 1)
                        split(s, 2, 3, rot_split)
                    if k == 7 and live(s - 5):
                        resid_2(s - 5)
                    if k in (8, 9) and live(s - 4):
                        divide(s - 4, k - 8)
                    if k == 10 and live(s + 1):
                        apply_1(s + 1)
                    if k == 11 and live(s - 4):
                        resid_1(s - 4)
                        stats_2(s - 4)

            slots(dve, slot)

        @block.gpsimd
        def _(pool):
            pool.memset(v_pad[:], 0.0).then_inc(zeros_filled, 1)
            pool.wait_ge(zeros_filled, 1)
            pool.memset(v_pad[:, :, :, :, HD:HD + 1], 1.0).then_inc(prefilled, 1)
            pool.wait_ge(prefilled, 2)
            with pool.Fori(0, B // PER) as c:
                wait_alone(pool, mv0_ready, c + 1, apart_pool)
                pool.tensor_scalar(ve0[:], mv0[:, :, 1], 1e-5, None, ALU.add).then_inc(ve0_ready, 1)
                pool.wait_ge(ve0_ready, c + 1)
                pool.tensor_tensor(rstd0[:], ve0[:], expo[:, 0:PER * T], ALU.pow).then_inc(rstd0_ready, 1)
            pool.wait_ge(consts_landed, 16 * CONST_DMAS)

            def power(ve, mv, rstd, mv_sem, ve_sem, rstd_sem, n):
                wait_alone(pool, mv_sem, n + 1, apart_pool)
                pool.tensor_scalar(ve[:], mv[:, :, 1], 1e-6, None, ALU.add).then_inc(ve_sem, 1)
                pool.wait_ge(ve_sem, n + 1)
                pool.tensor_tensor(rstd[:], ve[:], expo[:, 0:T], ALU.pow).then_inc(rstd_sem, 1)

            def turned(n):
                pool.wait_ge(qk_ready, 2 * (n + 1))
                pool.tensor_tensor(qu[:], feats[:, :, 0], b_u[:, layer(n)].unsqueeze(1).broadcast_to([128, T, D]),
                                   ALU.add).then_inc(qu_ready, 1)
                pool.wait_ge(qu_ready, n + 1)
                hf = D // 2
                pool.tensor_tensor(turn_s[:], qu[:], turn[:, 0], ALU.mult)
                pool.tensor_tensor(turn_c[:, :, 0:hf], qu[:, :, hf:D], turn[:, 1, :, 0:hf], ALU.mult)
                pool.tensor_tensor(turn_c[:, :, hf:D], qu[:, :, 0:hf], turn[:, 1, :, hf:D], ALU.mult
                                   ).then_inc(turn_steps, 1)
                pool.wait_ge(turn_steps, n + 1)
                at_least(pool, rot_split, 4 * n)
                pool.tensor_tensor(feats[:, :, 2], turn_s[:], turn_c[:], ALU.add).then_inc(rot_ready, 1)

            def v_padded(n, u):
                pool.wait_ge(v_ready, 2 * (n + 1))
                wait_alone(pool, context_done, 4 * (n - 1), apart_pool)
                pool.tensor_copy(v_pad[:, u % 2, :, :, 0:HD],
                                 v_tok[:, u % RING].rearrange("p t (h w) -> p t h w", w=HD)
                                 ).then_inc(vpad_ready, 1)

            def add_row(n, rows, read_sem, value, added_sem):
                pool.wait_ge(read_sem, value)
                h = h_all[:, mod(n, B)]
                pool.tensor_tensor(h, h, rows[:, layer(n)].unsqueeze(1).broadcast_to([128, T, D]), ALU.add
                                   ).then_inc(added_sem, 1)

            def slot(s, u):
                for k in range(STEPS):
                    if k == 0 and live(s - 5):
                        power(ve2, mv2, rstd2, mv2_ready, ve2_ready, rstd2_ready, s - 5)
                    if k == 2 and live(s - 5):
                        add_row(s - 5, b_2, xn2_ready, 2 * (s - 4), b2_added)
                    if k == 3 and live(s):
                        turned(s)
                    if k == 6 and live(s + 1):
                        power(ve1, mv1, rstd1, mv1_ready, ve1_ready, rstd1_ready, s + 1)
                    if k == 8 and live(s - 2):
                        v_padded(s - 2, u - 2)
                    if k == 9 and live(s - 4):
                        add_row(s - 4, b_o, xn1_ready, 2 * (s - 3), bo_added)

            slots(pool, slot)


def experts_program(nc, a, h_all, out):
    with ExitStack() as ctx:
        def sb(name, shape, dt=F32):
            return ctx.enter_context(nc.sbuf_tensor(name, shape, dt))

        def sem(name):
            return ctx.enter_context(nc.semaphore(name))

        bank = ctx.enter_context(nc.psum_tensor("ebank", [128, 8, 512], F32))

        GT = 4
        NG = NT // GT
        w_in = sb("w_in", [128, 2 * GU])
        w_down = sb("w_down", [128, GU // 128, D])
        w_router = sb("w_router", [128, E])
        bias_rows = sb("bias_rows", [128, E])
        eye = sb("eeye", [128, 128])
        expo = sb("eexpo", [128, GT])
        xin = sb("xin", [128, 2, GT, D])
        stats = sb("estats", [128, GT, 6])
        mv = sb("emv", [128, GT, 2])
        ve = sb("eve", [128, GT])
        rstd = sb("erstd", [128, GT])
        xn = sb("exn", [128, GT, D])
        xT = sb("exT", [128, 2, GT, 128])
        score = sb("score", [128, GT, E])
        biased = sb("biased", [128, GT, E])
        larger = sb("larger", [128, GT * G, 2])
        smaller = sb("smaller", [128, GT * G, 2])
        tops = sb("tops", [128, 3, GT * G])
        gs = sb("gs", [128, GT, 14])
        gtop = sb("gtop", [128, GT, 8])
        grep = sb("grep", [128, GT, 8])
        gout = sb("gout", [128, GT, 10])
        kept = sb("kept", [128, GT, G])
        pen = sb("pen", [128, GT, G])
        cand = sb("cand", [128, GT, E + 4])
        ctop = sb("ctop", [128, GT, 8])
        crep = sb("crep", [128, GT, 8])
        cout = sb("cout", [128, GT, E + 4])
        chosen = sb("chosen", [128, GT, E])
        wsel = sb("wsel", [128, GT, E])
        wsum = sb("wsum", [128, GT])
        wsum1 = sb("wsum1", [128, GT])
        winv = sb("winv", [128, GT])
        combine = sb("combine", [128, 2, GT, E])
        gate_sig = sb("gate_sig", [128, 2, GU])
        gated = sb("gated", [128, GU])
        act_all = sb("act_all", [128, 2, GU])
        hw = sb("hw", [128, 2, E * EH])
        hT = sb("hT", [128, GU // 128, 128])
        ot = sb("ot", [128, 2, GT, D])

        weights_landed = sem("weights_landed")
        apart_dve, apart_pool, apart_sp = (sem(f"eapart_{e}") for e in ("dve", "pool", "sp"))
        xin_landed = [sem(f"xin_landed{i}") for i in range(2)]
        filled = sem("filled")
        x1_ready = sem("x1_ready")
        stats_done = sem("estats_done")
        mv_ready = sem("emv_ready")
        ve_ready = sem("eve_ready")
        rstd_ready = sem("erstd_ready")
        xn_ready = sem("exn_ready")
        xn_turned = sem("exn_turned")
        xT_ready = sem("exT_ready")
        logits_done = sem("logits_done")
        score_ready = sem("score_ready")
        route = sem("route")
        route_end = sem("route_end")
        combine_ready = sem("combine_ready")
        in_done = sem("in_done")
        sig_ready = sem("sig_ready")
        gated_ready = sem("gated_ready")
        act_ready = sem("act_ready")
        hw_ready = sem("hw_ready")
        h_turned = sem("h_turned")
        hT_ready = sem("hT_ready")
        down_done = sem("edown_done")
        out_ready = sem("out_ready")
        out_landed = [sem(f"out_landed{i}") for i in range(2)]

        h_groups = h_all[:].rearrange("p b t d -> p (b t) d").rearrange("p (q t) d -> p q t d", t=GT)
        h_tiles = h_all[:].rearrange("p b t d -> p (b t) d")
        x_groups = a["x"].rearrange("b (t p) d -> (b t) p d", p=128).rearrange("(q t) p d -> q p t d", t=GT)
        out_groups = out.rearrange("b (t p) d -> (b t) p d", p=128).rearrange("(q t) p d -> q p t d", t=GT)
        WEIGHT_DMAS = 5
        ROUTE = 17
        FIRST, LAST = 2, 6

        def live(n):
            return not isinstance(n, int) or 0 <= n < NG

        def live_tile(n):
            return not isinstance(n, int) or 0 <= n < NT

        def slots(eng, slot):
            for q in range(-2, 2 * FIRST):
                slot(q, q % 2)
            with eng.Fori(FIRST, LAST) as g:
                for v in range(2):
                    slot(2 * g + v, v)
            for q in range(2 * LAST, NG + 1):
                slot(q, q % 2)

        block = ctx.enter_context(nc.Block())

        @block.sync
        def _(sp):
            sp.dma_start(eye[:], a["c_squares"][:, 0:128]).then_inc(weights_landed, 16)

            def load(q, v):
                if live(q):
                    wait_alone(sp, x1_ready, q - 1, apart_sp)
                    sp.dma_start(xin[:, v % 2], x_groups[q]).then_inc(xin_landed[v % 2], 16)

            load(0, 0)
            load(1, 1)
            sp.dma_start(w_router[:], a["router"]).then_inc(weights_landed, 16)
            sp.dma_start(bias_rows[:], a["correction"].rearrange("(o e) -> o e", o=1).broadcast_to([128, E])
                         ).then_inc(weights_landed, 16)
            sp.dma_start(w_in[:], a["w_in"]).then_inc(weights_landed, 16)
            sp.dma_start(w_down[:], a["w_down"].rearrange("(c p) n -> p c n", p=128)).then_inc(weights_landed, 16)

            def slot(q, v):
                if not (isinstance(q, int) and q < -1):
                    load(q + 3, v + 3)
                if live(q - 1):
                    wait_alone(sp, out_ready, GT * q, apart_sp)
                    sp.dma_start(out_groups[q - 1], ot[:, (v - 1) % 2]).then_inc(out_landed[(v - 1) % 2], 16)

            slots(sp, slot)
            for r in range(2):
                sp.wait_ge(out_landed[r], 16 * (NG // 2))

        @block.tensor
        def _(pe):
            pe.wait_ge(weights_landed, 16 * WEIGHT_DMAS)

            def x_turn(q):
                pe.wait_ge(xn_ready, q + 1)
                at_least(pe, score_ready, q)
                for t in range(GT):
                    last = pe.transpose(bank[:, 6, t * 128:(t + 1) * 128], xn[:, t], eye[:])
                last.then_inc(xn_turned, 1)

            def router(q, v):
                pe.wait_ge(xT_ready, q + 1)
                for t in range(GT):
                    last = pe.matmul(bank[:, 6, t * E:(t + 1) * E], xT[:, v % 2, t], w_router[:],
                                     start=True, stop=True)
                last.then_inc(logits_done, 1)

            def product(n, v, u, i):
                if i == 0:
                    at_least(pe, act_ready, n - 1)
                last = pe.matmul(bank[:, 3 * (u % 2) + i, :], xT[:, v % 2, u], w_in[:, i * 512:(i + 1) * 512],
                                 start=True, stop=True)
                if i == 2:
                    last.then_inc(in_done, 1)

            def h_turn(n, u, half):
                if half == 0:
                    pe.wait_ge(hw_ready, n + 1)
                    at_least(pe, out_ready, n)
                else:
                    pe.wait_ge(hT_ready, 2 * n + 1)
                for i in range(3):
                    c = 3 * half + i
                    src = hw[:, u % 2, c * 128:(c + 1) * 128] if c < E * EH // 128 else \
                        act_all[:, u % 2, c * 128:(c + 1) * 128]
                    last = pe.transpose(bank[:, 7, i * 128:(i + 1) * 128], src, eye[:])
                last.then_inc(h_turned, 1)

            def down(n):
                pe.wait_ge(hT_ready, 2 * (n + 1))
                for c in range(GU // 128):
                    last = pe.matmul(bank[:, 7, 0:D], hT[:, c], w_down[:, c], start=(c == 0),
                                     stop=(c == GU // 128 - 1))
                last.then_inc(down_done, 1)

            def slot(q, v):
                for u in range(GT):
                    n = GT * q + u
                    if live(q):
                        product(n, v, u, 0)
                    if u == 0 and live(q + 1):
                        x_turn(q + 1)
                    if u == 1 and live(q + 1):
                        router(q + 1, v + 1)
                    if live_tile(n - 2):
                        h_turn(n - 2, u, 0)
                    if live(q):
                        product(n, v, u, 1)
                    if live_tile(n - 2):
                        h_turn(n - 2, u, 1)
                    if live(q):
                        product(n, v, u, 2)
                    if live_tile(n - 2):
                        down(n - 2)

            slots(pe, slot)

        @block.scalar
        def _(act):
            def half_out(n, half):
                act.wait_ge(h_turned, 2 * n + half + 1)
                if half == 0:
                    at_least(act, down_done, n)
                act.copy(hT[:, 3 * half:3 * half + 3].rearrange("p c n -> p (c n)"), bank[:, 7, 0:384]
                         ).then_inc(hT_ready, 1)

            def slot(q, v):
                for u in range(GT):
                    n = GT * q + u
                    if live_tile(n - 1):
                        act.wait_ge(in_done, n)
                        at_least(act, gated_ready, n - 2)
                        b = 3 * ((u - 1) % 2)
                        act.activation(gate_sig[:, (u - 1) % 2],
                                       bank[:, b:b + 3].rearrange("p b c -> p (b c)")[:, 0:GU], ACT.Sigmoid
                                       ).then_inc(sig_ready, 1)
                    if u == 0 and live(q + 1):
                        act.wait_ge(xn_turned, q + 2)
                        at_least(act, in_done, GT * q)
                        act.copy(xT[:, (v + 1) % 2].rearrange("p t c -> p (t c)"), bank[:, 6, :]
                                 ).then_inc(xT_ready, 1)
                    if live_tile(n - 2):
                        half_out(n - 2, 0)
                    if u == 1 and live(q + 1):
                        act.wait_ge(logits_done, q + 2)
                        at_least(act, combine_ready, q + 1)
                        act.activation(score[:].rearrange("p t e -> p (t e)"), bank[:, 6, 0:GT * E], ACT.Sigmoid
                                       ).then_inc(score_ready, 1)
                    if live_tile(n - 2):
                        half_out(n - 2, 1)

            slots(act, slot)

        @block.vector
        def _(dve):
            dve.memset(expo[:], -0.5)
            dve.memset(gs[:, :, 0:6], HIGH)
            dve.memset(gs[:, :, 10:14], LOW)
            dve.memset(grep[:], HIGH)
            dve.memset(cand[:, :, E:E + 4], HIGH)
            dve.memset(crep[:], HIGH).then_inc(filled, 1)
            dve.wait_ge(filled, 1)
            dve.wait_ge(weights_landed, 16 * WEIGHT_DMAS)

            def residual(q, v):
                dve.wait_ge(xin_landed[v % 2], 16 * (q // 2 + 1))
                h = h_groups[:, q]
                dve.tensor_tensor(h, xin[:, v % 2], h, ALU.add).then_inc(x1_ready, 1)
                wait_alone(dve, x1_ready, q + 1, apart_dve)
                for t in range(GT):
                    last = dve.bn_stats(stats[:, t], h_groups[:, q, t])
                last.then_inc(stats_done, 1)
                wait_alone(dve, stats_done, q + 1, apart_dve)
                for t in range(GT):
                    last = dve.bn_aggr(mv[:, t], stats[:, t])
                last.then_inc(mv_ready, 1)

            def norm(q):
                dve.wait_ge(rstd_ready, q + 1)
                at_least(dve, xn_turned, q)
                for t in range(GT):
                    last = dve.tensor_scalar(xn[:, t], h_groups[:, q, t], mv[:, t, 0:1], rstd[:, t:t + 1],
                                             ALU.subtract, ALU.mult)
                last.then_inc(xn_ready, 1)

            step = [0]

            def link(q, ins):
                step[0] += 1
                ins.then_inc(route, 1)
                wait_alone(dve, route, ROUTE * q + step[0], apart_dve)

            def routing_groups(q):
                step[0] = 0
                dve.wait_ge(score_ready, q + 1)
                link(q, dve.tensor_tensor(biased[:], score[:], bias_rows[:].unsqueeze(1).broadcast_to([128, GT, E]),
                                          ALU.add))
                v = biased[:].rearrange("p t (g a b) -> p (t g) a b", g=G, a=2)
                dve.tensor_tensor(larger[:], v[:, :, 0], v[:, :, 1], ALU.max)
                link(q, dve.tensor_tensor(smaller[:], v[:, :, 0], v[:, :, 1], ALU.min))
                dve.tensor_tensor(tops[:, 0], larger[:, :, 0], larger[:, :, 1], ALU.max)
                dve.tensor_tensor(tops[:, 1], larger[:, :, 0], larger[:, :, 1], ALU.min)
                link(q, dve.tensor_tensor(tops[:, 2], smaller[:, :, 0], smaller[:, :, 1], ALU.max))
                link(q, dve.tensor_tensor(tops[:, 1], tops[:, 1], tops[:, 2], ALU.max))
                link(q, dve.tensor_tensor(gs[:, :, 6:10], tops[:, 0].rearrange("p (t g) -> p t g", g=G),
                                          tops[:, 1].rearrange("p (t g) -> p t g", g=G), ALU.add))
                for t in range(GT):
                    last = dve.max(gtop[:, t], gs[:, t, 6:14])
                link(q, last)
                link(q, dve.tensor_copy(grep[:, :, 0:2], gtop[:, :, 0:2]))
                for t in range(GT):
                    last = dve.match_replace(gout[:, t], grep[:, t], gs[:, t, 0:10], LOW)
                link(q, last)
                link(q, dve.tensor_tensor(kept[:], gout[:, :, 6:10], gs[:, :, 6:10], ALU.is_equal))
                link(q, dve.tensor_scalar(pen[:], kept[:], LOW, None, ALU.mult))

            def routing_experts(q, v):
                link(q, dve.tensor_tensor(cand[:, :, 0:E].rearrange("p t (g k) -> p t g k", g=G),
                                          biased[:].rearrange("p t (g k) -> p t g k", g=G),
                                          pen[:].unsqueeze(3).broadcast_to([128, GT, G, E // G]), ALU.add))
                for t in range(GT):
                    last = dve.max(ctop[:, t], cand[:, t, 0:E])
                link(q, last)
                link(q, dve.tensor_copy(crep[:, :, 0:4], ctop[:, :, 0:4]))
                for t in range(GT):
                    last = dve.match_replace(cout[:, t], crep[:, t], cand[:, t], LOW / 2)
                link(q, last)
                link(q, dve.tensor_tensor(chosen[:], cout[:, :, 0:E], cand[:, :, 0:E], ALU.not_equal))
                link(q, dve.tensor_tensor(wsel[:], chosen[:], score[:], ALU.mult))
                link(q, dve.tensor_reduce(wsum[:], wsel[:], AX_X, ALU.add))
                assert step[0] == ROUTE, step[0]
                dve.tensor_scalar(wsum1[:], wsum[:], 1e-20, None, ALU.add).then_inc(route_end, 1)
                dve.wait_ge(route_end, 2 * q + 1)
                dve.reciprocal(winv[:], wsum1[:]).then_inc(route_end, 1)
                dve.wait_ge(route_end, 2 * q + 2)
                at_least(dve, hw_ready, GT * (q - 1))
                dve.tensor_tensor(combine[:, v % 2], wsel[:], winv[:].unsqueeze(2).broadcast_to([128, GT, E]),
                                  ALU.mult).then_inc(combine_ready, 1)

            def gating(n, u):
                g = bank[:, 3 * (u % 2):3 * (u % 2) + 3].rearrange("p b c -> p (b c)")
                dve.wait_ge(sig_ready, n + 1)
                at_least(dve, act_ready, n)
                dve.tensor_tensor(gated[:], g[:, 0:GU], gate_sig[:, u % 2], ALU.mult).then_inc(gated_ready, 1)
                dve.wait_ge(gated_ready, n + 1)
                at_least(dve, h_turned, 2 * (n - 1))
                at_least(dve, hw_ready, n - 1)
                dve.tensor_tensor(act_all[:, u % 2], g[:, GU:2 * GU], gated[:], ALU.mult).then_inc(act_ready, 1)

            def result(n, v, u):
                dve.wait_ge(down_done, n + 1)
                if u == 0 and not (isinstance(n, int) and n < 2 * GT):
                    dve.wait_ge(out_landed[v % 2], 16 * (n // (2 * GT)))
                dve.tensor_tensor(ot[:, v % 2, u], bank[:, 7, 0:D], h_tiles[:, n], ALU.add).then_inc(out_ready, 1)

            def slot(q, v):
                for u in range(GT):
                    n = GT * q + u
                    if live_tile(n - 3):
                        result(n - 3, v if u == 3 else v - 1, (u - 3) % GT)
                    if live_tile(n - 1):
                        gating(n - 1, u - 1)
                    if u == 0 and live(q + 2):
                        residual(q + 2, v + 2)
                    if u == 1 and live(q + 2):
                        norm(q + 2)
                    if u == 2 and live(q + 1):
                        routing_groups(q + 1)
                    if u == 3 and live(q + 1):
                        routing_experts(q + 1, v + 1)

            slots(dve, slot)

        @block.gpsimd
        def _(pool):
            pool.wait_ge(filled, 1)

            def slot(q, v):
                for u in range(GT):
                    n = GT * q + u - 1
                    if u == 1 and live(q + 2):
                        wait_alone(pool, mv_ready, q + 3, apart_pool)
                        pool.tensor_scalar(ve[:], mv[:, :, 1], 1e-5, None, ALU.add).then_inc(ve_ready, 1)
                        pool.wait_ge(ve_ready, q + 3)
                        pool.tensor_tensor(rstd[:], ve[:], expo[:], ALU.pow).then_inc(rstd_ready, 1)
                    if live_tile(n):
                        c = combine[:, (v if u > 0 else v - 1) % 2, (u - 1) % GT]
                        if u == 1:
                            pool.wait_ge(combine_ready, q + 1)
                        pool.wait_ge(act_ready, n + 1)
                        at_least(pool, h_turned, 2 * (n - 1))
                        pool.tensor_tensor(hw[:, (u - 1) % 2].rearrange("p (e h) -> p e h", e=E),
                                           act_all[:, (u - 1) % 2, 0:E * EH].rearrange("p (e h) -> p e h", e=E),
                                           c.unsqueeze(2).broadcast_to([128, E, EH]), ALU.mult).then_inc(hw_ready, 1)

            slots(pool, slot)


def kernel(**inputs):
    import concourse.bacc as bacc
    from concourse.bass_utils import run_bass_kernel_spmd

    def i(name):
        return np.asarray(inputs[name])

    def feature_major(w):
        return w.reshape(LAYERS, H, HD, D).transpose(0, 2, 1, 3).reshape(LAYERS, D, D)

    def feature_major_row(b):
        return b.reshape(LAYERS, H, HD).transpose(0, 2, 1).reshape(LAYERS, D)

    arrays = {
        "x": i("L0_attn_x"),
        "w_qkv": np.concatenate([feature_major(i("L0_attn_Wq")), feature_major(i("L0_attn_Wk")), i("L0_attn_Wv")],
                                axis=1).transpose(0, 2, 1),
        "b_qkv": np.concatenate([feature_major_row(i("L0_attn_bq")), feature_major_row(i("L0_attn_bk")),
                                 i("L0_attn_bv")], axis=1),
        "u": feature_major_row(i("L0_attn_u_bias")),
        "w_o": i("L0_attn_Wo").transpose(0, 2, 1),
        "bo": i("L0_attn_bo"),
        "w_1": i("L0_attn_W1").transpose(0, 2, 1),
        "b_1": i("L0_attn_b1").reshape(LAYERS * FC, 128).T,
        "w_2": i("L0_attn_W2").transpose(0, 2, 1),
        "b2": i("L0_attn_b2"),
        "ln_cols": np.stack([i("L0_attn_ln1_w"), i("L0_attn_ln1_b"), i("L0_attn_ln2_w"), i("L0_attn_ln2_b")],
                            axis=1).reshape(LAYERS * 4, D).T,
        "router": i("L0_ffn_router_w").T,
        "correction": i("L0_ffn_correction_bias"),
        "w_in": np.concatenate([i("L0_ffn_gate_w").transpose(1, 0, 2).reshape(D, E * EH),
                                i("L0_ffn_shared_gate_w").T,
                                i("L0_ffn_up_w").transpose(1, 0, 2).reshape(D, E * EH),
                                i("L0_ffn_shared_up_w").T], axis=1),
        "w_down": np.concatenate([i("L0_ffn_down_w").reshape(E * EH, D), i("L0_ffn_shared_down_w").T], axis=0),
    }
    arrays.update(position_tables())
    arrays = {f"in_{name}": np.ascontiguousarray(x) for name, x in arrays.items()}
    nc = bacc.Bacc("TRN2", target_bir_lowering=False, num_devices=1)
    a = {name[3:]: nc.dram_tensor(name, x.shape, mybir.dt.from_np(x.dtype), kind="ExternalInput").ap()
         for name, x in arrays.items()}
    out = nc.dram_tensor("out", (B, S, D), F32, kind="ExternalOutput").ap()
    with nc.sbuf_tensor("h_all", [128, B, T, D], F32) as h_all:
        layers_program(nc, a, h_all)
        experts_program(nc, a, h_all, out)
    r = run_bass_kernel_spmd(nc, [arrays], core_ids=[0])
    return r.results[0]["out"]
```

```python
from contextlib import ExitStack

import numpy as np

import concourse.bass as bass
from concourse import mybir

F32 = mybir.dt.float32
F32R = mybir.dt.float32r
BF16 = mybir.dt.bfloat16
ALU = mybir.AluOpType
ACT = mybir.ActivationFunctionType
AX_X = mybir.AxisListType.X

B, S, D = 32, 256, 128
H, HD = 16, 8
LAYERS, DI = 4, 512
T = S // 128
N = LAYERS * B
FC = DI // 128
SCALE = HD ** -0.5
PARTS_Q = (0, 0, 0, 1, 1, 2)
PARTS_K = (0, 1, 2, 0, 1, 0)
NB = len(PARTS_Q)
ROT0 = NB * HD
MROW = 2 * NB * HD
STACK = MROW + 2
RING = 4
STEPS = 12
PR = 6
HW = 16
VW = 3 * HW
MASK = -1.0e30
STACK_DMAS = 3 * NB
PER = 4
X_PARTS = 4
E, G, EH = 16, 4, 32
HS = 256
NT = B * T
GU = E * EH + HS
HIGH, LOW = 3.0e38, -3.0e38


def wait_alone(eng, sem, value, apart):
    if not isinstance(value, int):
        eng.wait_ge(sem, value)
        eng.sem_inc(apart, 1)
    elif value > 0:
        eng.wait_ge(sem, value)


def at_least(eng, sem, value):
    if not isinstance(value, int) or value > 0:
        eng.wait_ge(sem, value)


def capped(value, most):
    return min(value, most) if isinstance(value, int) else value


def bf16_parts(x):
    parts = []
    for _ in range(3):
        bits = x.astype(np.float32).view(np.uint32).astype(np.uint64)
        bits = (bits + 0x7FFF + ((bits >> 16) & 1)) & 0xFFFF0000
        p = bits.astype(np.uint32).view(np.float32)
        parts.append(p)
        x = x - p.astype(np.float64)
    return parts


def product_of_parts(pe, out, w, x):
    pe.matmul(out, w[0], x[0], start=True, stop=False)
    pe.matmul(out, w[1], x[0], start=False, stop=False)
    return pe.matmul(out, w[0], x[1], start=False, stop=True)


def position_tables():
    inv = (1.0 / np.float32(10000.0) ** (np.arange(0, HD, 2, dtype=np.float32) / np.float32(HD))).astype(np.float64)
    angle = np.arange(S, dtype=np.float64)[:, None] * inv[None, :]
    sin, cos = np.sin(angle), np.cos(angle)
    s64, c64 = np.repeat(sin.T, H, axis=0), np.repeat(cos.T, H, axis=0)
    turn = np.stack([np.concatenate([s64, s64], axis=0), np.concatenate([c64, -c64], axis=0)],
                    axis=1).astype(np.float32)
    parts = bf16_parts(np.ascontiguousarray(np.concatenate([cos, sin], axis=1).T))
    keys = np.concatenate([parts[p] for p in PARTS_K] + [np.full((2, S), -1, np.float32)], axis=0)
    q, k = np.arange(128)[:, None], np.arange(128)[None, :]
    mask = np.where(k > q, np.float32(MASK), np.float32(0))
    squares = np.concatenate([np.eye(128, dtype=np.float32), mask, mask.T], axis=1)
    return {"c_turn": turn.reshape(128, -1), "c_keys": keys, "c_squares": squares}


def layers_program(nc, a, h_all):
    with ExitStack() as ctx:
        def sb(name, shape, dt=F32):
            return ctx.enter_context(nc.sbuf_tensor(name, shape, dt))

        def sem(name):
            return ctx.enter_context(nc.semaphore(name))

        bank = ctx.enter_context(nc.psum_tensor("bank", [128, 8, 512], F32))

        def bank16(i):
            return bank[:, i, :].bitcast(BF16)

        w_qkv = sb("w_qkv", [128, LAYERS, 4 * D])
        w_now = sb("w_now", [128, 2, 2, 3 * D], F32R)
        w_o = sb("w_o", [128, LAYERS, D])
        w_1 = sb("w_1", [128, DI])
        w_1_parts = sb("w_1_parts", [128, 2, DI], F32R)
        w_2 = sb("w_2", [128, LAYERS, FC, D])
        b_v = sb("b_v", [128, LAYERS, D])
        b_o = sb("b_o", [128, LAYERS, D])
        b_2 = sb("b_2", [128, LAYERS, D])
        ln_cols = sb("ln_cols", [128, LAYERS, 4])
        b_cols = sb("b_cols", [128, LAYERS, 4])
        u_cols = sb("u_cols", [128, LAYERS, 2])
        cols_now = sb("cols_now", [128, 2, 4])
        b_1 = sb("b_1", [128, LAYERS, FC])
        turn = sb("turn", [128, 2, S])
        mask = sb("mask", [128, 2, 128], BF16)
        maskT = sb("maskT", [128, 4, 128], BF16)
        squares = sb("squares", [128, 3, 128])
        eye = squares[:, 0]
        eyeb = sb("eyeb", [128, 128], BF16)
        keys_f = sb("keys_f", [STACK - ROT0, S])
        keys_b = sb("keys_b", [STACK - ROT0, S], BF16)
        expo = sb("expo", [128, 16])

        stats0 = sb("stats0", [128, PER * T, 6])
        mv0 = sb("mv0", [128, PER * T, 2])
        ve0 = sb("ve0", [128, PER * T])
        rstd0 = sb("rstd0", [128, PER * T])

        stats1 = sb("stats1", [128, T, 6])
        mv1 = sb("mv1", [128, T, 2])
        ve1 = sb("ve1", [128, T])
        rstd1 = sb("rstd1", [128, T])
        xn1 = sb("xn1", [128, T, D])
        xn1T = sb("xn1T", [128, S])
        xn1T_parts = sb("xn1T_parts", [128, 2, S], F32R)
        turn_s = sb("turn_s", [128, S])
        turn_c = sb("turn_c", [128, S])
        rotated = sb("rotated", [128, S])
        rest = sb("rest", [128, 3, S])
        base = sb("base", [128, 2, 3, 3, S], BF16)
        v_tok = sb("v_tok", [128, RING, T, D])
        v_pad = sb("v_pad", [128, 2, T, H, VW])
        qstack = sb("qstack", [STACK, RING, H, S], BF16)
        kstack = sb("kstack", [STACK, RING, H, S], BF16)
        rowmax = sb("rowmax", [128, 2, T, H])
        maxparts = sb("maxparts", [128, T, 2, H], BF16)
        maxrows = sb("maxrows", [2 * H, S], BF16)
        probs = sb("probs", [128, PR, 512])
        ctxT_raw = sb("ctxT_raw", [128, 2, S])
        rsum = sb("rsum", [128, T * H])
        ctx_tok = sb("ctx_tok", [128, T * D])
        ctxT = sb("ctxT", [128, S])
        stats2 = sb("stats2", [128, T, 6])
        mv2 = sb("mv2", [128, T, 2])
        ve2 = sb("ve2", [128, T])
        rstd2 = sb("rstd2", [128, T])
        xn2 = sb("xn2", [128, T, D])
        xn2T = sb("xn2T", [128, S])
        xn2T_parts = sb("xn2T_parts", [128, 2, S], F32R)
        hidden = sb("hidden", [128, FC, S])
        table_probe = sb("table_probe", [128, 1])

        x_landed = [sem(f"x_landed{i}") for i in range(X_PARTS)]
        consts_landed = sem("consts_landed")
        keys_landed = sem("keys_landed")
        squares_landed = sem("squares_landed")
        consts_cast = sem("consts_cast")
        prefilled = sem("prefilled")
        zeros_filled = sem("zeros_filled")
        apart_dve, apart_pool, apart_sp = (sem(f"apart_{e}") for e in ("dve", "pool", "sp"))
        stats0_done = sem("stats0_done")
        mv0_ready = sem("mv0_ready")
        ve0_ready = sem("ve0_ready")
        rstd0_ready = sem("rstd0_ready")
        ln0_done = sem("ln0_done")
        w1_landed = sem("w1_landed")
        w1_split = sem("w1_split")
        stats1_done = sem("stats1_done")
        mv1_ready = sem("mv1_ready")
        ve1_ready = sem("ve1_ready")
        rstd1_ready = sem("rstd1_ready")
        xn1_ready = sem("xn1_ready")
        xn1_turned = sem("xn1_turned")
        xn1T_ready = sem("xn1T_ready")
        qkv_done = sem("qkv_done")
        weights_high = sem("weights_high")
        weights_now = sem("weights_now")
        xn1_high = sem("xn1_high")
        xn1_low = sem("xn1_low")
        v_ready = sem("v_ready")
        turn_steps = sem("turn_steps")
        rot_ready = sem("rot_ready")
        qk_first = sem("qk_first")
        qk_rest = sem("qk_rest")
        qk_second = sem("qk_second")
        qk_third = sem("qk_third")
        rot_first = sem("rot_first")
        rot_rest = sem("rot_rest")
        rot_second = sem("rot_second")
        rot_third = sem("rot_third")
        stack_landed = [sem(f"stack_landed{i}") for i in range(RING)]
        vpad_ready = sem("vpad_ready")
        scores_done = sem("scores_done")
        max_done = sem("max_done")
        max_split = sem("max_split")
        max_turned = sem("max_turned")
        maxrows_ready = sem("maxrows_ready")
        maxrows_landed = sem("maxrows_landed")
        scoresT_done = sem("scoresT_done")
        exp_done = sem("exp_done")
        context_done = sem("context_done")
        context_out = sem("context_out")
        context_turned = sem("context_turned")
        rsum_ready = sem("rsum_ready")
        ctx_ready = sem("ctx_ready")
        ctx_turned = sem("ctx_turned")
        ctxT_ready = sem("ctxT_ready")
        proj_done = sem("proj_done")
        bo_added = sem("bo_added")
        h1_ready = sem("h1_ready")
        stats2_done = sem("stats2_done")
        mv2_ready = sem("mv2_ready")
        ve2_ready = sem("ve2_ready")
        rstd2_ready = sem("rstd2_ready")
        xn2_ready = sem("xn2_ready")
        xn2_turned = sem("xn2_turned")
        xn2T_ready = sem("xn2T_ready")
        xn2_high = sem("xn2_high")
        xn2_low = sem("xn2_low")
        up_done = sem("up_done")
        tables_loaded = sem("tables_loaded")
        gelu_done = sem("gelu_done")
        down_done = sem("down_done")
        b2_added = sem("b2_added")
        h2_ready = sem("h2_ready")

        x_tiles = a["x"].rearrange("b (t p) d -> p b t d", p=128)

        def mod(n, m):
            return n % m

        def layer(n):
            return n // B

        CONST_DMAS = 11

        FIRST_LOOP, LAST_LOOP = 2, 31
        LAST_SLOT = N + 5

        def slots(eng, slot, new_layer=None):
            for s in range(-2, 4 * FIRST_LOOP):
                slot(s, s % 4)
            g0 = FIRST_LOOP
            for ly in range(1, LAYERS) if new_layer else ():
                g1 = (B * ly + 4) // 4
                with eng.Fori(g0, g1) as g:
                    for u in range(4):
                        slot(4 * g + u, u)
                slot(4 * g1, 0)
                new_layer(ly)
                for u in range(1, 4):
                    slot(4 * g1 + u, u)
                g0 = g1 + 1
            with eng.Fori(g0, LAST_LOOP) as g:
                for u in range(4):
                    slot(4 * g + u, u)
            for s in range(4 * LAST_LOOP, LAST_SLOT):
                slot(s, s % 4)

        def live(n):
            return not isinstance(n, int) or 0 <= n < N

        A_STEPS = ((5,), (6,), (7, 8), (9,), (10,), (11,), (), (), (), (0, 1), (2, 3), (4,))

        def a_steps(s, u, k):
            n, v = (s - 3, u - 3) if k > 8 else (s - 4, u - 4)
            return [(n, v, bk) for bk in A_STEPS[k] if live(n)]

        def group_heads(grp):
            return [H // 2 * (grp // 2) + 2 * i + grp % 2 for i in range(4)]

        block = ctx.enter_context(nc.Block())

        @block.sync
        def _(sp):
            sp.dma_start(squares[:], a["c_squares"].rearrange("p (a n) -> p a n", a=3)).then_inc(squares_landed, 16)
            sp.dma_start(keys_f[:], a["c_keys"]).then_inc(squares_landed, 16)
            for c in range(X_PARTS):
                w = B // X_PARTS
                sp.dma_start(h_all[:, c * w:(c + 1) * w], x_tiles[:, c * w:(c + 1) * w]).then_inc(x_landed[c], 16)
            sp.dma_start(w_qkv[:], a["w_qkv"].rearrange("l p n -> p l n")).then_inc(consts_landed, 16)
            sp.dma_start(ln_cols[:], a["ln_cols"].rearrange("p (l c) -> p l c", l=LAYERS)).then_inc(consts_landed, 16)
            sp.dma_start(b_cols[:], a["b_cols"].rearrange("p (l c) -> p l c", l=LAYERS)).then_inc(consts_landed, 16)
            sp.dma_start(u_cols[:], a["u_cols"].rearrange("p (l c) -> p l c", l=LAYERS)).then_inc(consts_landed, 16)
            sp.dma_start(b_v[:], a["b_v"].rearrange("(o l) n -> o l n", o=1).broadcast_to([128, LAYERS, D])).then_inc(consts_landed, 16)
            sp.dma_start(turn[:], a["c_turn"].rearrange("p (a n) -> p a n", a=2)).then_inc(consts_landed, 16)
            sp.wait_ge(consts_cast, 5)
            for r in range(RING):
                sp.dma_start(kstack[ROT0:STACK, r], keys_b[:].unsqueeze(1).broadcast_to([STACK - ROT0, H, S])
                             ).then_inc(keys_landed, 16)
            sp.dma_start(b_o[:], a["bo"].rearrange("(o l) n -> o l n", o=1).broadcast_to([128, LAYERS, D])).then_inc(consts_landed, 16)
            sp.dma_start(b_2[:], a["b2"].rearrange("(o l) n -> o l n", o=1).broadcast_to([128, LAYERS, D])).then_inc(consts_landed, 16)
            sp.dma_start(w_o[:], a["w_o"].rearrange("l p n -> p l n")).then_inc(consts_landed, 16)
            sp.dma_start(b_1[:], a["b_1"].rearrange("p (l c) -> p l c", l=LAYERS)).then_inc(consts_landed, 16)
            sp.dma_start(w_2[:], a["w_2"].rearrange("l (c p) n -> p l c n", p=128)).then_inc(consts_landed, 16)
            sp.dma_start(w_1[:], a["w_1"][0]).then_inc(w1_landed, 16)

            def slot(s, u):
                n, r, p = s - 1, (u - 1) % RING, (u - 1) % 2
                m, mr = s - 3, (u - 3) % RING
                if live(n):
                    wait_alone(sp, qk_third, n + 1, apart_sp)
                    wait_alone(sp, rot_third, n + 1, apart_sp)
                    wait_alone(sp, scoresT_done, STEPS * (n - 3), apart_sp)
                for c in range(NB):
                    rows = slice(c * HD, (c + 1) * HD)
                    rot_rows = slice(ROT0 + c * HD, ROT0 + (c + 1) * HD)
                    if c == NB // 2 and live(m):
                        wait_alone(sp, maxrows_ready, m + 1, apart_sp)
                        for i in range(2):
                            sp.dma_start(qstack[MROW + i:MROW + i + 1, mr], maxrows[i * H:(i + 1) * H, :]
                                         ).then_inc(maxrows_landed, 16)
                    if live(n):
                        sp.dma_start(qstack[rows, r], base[:, p, PARTS_Q[c], 0]).then_inc(stack_landed[r], 16)
                        sp.dma_start(kstack[rows, r], base[:, p, PARTS_K[c], 1]).then_inc(stack_landed[r], 16)
                        sp.dma_start(qstack[rot_rows, r], base[:, p, PARTS_Q[c], 2]).then_inc(stack_landed[r], 16)

            def next_w1(ly):
                sp.wait_ge(w1_split, 2 * ly)
                sp.dma_start(w_1[:], a["w_1"][ly]).then_inc(w1_landed, 16)

            slots(sp, slot, next_w1)

        @block.tensor
        def _(pe):
            def f1(n):
                pe.wait_ge(xn1_ready, 2 * (n + 1))
                at_least(pe, qk_rest, n)
                for t in range(T):
                    last = pe.transpose(bank[:, 5, t * 128:(t + 1) * 128], xn1[:, t], eye)
                last.then_inc(xn1_turned, 1)

            def f2(n, u, half):
                b = 5 + half
                x = [xn1T_parts[:, p] for p in range(2)]

                def w(i):
                    return [w_now[:, u % 2, p, i * D:(i + 1) * D] for p in range(2)]

                if half == 0:
                    pe.wait_ge(xn1_low, n + 1)
                    pe.wait_ge(weights_now, n + 1)
                    product_of_parts(pe, bank[:, b, 0:S], w(0), x)
                    product_of_parts(pe, bank[:, b, S:2 * S], w(1), x).then_inc(qkv_done, 1)
                else:
                    at_least(pe, v_ready, n)
                    at_least(pe, maxrows_ready, n - 2)
                    product_of_parts(pe, bank[:, b, 0:S], w(2), x)
                    for t in range(T):
                        last = pe.matmul(bank[:, b, S + t * D:S + (t + 1) * D], xn1T[:, t * 128:(t + 1) * 128],
                                         w_qkv[:, layer(n), 3 * D:4 * D], start=True, stop=True)
                    last.then_inc(qkv_done, 1)

            def m_bank(n, u, k):
                r = u % RING
                if k == 0:
                    pe.wait_ge(stack_landed[r], 16 * STACK_DMAS * (n // RING + 1))
                at_least(pe, max_done, STEPS * n + k - 1)
                b = k % 2
                if k < 4:
                    for i in range(4):
                        hd = 4 * k + i
                        last = pe.matmul(bank[:, b, i * 128:(i + 1) * 128], qstack[0:MROW, r, hd, 0:128],
                                         kstack[0:MROW, r, hd, 0:128], start=True, stop=True)
                else:
                    two = bank[:, b, :].rearrange("p (h k) -> p h k", h=2)
                    for i in range(2):
                        hd = 2 * (k - 4) + i
                        last = pe.matmul(two[:, i], qstack[0:MROW, r, hd, 128:256], kstack[0:MROW, r, hd, :],
                                         start=True, stop=True)
                last.then_inc(scores_done, 1)

            def m1(n):
                pe.wait_ge(max_split, 2 * (n + 1))
                pe.wait_ge(v_ready, capped(n + 3, N))
                at_least(pe, gelu_done, FC * (n - 2))
                for t in range(T):
                    last = pe.transpose(bank16(6)[0:2 * H, t * 128:(t + 1) * 128],
                                        maxparts[:, t].rearrange("p a h -> p (a h)"), eyeb[:])
                last.then_inc(max_turned, 1)

            def a_bank(n, u, k):
                r = u % RING
                if k == 0:
                    pe.wait_ge(maxrows_landed, 32 * (n + 1))
                at_least(pe, exp_done, STEPS * n + k - 1)
                b = 2 + k % 2
                grp, kind = k // 3, k % 3
                heads = group_heads(grp)
                if kind < 2:
                    two = bank[:, b, :].rearrange("p (h q) -> p h q", h=2)
                    pe.matmul(two[:, :, 0:128], eyeb[:], maskT[:, 0:2], start=True, stop=True)
                    for i in range(2):
                        hd = heads[2 * kind + i]
                        last = pe.matmul(two[:, i], kstack[:, r, hd, 0:128], qstack[:, r, hd, :],
                                         start=False, stop=True, skip_group_check=True)
                else:
                    pe.matmul(bank[:, b, :], eyeb[:], maskT[:], start=True, stop=True)
                    for i in range(4):
                        hd = heads[i]
                        last = pe.matmul(bank[:, b, i * 128:(i + 1) * 128], kstack[:, r, hd, 128:256],
                                         qstack[:, r, hd, 128:256], start=False, stop=True, skip_group_check=True)
                last.then_inc(scoresT_done, 1)

            def pv(n, u, grp):
                pe.wait_ge(exp_done, STEPS * n + 3 * grp + 3)
                if grp == 0:
                    pe.wait_ge(vpad_ready, n + 1)
                    at_least(pe, context_out, n)
                v = u % 2
                c0, j = (grp // 2) * S, grp % 2
                w = slice(HW, 3 * HW) if j == 0 else slice(0, 2 * HW)
                for i, hd in enumerate(group_heads(grp)):
                    p0 = probs[:, (3 * grp + i // 2) % PR, (i % 2) * S:(i % 2 + 1) * S]
                    pe.matmul(bank[32 * i:32 * i + 32, 4, c0:c0 + S], v_pad[:, v, 0, hd, w], p0,
                              start=(j == 0), stop=True, skip_group_check=True)
                for i, hd in enumerate(group_heads(grp)):
                    p1 = probs[:, (3 * grp + 2) % PR, i * 128:(i + 1) * 128]
                    last = pe.matmul(bank[32 * i:32 * i + 32, 4, c0 + 128:c0 + S], v_pad[:, v, 1, hd, w], p1,
                                     start=False, stop=True, skip_group_check=True)
                last.then_inc(context_done, 1)

            def b1(n):
                pe.wait_ge(context_out, n + 1)
                at_least(pe, h2_ready, n)
                for t in range(T):
                    for half in range(2):
                        c = t * S + half * 128
                        last = pe.transpose(bank[:, 7, c:c + 128], ctxT_raw[:, half, t * 128:(t + 1) * 128], eye)
                last.then_inc(context_turned, 1)

            def b2(n):
                pe.wait_ge(ctx_ready, n + 1)
                for t in range(T):
                    last = pe.transpose(bank[:, 7, t * 128:(t + 1) * 128], ctx_tok[:, t * D:(t + 1) * D], eye)
                last.then_inc(ctx_turned, 1)

            def b3(n):
                pe.wait_ge(ctxT_ready, n + 1)
                for t in range(T):
                    last = pe.matmul(bank[:, 7, t * 128:(t + 1) * 128], ctxT[:, t * 128:(t + 1) * 128],
                                     w_o[:, layer(n)], start=True, stop=True)
                last.then_inc(proj_done, 1)

            def b4(n):
                pe.wait_ge(xn2_ready, 2 * (n + 1))
                for t in range(T):
                    last = pe.transpose(bank[:, 7, t * 128:(t + 1) * 128], xn2[:, t], eye)
                last.then_inc(xn2_turned, 1)

            def b5(n, half):
                if half == 0:
                    pe.wait_ge(xn2_low, n + 1)
                    pe.wait_ge(w1_split, 2 * (layer(n) + 1))
                else:
                    pe.wait_ge(v_ready, capped(n + 6, N))
                    pe.wait_ge(maxrows_ready, capped(n + 3, N))
                b = 7 - half
                for i in range(2):
                    c = 2 * half + i
                    last = product_of_parts(pe, bank[:, b, i * S:(i + 1) * S],
                                            [w_1_parts[:, p, c * 128:(c + 1) * 128] for p in range(2)],
                                            [xn2T_parts[:, p] for p in range(2)])
                last.then_inc(up_done, 1)

            def b6(n):
                pe.wait_ge(gelu_done, FC * (n + 1))
                for t in range(T):
                    for c in range(FC):
                        last = pe.matmul(bank[:, 7, t * 128:(t + 1) * 128], hidden[:, c, t * 128:(t + 1) * 128],
                                         w_2[:, layer(n), c], start=(c == 0), stop=(c == FC - 1))
                last.then_inc(down_done, 1)

            pe.wait_ge(consts_landed, 16 * CONST_DMAS)
            pe.wait_ge(keys_landed, 16 * RING)
            pe.wait_ge(consts_cast, 6)
            pe.wait_ge(prefilled, 2)

            def slot(s, u):
                for k in range(STEPS):
                    if live(s - 2):
                        m_bank(s - 2, u - 2, k)
                    if k == 11 and live(s + 1):
                        f2(s + 1, u + 1, 0)
                    for n, v, bk in a_steps(s, u, k):
                        if bk == 8:
                            pv(n, v, 1)
                        a_bank(n, v, bk)
                    if k == 0 and live(s - 5):
                        b3(s - 5)
                    if k == 0 and live(s - 4):
                        pv(s - 4, u - 4, 0)
                    if k == 1 and live(s - 3):
                        m1(s - 3)
                    if k == 3 and live(s):
                        f2(s, u, 1)
                    if k == 3 and live(s - 5):
                        b4(s - 5)
                    if k == 5 and live(s - 4):
                        pv(s - 4, u - 4, 2)
                    if k in (5, 6) and live(s - 5):
                        b5(s - 5, k - 5)
                    if k == 7 and live(s - 4):
                        pv(s - 4, u - 4, 3)
                    if k == 8 and live(s + 1):
                        f1(s + 1)
                    if k == 8 and live(s - 5):
                        b6(s - 5)
                    if k == 9 and live(s - 4):
                        b1(s - 4)
                    if k == 11 and live(s - 4):
                        b2(s - 4)

            slots(pe, slot)

        @block.scalar
        def _(act):
            def exp_bank(n, k):
                act.wait_ge(scoresT_done, STEPS * n + k + 1)
                at_least(act, context_done, 4 * n + (k - PR) // 3 + 1)
                act.activation(probs[:, k % PR], bank[:, 2 + k % 2, :], ACT.Exp, scale=SCALE).then_inc(exp_done, 1)

            def xn1T_out(n):
                scale, bias = ln_cols[:, layer(n), 0:1], ln_cols[:, layer(n), 1:2]
                act.wait_ge(xn1_turned, n + 1)
                at_least(act, qkv_done, 2 * n)
                act.activation(xn1T[:], bank[:, 5, 0:S], ACT.Identity, scale=scale, bias=bias).then_inc(xn1T_ready, 1)
                act.wait_ge(xn1T_ready, n + 1)
                act.copy(xn1T_parts[:, 0], xn1T[:]).then_inc(xn1_high, 1)

            def xn2T_out(n):
                scale, bias = ln_cols[:, layer(n), 2:3], ln_cols[:, layer(n), 3:4]
                act.wait_ge(xn2_turned, n + 1)
                at_least(act, up_done, 2 * n)
                act.activation(xn2T[:], bank[:, 7, 0:S], ACT.Identity, scale=scale, bias=bias).then_inc(xn2T_ready, 1)
                act.wait_ge(xn2T_ready, n + 1)
                act.copy(xn2T_parts[:, 0], xn2T[:]).then_inc(xn2_high, 1)

            def split_first(n, u):
                act.wait_ge(qkv_done, 2 * n + 1)
                if not (isinstance(n, int) and n < 2):
                    act.wait_ge(stack_landed[(u - 2) % RING], 16 * STACK_DMAS * ((n - 2) // RING + 1))
                for src in range(2):
                    last = act.activation(base[:, u % 2, 0, src], bank[:, 5, src * S:(src + 1) * S], ACT.Identity,
                                          bias=cols_now[:, u % 2, src:src + 1])
                last.then_inc(qk_first, 1)

            def split_second(n, u):
                act.wait_ge(qk_rest, n + 1)
                act.copy(base[:, u % 2, 1, 0:2], rest[:, 0:2]).then_inc(qk_second, 1)

            def rot_split_first(n, u):
                act.wait_ge(rot_ready, n + 1)
                act.copy(base[:, u % 2, 0, 2], rotated[:]).then_inc(rot_first, 1)

            def rot_split_second(n, u):
                act.wait_ge(rot_rest, n + 1)
                act.copy(base[:, u % 2, 1, 2], rest[:, 2]).then_inc(rot_second, 1)

            def context_copy(n):
                act.wait_ge(context_done, 4 * (n + 1))
                at_least(act, context_turned, n)
                act.copy(ctxT_raw[:].rearrange("p g c -> p (g c)"), bank[:, 4, :]).then_inc(context_out, 1)

            def maxrows_out(n):
                act.wait_ge(max_turned, n + 1)
                at_least(act, maxrows_landed, 32 * n)
                act.copy(maxrows[:], bank16(6)[0:2 * H, 0:S]).then_inc(maxrows_ready, 1)

            def ctxT_out(n):
                act.wait_ge(ctx_turned, n + 1)
                at_least(act, proj_done, n)
                act.copy(ctxT[:], bank[:, 7, 0:S]).then_inc(ctxT_ready, 1)

            def load_table(count, function):
                at_least(act, tables_loaded, count)
                act.activation(table_probe[:], expo[:, 0:1], function).then_inc(tables_loaded, 1)

            def gelu(n):
                for c in range(FC):
                    act.wait_ge(up_done, 2 * n + c // 2 + 1)
                    if c == 0:
                        at_least(act, down_done, n)
                    act.activation(hidden[:, c], bank[:, 7 - c // 2, (c % 2) * S:(c % 2 + 1) * S], ACT.Gelu,
                                   bias=b_1[:, layer(n), c:c + 1]).then_inc(gelu_done, 1)

            act.wait_ge(consts_landed, 16 * CONST_DMAS)
            act.wait_ge(prefilled, 2)

            def slot(s, u):
                for k in range(STEPS):
                    if k == 4 and live(s - 5):
                        xn2T_out(s - 5)
                    for n, _, bk in a_steps(s, u, k):
                        exp_bank(n, bk)
                    if k == 0 and live(s):
                        split_first(s, u)
                    if k == 1 and live(s - 3):
                        maxrows_out(s - 3)
                    if k == 5 and live(s - 5):
                        load_table(2 * (s - 5), ACT.Gelu)
                    if k == 6 and live(s - 5):
                        gelu(s - 5)
                        load_table(2 * (s - 5) + 1, ACT.Exp)
                    if k == 8 and live(s - 4):
                        context_copy(s - 4)
                    if k == 8 and live(s):
                        rot_split_first(s, u)
                    if k == 11 and live(s - 4):
                        ctxT_out(s - 4)
                    if k == 11 and live(s):
                        split_second(s, u)
                    if k == 8 and live(s + 1):
                        xn1T_out(s + 1)
                    if k == 10 and live(s):
                        rot_split_second(s, u)

            slots(act, slot)

        @block.vector
        def _(dve):
            dve.memset(expo[:], -0.5).then_inc(prefilled, 1)
            dve.wait_ge(squares_landed, 32)
            dve.tensor_copy(keys_b[:], keys_f[:]).then_inc(consts_cast, 1)
            dve.tensor_copy(eyeb[:], eye).then_inc(consts_cast, 1)
            dve.memset(mask[:, 0], 0.0).then_inc(consts_cast, 1)
            dve.tensor_copy(mask[:, 1], squares[:, 1]).then_inc(consts_cast, 1)
            dve.tensor_copy(maskT[:], squares[:, 2:3].broadcast_to([128, 4, 128])).then_inc(consts_cast, 1)
            rounds = B // PER // X_PARTS
            for part in range(X_PARTS):
                dve.wait_ge(x_landed[part], 16)
                with dve.Fori(part * rounds, (part + 1) * rounds) as c:
                    for i in range(PER * T):
                        last = dve.bn_stats(stats0[:, i], h_all[:, c * PER + i // T, i % T])
                    last.then_inc(stats0_done, 1)
                    wait_alone(dve, stats0_done, c + 1, apart_dve)
                    for i in range(PER * T):
                        last = dve.bn_aggr(mv0[:, i], stats0[:, i])
                    last.then_inc(mv0_ready, 1)
                    dve.wait_ge(rstd0_ready, c + 1)
                    for i in range(PER * T):
                        tile = h_all[:, c * PER + i // T, i % T]
                        last = dve.tensor_scalar(tile, tile, mv0[:, i, 0:1], rstd0[:, i:i + 1], ALU.subtract, ALU.mult)
                    last.then_inc(ln0_done, 1)
            dve.wait_ge(ln0_done, B // PER)

            def norm_stats(stats, mv, stats_sem, mv_sem, n):
                b = mod(n, B)
                for t in range(T):
                    last = dve.bn_stats(stats[:, t], h_all[:, b, t])
                last.then_inc(stats_sem, 1)
                wait_alone(dve, stats_sem, n + 1, apart_dve)
                for t in range(T):
                    last = dve.bn_aggr(mv[:, t], stats[:, t])
                last.then_inc(mv_sem, 1)

            def norm_apply(xn, mv, rstd, rstd_sem, used_sem, xn_sem, n):
                b = mod(n, B)
                dve.wait_ge(rstd_sem, n + 1)
                at_least(dve, used_sem, n)
                for t in range(T):
                    dve.tensor_scalar(xn[:, t], h_all[:, b, t], mv[:, t, 0:1], rstd[:, t:t + 1],
                                      ALU.subtract, ALU.mult).then_inc(xn_sem, 1)

            def stats_1(n):
                norm_stats(stats1, mv1, stats1_done, mv1_ready, n)

            def apply_1(n):
                norm_apply(xn1, mv1, rstd1, rstd1_ready, xn1_turned, xn1_ready, n)

            def stats_2(n):
                wait_alone(dve, h1_ready, n + 1, apart_dve)
                norm_stats(stats2, mv2, stats2_done, mv2_ready, n)

            def apply_2(n):
                norm_apply(xn2, mv2, rstd2, rstd2_ready, xn2_turned, xn2_ready, n)

            def xn2_rest(n):
                dve.wait_ge(xn2_high, n + 1)
                at_least(dve, up_done, 2 * n)
                dve.tensor_tensor(xn2T_parts[:, 1], xn2T[:], xn2T_parts[:, 0].bitcast(F32), ALU.subtract
                                  ).then_inc(xn2_low, 1)

            def turn_q(n, u, half):
                if half == 0:
                    dve.wait_ge(qk_first, n + 1)
                else:
                    dve.wait_ge(qkv_done, 2 * (n + 1))
                at_least(dve, rot_ready, n)
                dve.scalar_tensor_tensor((turn_s, turn_c)[half][:], bank[:, 5 + half, 0:S],
                                         cols_now[:, u % 2, 2 + half:3 + half], turn[:, half], ALU.add, ALU.mult
                                         ).then_inc(turn_steps, 1)

            def v_out(n, u):
                at_least(dve, vpad_ready, n - 3)
                dve.tensor_tensor(v_tok[:, u % RING], bank[:, 6, S:2 * S].rearrange("p (t c) -> p t c", t=T),
                                  b_v[:, layer(n)].unsqueeze(1).broadcast_to([128, T, D]), ALU.add
                                  ).then_inc(v_ready, 1)

            def split_rest(n, u):
                at_least(dve, qk_third, n)
                for src in range(2):
                    last = dve.scalar_tensor_tensor(rest[:, src], bank[:, 5, src * S:(src + 1) * S],
                                                    cols_now[:, u % 2, src:src + 1], base[:, u % 2, 0, src],
                                                    ALU.add, ALU.subtract)
                last.then_inc(qk_rest, 1)

            def max_bank(n, u, k):
                wait_alone(dve, scores_done, STEPS * n + k + 1, apart_dve)
                t, heads = (0, 4) if k < 4 else (1, 2)
                wide = 512 // heads
                for i in range(heads):
                    hd = heads * (k - 4 * t) + i
                    at = bank[:, k % 2, i * wide:(i + 1) * wide]
                    m = mask[:, 1] if t == 0 else mask[:].rearrange("p a c -> p (a c)")
                    last = dve.tensor_tensor_reduce(at, at, m, 1.0, LOW, ALU.add, ALU.max,
                                                    rowmax[:, u % 2, t, hd:hd + 1])
                last.then_inc(max_done, 1)

            def max_parts(n, u):
                dve.wait_ge(max_done, STEPS * (n + 1))
                at_least(dve, max_turned, n)
                m = rowmax[:, u % 2]
                dve.tensor_copy(maxparts[:, :, 0], m).then_inc(max_split, 1)
                dve.wait_ge(max_split, 2 * n + 1)
                dve.tensor_tensor(maxparts[:, :, 1], m, maxparts[:, :, 0], ALU.subtract).then_inc(max_split, 1)

            def divide(n):
                dve.wait_ge(context_turned, n + 1)
                v = bank[:, 7, :].rearrange("p (h w) -> p h w", w=HW)
                dve.reciprocal(rsum[:], v[:, :, HD]).then_inc(rsum_ready, 1)
                dve.wait_ge(rsum_ready, n + 1)
                at_least(dve, ctx_turned, n)
                dve.tensor_tensor(ctx_tok[:].rearrange("p (h w) -> p h w", w=HD), v[:, :, 0:HD],
                                  rsum[:].unsqueeze(2).broadcast_to([128, T * H, HD]), ALU.mult
                                  ).then_inc(ctx_ready, 1)

            def resid_1(n):
                h = h_all[:, mod(n, B)].rearrange("p t c -> p (t c)")
                dve.wait_ge(bo_added, n + 1)
                dve.wait_ge(proj_done, n + 1)
                dve.tensor_tensor(h, bank[:, 7, 0:S], h, ALU.add).then_inc(h1_ready, 1)

            def resid_2(n):
                h = h_all[:, mod(n, B)].rearrange("p t c -> p (t c)")
                dve.wait_ge(b2_added, n + 1)
                dve.wait_ge(down_done, n + 1)
                dve.tensor_tensor(h, bank[:, 7, 0:S], h, ALU.add).then_inc(h2_ready, 1)

            dve.wait_ge(consts_landed, 16 * CONST_DMAS)
            dve.tensor_tensor(b_cols[:, :, 2:4], b_cols[:, :, 2:4], u_cols[:], ALU.add).then_inc(consts_cast, 1)

            def slot(s, u):
                for k in range(STEPS):
                    if k == 0 and live(s - 3):
                        max_parts(s - 3, u - 3)
                    if k == 0 and live(s + 1):
                        apply_1(s + 1)
                    if k == 1 and live(s - 5):
                        resid_1(s - 5)
                    if k == 3 and live(s - 5):
                        apply_2(s - 5)
                    if k == 9 and live(s - 5):
                        resid_2(s - 5)
                    if k == 11 and live(s - 4):
                        divide(s - 4)
                    if live(s - 2):
                        max_bank(s - 2, u - 2, k)
                    if k == 1 and live(s - 5):
                        stats_2(s - 5)
                    if k == 4 and live(s):
                        turn_q(s, u, 1)
                    if k == 4 and live(s - 5):
                        xn2_rest(s - 5)
                    if k == 4 and live(s):
                        v_out(s, u)
                    if k == 5 and live(s):
                        turn_q(s, u, 0)
                        split_rest(s, u)
                    if k == 8 and live(s + 2):
                        stats_1(s + 2)

            slots(dve, slot)

        @block.gpsimd
        def _(pool):
            pool.memset(v_pad[:], 0.0).then_inc(zeros_filled, 1)
            pool.wait_ge(zeros_filled, 1)
            pool.memset(v_pad[:, :, :, :, HW + HD:HW + HD + 1], 1.0).then_inc(prefilled, 1)
            pool.wait_ge(prefilled, 2)
            with pool.Fori(0, B // PER) as c:
                wait_alone(pool, mv0_ready, c + 1, apart_pool)
                pool.tensor_scalar(ve0[:], mv0[:, :, 1], 1e-5, None, ALU.add).then_inc(ve0_ready, 1)
                pool.wait_ge(ve0_ready, c + 1)
                pool.tensor_tensor(rstd0[:], ve0[:], expo[:, 0:PER * T], ALU.pow).then_inc(rstd0_ready, 1)
            pool.wait_ge(consts_landed, 16 * CONST_DMAS)
            pool.wait_ge(consts_cast, 6)

            def power(ve, mv, rstd, mv_sem, ve_sem, rstd_sem, n):
                wait_alone(pool, mv_sem, n + 1, apart_pool)
                pool.tensor_scalar(ve[:], mv[:, :, 1], 1e-6, None, ALU.add).then_inc(ve_sem, 1)
                pool.wait_ge(ve_sem, n + 1)
                pool.tensor_tensor(rstd[:], ve[:], expo[:, 0:T], ALU.pow).then_inc(rstd_sem, 1)

            def layer_now(n, u):
                wait_alone(pool, v_ready, n - 1, apart_pool)
                wait_alone(pool, qk_rest, n - 1, apart_pool)
                w, high = w_qkv[:, layer(n), 0:3 * D], w_now[:, u % 2, 0]
                pool.tensor_copy(high, w)
                pool.tensor_copy(cols_now[:, u % 2], b_cols[:, layer(n)]).then_inc(weights_high, 1)
                wait_alone(pool, weights_high, n + 1, apart_pool)
                pool.tensor_tensor(w_now[:, u % 2, 1], w, high.bitcast(F32), ALU.subtract).then_inc(weights_now, 1)

            def split_w1(ly):
                at_least(pool, up_done, 2 * B * ly)
                pool.wait_ge(w1_landed, 16 * (ly + 1))
                pool.tensor_copy(w_1_parts[:, 0], w_1[:]).then_inc(w1_split, 1)
                pool.wait_ge(w1_split, 2 * ly + 1)
                pool.tensor_tensor(w_1_parts[:, 1], w_1[:], w_1_parts[:, 0].bitcast(F32), ALU.subtract
                                   ).then_inc(w1_split, 1)

            def xn1_rest(n):
                pool.wait_ge(xn1_high, n + 1)
                at_least(pool, qkv_done, 2 * n)
                pool.tensor_tensor(xn1T_parts[:, 1], xn1T[:], xn1T_parts[:, 0].bitcast(F32), ALU.subtract
                                   ).then_inc(xn1_low, 1)

            def turned(n):
                pool.wait_ge(turn_steps, 2 * (n + 1))
                at_least(pool, rot_third, n)
                pool.tensor_tensor(rotated[:], turn_s[:], turn_c[:], ALU.add).then_inc(rot_ready, 1)

            def split_third(n, u):
                pool.wait_ge(qk_second, n + 1)
                pool.tensor_tensor(base[:, u % 2, 2, 0:2], rest[:, 0:2], base[:, u % 2, 1, 0:2], ALU.subtract
                                   ).then_inc(qk_third, 1)

            def rot_split_rest(n, u):
                pool.wait_ge(rot_first, n + 1)
                pool.tensor_tensor(rest[:, 2], rotated[:], base[:, u % 2, 0, 2], ALU.subtract).then_inc(rot_rest, 1)

            def rot_split_third(n, u):
                pool.wait_ge(rot_second, n + 1)
                pool.tensor_tensor(base[:, u % 2, 2, 2], rest[:, 2], base[:, u % 2, 1, 2], ALU.subtract
                                   ).then_inc(rot_third, 1)

            def v_padded(n, u):
                pool.wait_ge(v_ready, n + 1)
                wait_alone(pool, context_done, 4 * (n - 1), apart_pool)
                pool.tensor_copy(v_pad[:, u % 2, :, :, HW:HW + HD],
                                 v_tok[:, u % RING].rearrange("p t (h w) -> p t h w", w=HD)
                                 ).then_inc(vpad_ready, 1)

            def add_row(n, rows, read_sem, value, added_sem):
                wait_alone(pool, read_sem, value, apart_pool)
                h = h_all[:, mod(n, B)]
                pool.tensor_tensor(h, h, rows[:, layer(n)].unsqueeze(1).broadcast_to([128, T, D]), ALU.add
                                   ).then_inc(added_sem, 1)

            def slot(s, u):
                for k in range(STEPS):
                    if k == 2 and live(s - 5):
                        power(ve2, mv2, rstd2, mv2_ready, ve2_ready, rstd2_ready, s - 5)
                    if k == 4 and live(s - 5):
                        add_row(s - 5, b_2, xn2_ready, 2 * (s - 4), b2_added)
                    if k == 5 and live(s + 1):
                        layer_now(s + 1, u + 1)
                    if k == 6 and live(s):
                        turned(s)
                    if k == 8 and live(s):
                        rot_split_rest(s, u)
                    if k == 9 and live(s + 1):
                        xn1_rest(s + 1)
                    if k == 9 and live(s - 4):
                        add_row(s - 4, b_o, xn1_ready, 2 * (s - 3), bo_added)
                    if k == 9 and live(s + 2):
                        power(ve1, mv1, rstd1, mv1_ready, ve1_ready, rstd1_ready, s + 2)
                    if k == 10 and live(s):
                        rot_split_third(s, u)
                    if k == 10 and live(s - 2):
                        v_padded(s - 2, u - 2)
                    if k == 11 and live(s):
                        split_third(s, u)

            split_w1(0)
            slots(pool, slot, split_w1)


def experts_program(nc, a, h_all, out):
    with ExitStack() as ctx:
        def sb(name, shape, dt=F32):
            return ctx.enter_context(nc.sbuf_tensor(name, shape, dt))

        def sem(name):
            return ctx.enter_context(nc.semaphore(name))

        bank = ctx.enter_context(nc.psum_tensor("ebank", [128, 8, 512], F32))

        GT = 4
        NG = NT // GT
        w_in = sb("w_in", [128, 2 * GU])
        w_in_parts = sb("w_in_parts", [128, 2, 2 * GU], F32R)
        w_down = sb("w_down", [128, GU // 128, D])
        w_router = sb("w_router", [128, E])
        bias_rows = sb("bias_rows", [128, E])
        eye = sb("eeye", [128, 128])
        expo = sb("eexpo", [128, GT])
        xin = sb("xin", [128, 2, GT, D])
        stats = sb("estats", [128, GT, 6])
        mv = sb("emv", [128, GT, 2])
        ve = sb("eve", [128, GT])
        rstd = sb("erstd", [128, GT])
        xn = sb("exn", [128, GT, D])
        xT = sb("exT", [128, 2, GT, 128])
        xT_parts = sb("exT_parts", [128, 2, 2, GT, 128], F32R)
        score = sb("score", [128, GT, E])
        biased = sb("biased", [128, GT, E])
        larger = sb("larger", [128, GT * G, 2])
        smaller = sb("smaller", [128, GT * G, 2])
        tops = sb("tops", [128, 3, GT * G])
        gs = sb("gs", [128, GT, 14])
        gtop = sb("gtop", [128, GT, 8])
        grep = sb("grep", [128, GT, 8])
        gout = sb("gout", [128, GT, 10])
        kept = sb("kept", [128, GT, G])
        pen = sb("pen", [128, GT, G])
        cand = sb("cand", [128, GT, E + 4])
        ctop = sb("ctop", [128, GT, 8])
        crep = sb("crep", [128, GT, 8])
        cout = sb("cout", [128, GT, E + 4])
        chosen = sb("chosen", [128, GT, E])
        wsel = sb("wsel", [128, GT, E])
        wsum = sb("wsum", [128, GT])
        wsum1 = sb("wsum1", [128, GT])
        winv = sb("winv", [128, GT])
        combine = sb("combine", [128, 2, GT, E])
        gate_act = sb("gate_act", [128, 2, GU])
        act_all = sb("act_all", [128, 2, GU])
        hw = sb("hw", [128, 2, E * EH])
        hT = sb("hT", [128, GU // 128, 128])
        ot = sb("ot", [128, 2, GT, D])

        weights_landed = sem("weights_landed")
        apart_dve, apart_pool, apart_sp = (sem(f"eapart_{e}") for e in ("dve", "pool", "sp"))
        xin_landed = [sem(f"xin_landed{i}") for i in range(2)]
        filled = sem("filled")
        x1_ready = sem("x1_ready")
        stats_done = sem("estats_done")
        mv_ready = sem("emv_ready")
        ve_ready = sem("eve_ready")
        rstd_ready = sem("erstd_ready")
        xn_ready = sem("exn_ready")
        xn_turned = sem("exn_turned")
        xT_ready = sem("exT_ready")
        weights_split = sem("weights_split")
        xT_high = sem("xT_high")
        xT_low = sem("xT_low")
        logits_done = sem("logits_done")
        score_ready = sem("score_ready")
        route = sem("route")
        route_end = sem("route_end")
        combine_ready = sem("combine_ready")
        in_done = sem("in_done")
        gate_ready = sem("gate_ready")
        act_ready = sem("act_ready")
        hw_ready = sem("hw_ready")
        h_turned = sem("h_turned")
        hT_ready = sem("hT_ready")
        down_done = sem("edown_done")
        out_ready = sem("out_ready")
        out_landed = [sem(f"out_landed{i}") for i in range(2)]

        h_groups = h_all[:].rearrange("p b t d -> p (b t) d").rearrange("p (q t) d -> p q t d", t=GT)
        h_tiles = h_all[:].rearrange("p b t d -> p (b t) d")
        x_groups = a["x"].rearrange("b (t p) d -> (b t) p d", p=128).rearrange("(q t) p d -> q p t d", t=GT)
        out_groups = out.rearrange("b (t p) d -> (b t) p d", p=128).rearrange("(q t) p d -> q p t d", t=GT)
        WEIGHT_DMAS = 5
        ROUTE, GROUP_LINKS = 17, 10
        FIRST, LAST = 2, 6

        def live(n):
            return not isinstance(n, int) or 0 <= n < NG

        def live_tile(n):
            return not isinstance(n, int) or 0 <= n < NT

        def slots(eng, slot):
            for q in range(-2, 2 * FIRST):
                slot(q, q % 2)
            with eng.Fori(FIRST, LAST) as g:
                for v in range(2):
                    slot(2 * g + v, v)
            for q in range(2 * LAST, NG + 1):
                slot(q, q % 2)

        block = ctx.enter_context(nc.Block())

        @block.sync
        def _(sp):
            sp.dma_start(eye[:], a["c_squares"][:, 0:128]).then_inc(weights_landed, 16)

            def load(q, v):
                if live(q):
                    wait_alone(sp, x1_ready, q - 1, apart_sp)
                    sp.dma_start(xin[:, v % 2], x_groups[q]).then_inc(xin_landed[v % 2], 16)

            load(0, 0)
            load(1, 1)
            sp.dma_start(w_router[:], a["router"]).then_inc(weights_landed, 16)
            sp.dma_start(bias_rows[:], a["correction"].rearrange("(o e) -> o e", o=1).broadcast_to([128, E])
                         ).then_inc(weights_landed, 16)
            sp.dma_start(w_in[:], a["w_in"]).then_inc(weights_landed, 16)
            sp.dma_start(w_down[:], a["w_down"].rearrange("(c p) n -> p c n", p=128)).then_inc(weights_landed, 16)

            def slot(q, v):
                if not (isinstance(q, int) and q < -1):
                    load(q + 3, v + 3)
                if live(q - 1):
                    wait_alone(sp, out_ready, GT * q, apart_sp)
                    sp.dma_start(out_groups[q - 1], ot[:, (v - 1) % 2]).then_inc(out_landed[(v - 1) % 2], 16)

            slots(sp, slot)
            for r in range(2):
                sp.wait_ge(out_landed[r], 16 * (NG // 2))

        @block.tensor
        def _(pe):
            pe.wait_ge(weights_landed, 16 * WEIGHT_DMAS)
            pe.wait_ge(weights_split, 2)

            def x_turn(q):
                pe.wait_ge(xn_ready, q + 1)
                at_least(pe, score_ready, q)
                for t in range(GT):
                    last = pe.transpose(bank[:, 6, t * 128:(t + 1) * 128], xn[:, t], eye[:])
                last.then_inc(xn_turned, 1)

            def router(q, v):
                pe.wait_ge(xT_ready, q + 1)
                for t in range(GT):
                    last = pe.matmul(bank[:, 6, t * E:(t + 1) * E], xT[:, v % 2, t], w_router[:],
                                     start=True, stop=True)
                last.then_inc(logits_done, 1)

            def product(n, v, u, i):
                if i == 0:
                    at_least(pe, act_ready, n - 1)
                if u == 0 and i == 0:
                    pe.wait_ge(xT_low, n // GT + 1)
                last = product_of_parts(pe, bank[:, 3 * (u % 2) + i, :],
                                        [xT_parts[:, v % 2, p, u] for p in range(2)],
                                        [w_in_parts[:, p, i * 512:(i + 1) * 512] for p in range(2)])
                if i == 2:
                    last.then_inc(in_done, 1)

            def h_turn(n, u, half):
                if half == 0:
                    pe.wait_ge(hw_ready, n + 1)
                    at_least(pe, out_ready, n)
                else:
                    pe.wait_ge(hT_ready, 2 * n + 1)
                for i in range(3):
                    c = 3 * half + i
                    src = hw[:, u % 2, c * 128:(c + 1) * 128] if c < E * EH // 128 else \
                        act_all[:, u % 2, c * 128:(c + 1) * 128]
                    last = pe.transpose(bank[:, 7, i * 128:(i + 1) * 128], src, eye[:])
                last.then_inc(h_turned, 1)

            def down(n):
                pe.wait_ge(hT_ready, 2 * (n + 1))
                for c in range(GU // 128):
                    last = pe.matmul(bank[:, 7, 0:D], hT[:, c], w_down[:, c], start=(c == 0),
                                     stop=(c == GU // 128 - 1))
                last.then_inc(down_done, 1)

            def slot(q, v):
                for u in range(GT):
                    n = GT * q + u
                    if live(q):
                        product(n, v, u, 0)
                    if u == 0 and live(q + 1):
                        x_turn(q + 1)
                    if u == 1 and live(q + 1):
                        router(q + 1, v + 1)
                    if live_tile(n - 2):
                        h_turn(n - 2, u, 0)
                    if live(q):
                        product(n, v, u, 1)
                    if live_tile(n - 2):
                        h_turn(n - 2, u, 1)
                    if live(q):
                        product(n, v, u, 2)
                    if live_tile(n - 2):
                        down(n - 2)

            slots(pe, slot)

        @block.scalar
        def _(act):
            def half_out(n, half):
                act.wait_ge(h_turned, 2 * n + half + 1)
                if half == 0:
                    at_least(act, down_done, n)
                act.copy(hT[:, 3 * half:3 * half + 3].rearrange("p c n -> p (c n)"), bank[:, 7, 0:384]
                         ).then_inc(hT_ready, 1)

            def slot(q, v):
                for u in range(GT):
                    n = GT * q + u
                    if live_tile(n - 1):
                        act.wait_ge(in_done, n)
                        at_least(act, act_ready, n - 2)
                        b = 3 * ((u - 1) % 2)
                        act.activation(gate_act[:, (u - 1) % 2],
                                       bank[:, b:b + 3].rearrange("p b c -> p (b c)")[:, 0:GU], ACT.Silu
                                       ).then_inc(gate_ready, 1)
                    if live_tile(n - 2):
                        half_out(n - 2, 0)
                    if u == 0 and live(q + 1):
                        act.wait_ge(xn_turned, q + 2)
                        at_least(act, in_done, GT * q)
                        act.copy(xT[:, (v + 1) % 2].rearrange("p t c -> p (t c)"), bank[:, 6, :]
                                 ).then_inc(xT_ready, 1)
                    if live_tile(n - 2):
                        half_out(n - 2, 1)
                    if u == 0 and live(q + 1):
                        act.wait_ge(xT_ready, q + 2)
                        act.copy(xT_parts[:, (v + 1) % 2, 0], xT[:, (v + 1) % 2]).then_inc(xT_high, 1)
                    if u == 1 and live(q + 1):
                        act.wait_ge(logits_done, q + 2)
                        at_least(act, combine_ready, q + 1)
                        act.activation(score[:].rearrange("p t e -> p (t e)"), bank[:, 6, 0:GT * E], ACT.Sigmoid
                                       ).then_inc(score_ready, 1)

            slots(act, slot)

        @block.vector
        def _(dve):
            dve.memset(expo[:], -0.5)
            dve.memset(gs[:, :, 0:6], HIGH)
            dve.memset(gs[:, :, 10:14], LOW)
            dve.memset(grep[:], HIGH)
            dve.memset(cand[:, :, E:E + 4], HIGH)
            dve.memset(crep[:], HIGH).then_inc(filled, 1)
            dve.wait_ge(filled, 1)
            dve.wait_ge(weights_landed, 16 * WEIGHT_DMAS)
            dve.tensor_copy(w_in_parts[:, 0], w_in[:]).then_inc(weights_split, 1)
            dve.wait_ge(weights_split, 1)
            dve.tensor_tensor(w_in_parts[:, 1], w_in[:], w_in_parts[:, 0].bitcast(F32), ALU.subtract
                              ).then_inc(weights_split, 1)

            def residual(q, v):
                dve.wait_ge(xin_landed[v % 2], 16 * (q // 2 + 1))
                h = h_groups[:, q]
                dve.tensor_tensor(h, xin[:, v % 2], h, ALU.add).then_inc(x1_ready, 1)
                wait_alone(dve, x1_ready, q + 1, apart_dve)
                for t in range(GT):
                    last = dve.bn_stats(stats[:, t], h_groups[:, q, t])
                last.then_inc(stats_done, 1)
                wait_alone(dve, stats_done, q + 1, apart_dve)
                for t in range(GT):
                    last = dve.bn_aggr(mv[:, t], stats[:, t])
                last.then_inc(mv_ready, 1)

            def norm(q):
                dve.wait_ge(rstd_ready, q + 1)
                at_least(dve, xn_turned, q)
                for t in range(GT):
                    last = dve.tensor_scalar(xn[:, t], h_groups[:, q, t], mv[:, t, 0:1], rstd[:, t:t + 1],
                                             ALU.subtract, ALU.mult)
                last.then_inc(xn_ready, 1)

            step = [0]

            def link(q, ins):
                step[0] += 1
                ins.then_inc(route, 1)
                wait_alone(dve, route, ROUTE * q + step[0], apart_dve)

            def routing_groups_1(q):
                step[0] = 0
                dve.wait_ge(score_ready, q + 1)
                link(q, dve.tensor_tensor(biased[:], score[:], bias_rows[:].unsqueeze(1).broadcast_to([128, GT, E]),
                                          ALU.add))
                v = biased[:].rearrange("p t (g a b) -> p (t g) a b", g=G, a=2)
                dve.tensor_tensor(larger[:], v[:, :, 0], v[:, :, 1], ALU.max)
                link(q, dve.tensor_tensor(smaller[:], v[:, :, 0], v[:, :, 1], ALU.min))
                dve.tensor_tensor(tops[:, 0], larger[:, :, 0], larger[:, :, 1], ALU.max)
                dve.tensor_tensor(tops[:, 1], larger[:, :, 0], larger[:, :, 1], ALU.min)
                link(q, dve.tensor_tensor(tops[:, 2], smaller[:, :, 0], smaller[:, :, 1], ALU.max))
                link(q, dve.tensor_tensor(tops[:, 1], tops[:, 1], tops[:, 2], ALU.max))
                link(q, dve.tensor_tensor(gs[:, :, 6:10], tops[:, 0].rearrange("p (t g) -> p t g", g=G),
                                          tops[:, 1].rearrange("p (t g) -> p t g", g=G), ALU.add))
                for t in range(GT):
                    last = dve.max(gtop[:, t], gs[:, t, 6:14])
                link(q, last)
                link(q, dve.tensor_copy(grep[:, :, 0:2], gtop[:, :, 0:2]))

            def routing_groups_2(q):
                for t in range(GT):
                    last = dve.match_replace(gout[:, t], grep[:, t], gs[:, t, 0:10], LOW)
                link(q, last)
                link(q, dve.tensor_tensor(kept[:], gout[:, :, 6:10], gs[:, :, 6:10], ALU.is_equal))
                link(q, dve.tensor_scalar(pen[:], kept[:], LOW, None, ALU.mult))
                assert step[0] == GROUP_LINKS, step[0]

            def routing_experts(q, v):
                step[0] = GROUP_LINKS
                link(q, dve.tensor_tensor(cand[:, :, 0:E].rearrange("p t (g k) -> p t g k", g=G),
                                          biased[:].rearrange("p t (g k) -> p t g k", g=G),
                                          pen[:].unsqueeze(3).broadcast_to([128, GT, G, E // G]), ALU.add))
                for t in range(GT):
                    last = dve.max(ctop[:, t], cand[:, t, 0:E])
                link(q, last)
                link(q, dve.tensor_copy(crep[:, :, 0:4], ctop[:, :, 0:4]))
                for t in range(GT):
                    last = dve.match_replace(cout[:, t], crep[:, t], cand[:, t], LOW / 2)
                link(q, last)
                link(q, dve.tensor_tensor(chosen[:], cout[:, :, 0:E], cand[:, :, 0:E], ALU.not_equal))
                link(q, dve.tensor_tensor(wsel[:], chosen[:], score[:], ALU.mult))
                link(q, dve.tensor_reduce(wsum[:], wsel[:], AX_X, ALU.add))
                assert step[0] == ROUTE, step[0]
                dve.tensor_scalar(wsum1[:], wsum[:], 1e-20, None, ALU.add).then_inc(route_end, 1)
                dve.wait_ge(route_end, 2 * q + 1)
                dve.reciprocal(winv[:], wsum1[:]).then_inc(route_end, 1)
                dve.wait_ge(route_end, 2 * q + 2)
                at_least(dve, hw_ready, GT * (q - 1))
                dve.tensor_tensor(combine[:, v % 2], wsel[:], winv[:].unsqueeze(2).broadcast_to([128, GT, E]),
                                  ALU.mult).then_inc(combine_ready, 1)

            def gating(n, u):
                g = bank[:, 3 * (u % 2):3 * (u % 2) + 3].rearrange("p b c -> p (b c)")
                at_least(dve, h_turned, 2 * (n - 1))
                at_least(dve, hw_ready, n - 1)
                dve.wait_ge(gate_ready, n + 1)
                dve.tensor_tensor(act_all[:, u % 2], g[:, GU:2 * GU], gate_act[:, u % 2], ALU.mult
                                  ).then_inc(act_ready, 1)

            def result(n, v, u):
                dve.wait_ge(down_done, n + 1)
                if u == 0 and not (isinstance(n, int) and n < 2 * GT):
                    dve.wait_ge(out_landed[v % 2], 16 * (n // (2 * GT)))
                dve.tensor_tensor(ot[:, v % 2, u], bank[:, 7, 0:D], h_tiles[:, n], ALU.add).then_inc(out_ready, 1)

            def slot(q, v):
                for u in range(GT):
                    n = GT * q + u
                    if live_tile(n - 3):
                        result(n - 3, v if u == 3 else v - 1, (u - 3) % GT)
                    if live_tile(n - 1):
                        gating(n - 1, u - 1)
                    if u == 0 and live(q):
                        routing_experts(q, v)
                    if u == 1 and live(q + 2):
                        residual(q + 2, v + 2)
                    if u == 2 and live(q + 1):
                        routing_groups_1(q + 1)
                    if u == 3 and live(q + 1):
                        routing_groups_2(q + 1)
                    if u == 3 and live(q + 2):
                        norm(q + 2)

            slots(dve, slot)

        @block.gpsimd
        def _(pool):
            pool.wait_ge(filled, 1)

            def slot(q, v):
                for u in range(GT):
                    n = GT * q + u - 1
                    if u == 2 and live(q + 2):
                        wait_alone(pool, mv_ready, q + 3, apart_pool)
                        pool.tensor_scalar(ve[:], mv[:, :, 1], 1e-5, None, ALU.add).then_inc(ve_ready, 1)
                        pool.wait_ge(ve_ready, q + 3)
                        pool.tensor_tensor(rstd[:], ve[:], expo[:], ALU.pow).then_inc(rstd_ready, 1)
                    if u == 1 and live(q + 1):
                        pool.wait_ge(xT_high, q + 2)
                        at_least(pool, in_done, GT * q)
                        p = (v + 1) % 2
                        pool.tensor_tensor(xT_parts[:, p, 1], xT[:, p], xT_parts[:, p, 0].bitcast(F32),
                                           ALU.subtract).then_inc(xT_low, 1)
                    if live_tile(n):
                        c = combine[:, (v if u > 0 else v - 1) % 2, (u - 1) % GT]
                        if u == 1:
                            pool.wait_ge(combine_ready, q + 1)
                        pool.wait_ge(act_ready, n + 1)
                        at_least(pool, h_turned, 2 * (n - 1))
                        pool.tensor_tensor(hw[:, (u - 1) % 2].rearrange("p (e h) -> p e h", e=E),
                                           act_all[:, (u - 1) % 2, 0:E * EH].rearrange("p (e h) -> p e h", e=E),
                                           c.unsqueeze(2).broadcast_to([128, E, EH]), ALU.mult).then_inc(hw_ready, 1)

            slots(pool, slot)


def kernel(**inputs):
    import concourse.bacc as bacc
    from concourse.bass_utils import run_bass_kernel_spmd

    def i(name):
        return np.asarray(inputs[name])

    def feature_major(w):
        return w.reshape(LAYERS, H, HD, D).transpose(0, 2, 1, 3).reshape(LAYERS, D, D)

    def feature_major_row(b):
        return b.reshape(LAYERS, H, HD).transpose(0, 2, 1).reshape(LAYERS, D)

    def swapped(x):
        return np.roll(x, D // 2, axis=1)

    wq = feature_major(i("L0_attn_Wq"))
    bq, u = feature_major_row(i("L0_attn_bq")), feature_major_row(i("L0_attn_u_bias"))
    arrays = {
        "x": i("L0_attn_x"),
        "w_qkv": np.concatenate([wq, feature_major(i("L0_attn_Wk")), swapped(wq), i("L0_attn_Wv")],
                                axis=1).transpose(0, 2, 1),
        "b_cols": np.stack([bq, feature_major_row(i("L0_attn_bk")), bq, swapped(bq)], axis=1).reshape(LAYERS * 4, D).T,
        "u_cols": np.stack([u, swapped(u)], axis=1).reshape(LAYERS * 2, D).T,
        "b_v": i("L0_attn_bv"),
        "w_o": i("L0_attn_Wo").transpose(0, 2, 1),
        "bo": i("L0_attn_bo"),
        "w_1": i("L0_attn_W1").transpose(0, 2, 1),
        "b_1": i("L0_attn_b1").reshape(LAYERS * FC, 128).T,
        "w_2": i("L0_attn_W2").transpose(0, 2, 1),
        "b2": i("L0_attn_b2"),
        "ln_cols": np.stack([i("L0_attn_ln1_w"), i("L0_attn_ln1_b"), i("L0_attn_ln2_w"), i("L0_attn_ln2_b")],
                            axis=1).reshape(LAYERS * 4, D).T,
        "router": i("L0_ffn_router_w").T,
        "correction": i("L0_ffn_correction_bias"),
        "w_in": np.concatenate([i("L0_ffn_gate_w").transpose(1, 0, 2).reshape(D, E * EH),
                                i("L0_ffn_shared_gate_w").T,
                                i("L0_ffn_up_w").transpose(1, 0, 2).reshape(D, E * EH),
                                i("L0_ffn_shared_up_w").T], axis=1),
        "w_down": np.concatenate([i("L0_ffn_down_w").reshape(E * EH, D), i("L0_ffn_shared_down_w").T], axis=0),
    }
    arrays.update(position_tables())
    arrays = {f"in_{name}": np.ascontiguousarray(x) for name, x in arrays.items()}
    nc = bacc.Bacc("TRN2", target_bir_lowering=False, num_devices=1)
    a = {name[3:]: nc.dram_tensor(name, x.shape, mybir.dt.from_np(x.dtype), kind="ExternalInput").ap()
         for name, x in arrays.items()}
    out = nc.dram_tensor("out", (B, S, D), F32, kind="ExternalOutput").ap()
    with nc.sbuf_tensor("h_all", [128, B, T, D], F32) as h_all:
        layers_program(nc, a, h_all)
        experts_program(nc, a, h_all, out)
    r = run_bass_kernel_spmd(nc, [arrays], core_ids=[0])
    return r.results[0]["out"]
```
